# Optimizing a Trainium2 kernel written in Bass

```python
import numpy as np
import jax
import jax.numpy as jnp

def _softmax(x, axis=-1):
    return jax.nn.softmax(x, axis=axis)

def _gelu(x):
    return jax.nn.gelu(x, approximate=True)

def _silu(x):
    return jax.nn.silu(x)

def _sigmoid(x):
    return jax.nn.sigmoid(x)

def _layernorm(x, axis=-1, eps=1e-05):
    m = jnp.mean(x, axis=axis, keepdims=True)
    v = jnp.var(x, axis=axis, keepdims=True)
    return (x - m) / jnp.sqrt(v + eps)

def _scatter_add(tgt, idx, src, axis=0):
    return tgt.at[idx].add(src)

def _segment_sum(src, seg, n):
    return jax.ops.segment_sum(src, seg, n)
kernel_name = 'mk_gnn_resnorm_d2_gnn_r64_ac8708'

def setup_inputs(seed: int=0):
    np.random.seed(seed)
    _w = jnp.asarray

    def _rec_inputs():
        import jax
        import jax.numpy as jnp
        _gk = jax.random.key(seed)
        x = -0.0003713 + 1 * jax.random.normal(jax.random.fold_in(_gk, 1), (100000, 128), jnp.float32)
        src = jax.random.randint(jax.random.fold_in(_gk, 2), (25000,), 0, 100000, jnp.int32)
        dst = jnp.minimum((100000 * jax.random.uniform(jax.random.fold_in(_gk, 3), (25000,)) ** 2.0).astype(jnp.int32), 99999)
        _o = jnp.argsort(dst, stable=True)
        src = src[_o]
        dst = dst[_o]
        edge_attr_128 = -6.37281e-06 + 0.999856 * jax.random.normal(jax.random.fold_in(_gk, 12), (25000, 128), jnp.float32)
        edge_weight = jax.random.uniform(jax.random.fold_in(_gk, 14), (25000,), jnp.float32, 0.0, 0.999998)
        return (x, src, dst, edge_attr_128, edge_weight)
    x, src, dst, edge_attr_128, edge_weight = _rec_inputs()

    def _L0_gnn_setup():
        import jax, jax.numpy as jnp
        import numpy as np
        N_NODES = 100000
        N_INCID = 31250
        HIDDEN = 128
        N_HE = 100000
        key = jax.random.key(seed)
        k1, k2, k3 = jax.random.split(key, 3)
        node_feats = jax.random.normal(k1, (N_NODES, HIDDEN), dtype=jnp.float32)
        hyperedge_index = jax.random.randint(k2, (2, N_INCID), 0, N_HE, dtype=jnp.int64)
        bound = float(np.sqrt(6.0 / (HIDDEN + 1)))
        W = jax.random.uniform(k3, (1, HIDDEN), dtype=jnp.float32, minval=-bound, maxval=bound)
        return {'node_feats': node_feats, 'hyperedge_index': hyperedge_index, 'num_hyperedges': N_HE, 'W': W}
    _L0_gnn_all = _L0_gnn_setup()
    _L0_gnn_in = {k: v for k, v in _L0_gnn_all.items() if k in ('W',)}
    del _L0_gnn_all

    def _L1_gnn_setup():
        import jax, jax.numpy as jnp
        import numpy as np
        N_NODES = 30000
        DEGREE = 16
        N_EDGES = N_NODES * DEGREE
        F = 128
        F_OUT = 128
        ONSET = 0.8
        CUTOFF = 1.0

        def _ssp(x):
            return jax.nn.softplus(x) - jnp.log(2.0).astype(x.dtype)

        def _smooth_cutoff(d):
            t = (d - ONSET) / (CUTOFF - ONSET)
            ramp = 0.5 * (jnp.cos(jnp.float32(np.pi) * t) + 1.0)
            return jnp.where(d < ONSET, 1.0, jnp.where(d > CUTOFF, 0.0, ramp))
        key = jax.random.key(seed)
        ks = jax.random.split(key, 10)
        h = jax.random.normal(ks[0], (N_NODES, F), dtype=jnp.float32)
        edge_feat = jax.random.normal(ks[1], (N_EDGES, F), dtype=jnp.float32)
        dist = jax.random.uniform(ks[2], (N_EDGES,), dtype=jnp.float32)
        src = jax.random.randint(ks[3], (N_EDGES,), 0, N_NODES, dtype=jnp.int32)
        dst = jnp.repeat(jnp.arange(N_NODES, dtype=jnp.int32), DEGREE)
        s = 1.0 / np.sqrt(F)
        W1 = jax.random.normal(ks[4], (F, F), dtype=jnp.float32) * s
        b1 = jnp.zeros((F,), dtype=jnp.float32)
        W2 = jax.random.normal(ks[5], (F, F), dtype=jnp.float32) * s
        b2 = jnp.zeros((F,), dtype=jnp.float32)
        W3 = jax.random.normal(ks[6], (F, F_OUT), dtype=jnp.float32) * s
        b3 = jnp.zeros((F_OUT,), dtype=jnp.float32)
        return {'h': h, 'edge_feat': edge_feat, 'dist': dist, 'src': src, 'dst': dst, 'W1': W1, 'b1': b1, 'W2': W2, 'b2': b2, 'W3': W3, 'b3': b3}
    _L1_gnn_all = _L1_gnn_setup()
    _L1_gnn_in = {k: v for k, v in _L1_gnn_all.items() if k in ('W1', 'b1', 'W2', 'b2', 'W3', 'b3')}
    del _L1_gnn_all
    return {'x': x, 'src': src, 'dst': dst, 'edge_attr_128': edge_attr_128, 'edge_weight': edge_weight, 'L0_gnn_W': _L0_gnn_in['W'], 'L1_gnn_W1': _L1_gnn_in['W1'], 'L1_gnn_b1': _L1_gnn_in['b1'], 'L1_gnn_W2': _L1_gnn_in['W2'], 'L1_gnn_b2': _L1_gnn_in['b2'], 'L1_gnn_W3': _L1_gnn_in['W3'], 'L1_gnn_b3': _L1_gnn_in['b3']}

def reference(x, src, dst, edge_attr_128, edge_weight, L0_gnn_W, L1_gnn_W1, L1_gnn_b1, L1_gnn_W2, L1_gnn_b2, L1_gnn_W3, L1_gnn_b3):
    import jax
    import jax.numpy as jnp

    def _L0_gnn_ref(node_feats, hyperedge_index, num_hyperedges, W):
        import jax, jax.numpy as jnp
        import numpy as np
        N_NODES = 100000
        N_INCID = 31250
        HIDDEN = 128
        N_HE = 100000
        node_idx = hyperedge_index[0]
        he_idx = hyperedge_index[1]
        gathered = node_feats[node_idx]
        scores = jnp.einsum('ed,d->e', gathered, W[0])
        seg_max = jax.ops.segment_max(scores, he_idx, num_segments=num_hyperedges)
        seg_max = jnp.where(jnp.isfinite(seg_max), seg_max, 0.0)
        w = jnp.exp(scores - seg_max[he_idx])
        denom = jax.ops.segment_sum(w, he_idx, num_segments=num_hyperedges)
        w_norm = w / jnp.maximum(denom, 1e-20)[he_idx]
        out = jax.ops.segment_sum(w_norm[:, None] * gathered, he_idx, num_segments=num_hyperedges)
        return out

    def _L1_gnn_ref(h, edge_feat, dist, src, dst, W1, b1, W2, b2, W3, b3):
        import jax, jax.numpy as jnp
        import numpy as np
        N_NODES = 30000
        DEGREE = 16
        N_EDGES = N_NODES * DEGREE
        F = 128
        F_OUT = 128
        ONSET = 0.8
        CUTOFF = 1.0

        def _ssp(x):
            return jax.nn.softplus(x) - jnp.log(2.0).astype(x.dtype)

        def _smooth_cutoff(d):
            t = (d - ONSET) / (CUTOFF - ONSET)
            ramp = 0.5 * (jnp.cos(jnp.float32(np.pi) * t) + 1.0)
            return jnp.where(d < ONSET, 1.0, jnp.where(d > CUTOFF, 0.0, ramp))
        N, Fdim = h.shape
        gamma = jnp.float32(Fdim)
        muk = jnp.linspace(0.0, 1.0, Fdim, dtype=jnp.float32)
        bf = jnp.exp(-gamma * (dist[:, None] - muk) ** 2)
        bf = _ssp(bf @ W1 + b1)
        bf = _ssp(bf @ W2 + b2)
        cut = _smooth_cutoff(dist)[:, None]
        msg = h[src] * edge_feat * bf * cut
        node_h = jax.ops.segment_prod(msg, dst, num_segments=N)
        return _ssp(node_h @ W3 + b3)
    edge_index = jnp.stack([src, dst])
    x = _layernorm(x + _L0_gnn_ref(x, edge_index, 100000, L0_gnn_W), axis=-1)
    x = _layernorm(x + _L1_gnn_ref(x, edge_attr_128, edge_weight, src, dst, L1_gnn_W1, L1_gnn_b1, L1_gnn_W2, L1_gnn_b2, L1_gnn_W3, L1_gnn_b3), axis=-1)
    return x

_drawn_inputs = setup_inputs


def setup_inputs(seed=0):
    import zlib

    import numpy as np

    out = dict(_drawn_inputs(seed))
    spreads = {'L1_gnn_b1': (0.0, 0.8), 'L1_gnn_b2': (0.0, 0.748), 'L1_gnn_b3': (0.0, 0.1)}
    factors = {'edge_attr_128': 2.901, 'edge_weight': 3.91, 'L1_gnn_W1': 3.492, 'L1_gnn_W2': 3.45}
    for name, (base, spread) in spreads.items():
        noise = np.random.default_rng([zlib.crc32(name.encode()), seed]).standard_normal(out[name].shape)
        drawn = base * np.exp(spread * noise) if base else spread * noise
        out[name] = jnp.asarray(drawn.astype(out[name].dtype))
    for name, factor in factors.items():
        out[name] = (out[name] * factor).astype(out[name].dtype)
    return out
```

```python
import concourse.bass as bass
from concourse import mybir
from contextlib import ExitStack

P = 128
OCT = 8
QUAD = 4
QE = QUAD * P
EPS = 1e-5
BIG = 1e37
SKIP = 1 << 20
LN2 = 0.6931471805599453
ONSET, CUTOFF = 0.8, 1.0
PI = 3.141592653589793


def live(q, n):
    return not isinstance(q, int) or 0 <= q < n


def wait_past(eng, sem, value):
    if not isinstance(value, int) or value > 0:
        eng.wait_ge(sem, value)


def sweep(eng, start, lo, hi, stop, body):
    for i in range(start, min(lo, stop)):
        body(i, i % 2, i // 2)
    if hi > lo:
        with eng.Fori(lo // 2, hi // 2) as half:
            body(2 * half, 0, half)
            body(2 * half + 1, 1, half)
    for i in range(max(hi, lo), stop):
        body(i, i % 2, i // 2)


def back(i, slot, half, k):
    return i - k, (slot - k) % 2, half + (slot - k) // 2


class Chain:

    def __init__(self, eng, sem, size):
        self.eng, self.sem, self.size = eng, sem, size

    def begin(self, q):
        self.base, self.n = self.size * q, 0

    def add(self, ins):
        self.n += 1
        ins.then_inc(self.sem, 1)

    def settle(self):
        self.eng.wait_ge(self.sem, self.base + self.n)

    def link(self, ins):
        self.add(ins)
        self.settle()

    def end(self):
        assert self.n == self.size, (self.n, self.size)


def gnn_kernel(nc, x, src_tiles, dst_tiles, next_tiles, weight_tiles, src_flat, dst_flat, weight_flat, attr,
               W0, W1, b1, W2, b2, W3, b3, eye, iota1, mu, out):
    F32, BF16, I32 = mybir.dt.float32, mybir.dt.bfloat16, mybir.dt.int32
    ALU, ACT, AX = mybir.AluOpType, mybir.ActivationFunctionType, mybir.AxisListType

    N, F = x.shape
    E = attr.shape[0]
    NT = src_tiles.shape[1]
    NQ = NT // QUAD
    H = NT // 2
    OROWS = OCT * P
    NO = -(-N // OROWS)
    assert NO == 2 * NQ and H <= P and F == P and N >= OROWS

    node_rows = nc.dram_tensor("node_rows", [NT * P, F], F32).ap()
    decay_flat = nc.dram_tensor("decay_flat", [NT * P], F32).ap()
    cont_flat = nc.dram_tensor("cont_flat", [NT * P], F32).ap()

    ctx = ExitStack()
    with ctx:
        def sb(name, shape, dt=F32):
            return ctx.enter_context(nc.sbuf_tensor(name, shape, dt))

        def sem(name):
            return ctx.enter_context(nc.semaphore(name))

        def sem2(name):
            return [sem(name + "_0"), sem(name + "_1")]

        G = sb("gathered", [P, NT, F])
        src_i = sb("src_i", [P, NT], I32)
        dst_i = sb("dst_i", [P, NT], I32)
        next_i = sb("next_i", [P, NT], I32)
        xd_idx = sb("xd_idx", [P, NT], I32)
        out_idx = sb("out_idx", [P, NT], I32)
        row_idx = sb("row_idx", [P, NT], I32)
        src21 = sb("src21", [P, NT])
        wt = sb("wt", [P, NT])
        cut = sb("cut", [P, NT])
        score = sb("score", [P, NT])
        hit = sb("hit", [P, NT])
        tile1 = sb("tile1", [P, NT])
        tmp_t = sb("tmp_t", [P, NT])
        bw = sb("bw", [P, NT])
        rden = sb("rden", [P, NT])
        ident = sb("ident", [P, P])
        iota = sb("iota", [P, P])
        ones = sb("ones", [P, P])
        w0 = sb("w0", [P, P])
        w1, w2, w3 = (sb(n, [P, P]) for n in ("w1s", "w2s", "w3s"))
        muneg = sb("muneg", [P, 1])
        b1c, b2c, nb1, nb2, kb2, b1m = (sb(n, [P, 1]) for n in ("b1c", "b2c", "nb1", "nb2", "kb2", "b1m"))
        b3row = sb("b3row", [1, QUAD, F])
        epst = sb("epst", [P, 1])
        halfpi = sb("halfpi", [P, 1])
        crow = sb("crow", [P, F])
        ctmp = sb("ctmp", [P, F])
        ctmp2 = sb("ctmp2", [P, F])
        cstat = sb("cstat", [P, 6])
        cneg2 = sb("cneg2", [P, 1])
        ceps = sb("ceps", [P, 1])
        c3 = sb("c3", [3, QUAD, F], BF16)
        ones3 = sb("ones3", [3, P], BF16)
        rhs_sel = sb("rhs_sel", [16, OCT, F])
        junk = sb("junk", [P, 2, F])
        ajunk = sb("ajunk", [P, 2, F])

        dst_c, prev_c = (sb(n, [H, 256], I32) for n in ("dst_c", "prev_c"))
        cont_c, pen_c, score_c, da_c, db_c, decay_c, bw_c, den_c = (
            sb(n, [H, 256]) for n in ("cont_c", "pen_c", "score_c", "da_c", "db_c", "decay_c", "bw_c", "den_c"))
        max_c = sb("max_c", [H, 257])
        zero_c = sb("zero_c", [H, 256])
        pass_c = sb("pass_c", [H, 2])
        rowbuf = sb("rowbuf", [1, 2 * P])
        carry_row = sb("carry_row", [1, P + 1])
        carry_c = sb("carry_c", [H, 1])

        WORK = 33 * QE
        work = sb("work", [P, WORK])
        used = [0]

        def take(*free, parts=P, dt=F32):
            n = 1
            for f in free:
                n *= f
            v = work[0:parts, used[0]:used[0] + n]
            used[0] += n
            assert used[0] <= WORK
            if dt is not F32:
                v = v.bitcast(dt)
            return v.rearrange("p (a b) -> p a b", b=free[1]) if len(free) == 2 else v

        def take2(*free, **kw):
            return [take(*free, **kw) for _ in range(2)]

        xo, oo = take2(OCT, F), take2(OCT, F)
        st = take2(OCT, 6)
        (sm, df, v2, dd, V, q1, q2, t1, t2, t3, t4, lnv, rstd, sdev, lnv2, rstd2, scale, qsum) = (
            take2(OCT) for _ in range(18))
        stats = take2(2 * OCT)
        statsT = take2(P, parts=16)
        srcrow = take2(QE, parts=H, dt=I32)
        ge = take2(2, QE, parts=H)
        drow_i, dnext_i, prow_i, pnext_i = (take(2, P, parts=H, dt=I32) for _ in range(4))
        dfirst = take(2, parts=H)
        dcode, dprev = (take(2, P + 1, parts=H) for _ in range(2))
        arow, bx, RT, xd, U = take2(QE), take2(QUAD, F), take2(QE), take2(QUAD, F), take2(QUAD, F)
        used[0] = 0
        wrow, attr_s, Ur, cont = take2(QE), take2(QUAD, F), take2(QUAD, F), take2(QE)
        sq, e0, ab = take(QE), take(QE), take(QE)
        l1, l2, l3 = take(QE), take(QE), take(QE)
        h1 = take(QE)
        bf = take2(QE)
        hn, hm, x1d = take2(QUAD, F), take2(QUAD, F), take2(QUAD, F)
        m, d0, d1 = take(QE), take(QE), take(QE)
        prod = take2(QE)
        t_, y = take(QE), take(QUAD, F)
        o = take2(QUAD, F)
        bst = take2(2 * QUAD, 6)
        (bsm, bdf, bv2, bdd, bV, bln, brs, brc, bnm) = (take2(2 * QUAD) for _ in range(9))
        yst = take2(QUAD, 6)
        (ysm, ydf, yv2, ydd, yV, yln, yrs, ynm) = (take2(QUAD) for _ in range(8))

        banks = [ctx.enter_context(nc.psum_tensor(f"bank{i}", [P, 512], F32)) for i in range(8)]
        D = [banks[0:2], banks[2:4]]
        psT = banks[4]
        psF = banks[5:7]
        psX = banks[5:7]
        psR = banks[7]
        E0, E1, E2 = banks[5], banks[6], banks[7]
        Z1, Z2, MT, Z3 = banks[0:2], banks[2:4], banks[4:6], banks[6:8]

        idx_in, tab_in, par_in = sem("idx_in"), sem("tab_in"), sem("par_in")
        setup_dve, setup_pe, setup_act = sem("setup_dve"), sem("setup_pe"), sem("setup_act")
        idx_ready, find_setup, cont_ready, cut_t, cut_sin, const_ready = (
            sem(n) for n in ("idx_ready", "find_setup", "cont_ready", "cut_t", "cut_sin", "const_ready"))
        x_in, o_stored = sem2("x_in"), sem2("o_stored")
        bn_done, d_filled, stat_T, stat_copied, d_final, o_ready = (
            sem(n) for n in ("bn_done", "d_filled", "stat_T", "stat_copied", "d_final", "o_ready"))
        c_var, c_var2, c_r, c_r2, c_junk, c_qsum = (
            sem(n) for n in ("c_var", "c_var2", "c_r", "c_r2", "c_junk", "c_qsum"))
        g_in, srcrow_in = sem2("g_in"), sem2("srcrow_in")
        ge_ready, found, find_used, rows_found = (sem(n) for n in ("ge_ready", "found", "find_used", "rows_found"))
        soft_dve, soft_pe, soft_act, decay_ready, decay_stored, cont_stored = (
            sem(n) for n in ("soft_dve", "soft_pe", "soft_act", "decay_ready", "decay_stored", "cont_stored"))
        arow_in, xd_in, u_stored = sem2("arow_in"), sem2("xd_in"), sem2("u_stored")
        bx_ready, bx_T, scan_done, r_T, u_ready = (sem(n) for n in ("bx_ready", "bx_T", "scan_done", "r_T", "u_ready"))
        a_done, a_stored = sem("a_done"), sem("a_stored")
        wrow_in, attr_in, ur_in, cont_in = sem2("wrow_in"), sem2("attr_in"), sem2("ur_in"), sem2("cont_in")
        row_in, scattered = sem2("row_in"), sem2("scattered")
        c_filter, c_norm_r, c_bvar, c_bmul = sem("c_filter"), sem("c_norm_r"), sem("c_bvar"), sem("c_bmul")
        z1_done, h1_ready, z2_done, bf_ready, hn_ready, x1d_ready, hm_ready, m_T = (
            sem(n) for n in ("z1_done", "h1_ready", "z2_done", "bf_ready", "hn_ready", "x1d_ready", "hm_ready", "m_T"))
        c_prod, z3_done, c_l3, c_y, c_yr, ynm_ready, row_ready = (
            sem(n) for n in ("c_prod", "z3_done", "c_l3", "c_y", "c_yr", "ynm_ready", "row_ready"))

        def octet_rows(i):
            return x[bass.ds(i * OROWS, OROWS), :].rearrange("(p j) f -> p j f", j=OCT)

        def quad_rows(t, q):
            return t[bass.ds(q * QE, QE), :].rearrange("(j p) f -> p j f", p=P)

        LAST = N - OROWS
        FRESH = (NO - 1) * OROWS - LAST
        assert FRESH % OCT == 0

        VAR_OPS, V_AT = 8, 7
        VAR2_OPS, S1_AT, VAR2_AT, SCALE_AT = 6, 3, 5, 6
        FILTER_OPS, E0_AT, L1_AT, L2_AT = 8, 2, 5, 8
        BVAR_OPS, BV_AT = 13, 13
        PROD_OPS, PROD_AT = 4, 4
        Y_OPS, YV_AT = 11, 11

        A1 = (0, 2, 2 + (NQ - 2) // 2 * 2, NQ)
        a2lo = NQ + 3 + (NQ + 3) % 2
        A2 = (NQ, a2lo, max(a2lo, (NO - 1) // 2 * 2), NO + 2)
        blo = 4
        B = (0, blo, max(blo, NQ // 2 * 2), NQ + 3)

        block = ctx.enter_context(nc.Block())

        @block.sync
        def _(sp):
            sp.dma_start(src_i[:, :], src_tiles).then_inc(idx_in, 16)
            for dst, src in ((dst_i, dst_tiles), (next_i, next_tiles), (wt, weight_tiles)):
                sp.dma_start(dst[:, :], src).then_inc(tab_in, 16)
            rows = "(k g j) -> k g j"
            base = P
            for dst, off in ((drow_i, 0), (dnext_i, 1), (prow_i, -P), (pnext_i, 1 - P)):
                for g in range(2):
                    v = dst_flat[base + off + g * H * P:base + off + (g + 1) * H * P].rearrange("(k j) -> k j", j=P)
                    sp.dma_start(dst[:, g, :], v).then_inc(tab_in, 16)
            for dst, off in ((dst_c, 0), (prev_c, -1)):
                sp.dma_start(dst[:, :], dst_flat[base + off:base + off + NT * P].rearrange("(k j) -> k j", j=256)
                             ).then_inc(tab_in, 16)
            for dst, src in ((ident, eye), (iota, iota1), (w1, W1), (w2, W2), (w3, W3), (muneg, mu),
                             (b1c, b1.rearrange("(p a) -> p a", a=1)), (b2c, b2.rearrange("(p a) -> p a", a=1))):
                sp.dma_start(dst[:, :], src).then_inc(par_in, 16)
            sp.dma_start(w0[:, :], W0[0, :].partition_broadcast(P)).then_inc(par_in, 16)
            for j in range(QUAD):
                sp.dma_start(b3row[:, j, :], b3.rearrange("(a f) -> a f", a=1)).then_inc(par_in, 16)

            def load_dense(i, slot, half):
                wait_past(sp, bn_done, i - 1)
                wait_past(sp, d_filled, i - 1)
                if isinstance(i, int) and i == NO - 1:
                    rows_ = x[LAST:N, :].rearrange("(p j) f -> p j f", j=OCT)
                else:
                    rows_ = octet_rows(i)
                sp.dma_start(xo[slot], rows_).then_inc(x_in[slot], 16)

            def store_dense(i, slot, half):
                sp.wait_ge(o_ready, i + 1)
                if isinstance(i, int) and i == NO - 1:
                    skip = FRESH // OCT
                    rows_ = out[(NO - 1) * OROWS:N, :].rearrange("(p j) f -> p j f", j=OCT)
                    sp.dma_start(rows_, oo[slot][skip:P]).then_inc(o_stored[slot], 16)
                else:
                    rows_ = out[bass.ds(i * OROWS, OROWS), :].rearrange("(p j) f -> p j f", j=OCT)
                    sp.dma_start(rows_, oo[slot]).then_inc(o_stored[slot], 16)

            def step_a1(i, slot, half):
                wait_past(sp, ge_ready, i - 1)
                sp.dma_start(srcrow[slot], src_flat[bass.ds(i * QE, QE)].partition_broadcast(H)
                             ).then_inc(srcrow_in[slot], 16)
                load_dense(i, slot, half)
                k, s, h = back(i, slot, half, 2)
                if live(k, NO):
                    store_dense(k, s, h)

            def step_a2(i, slot, half):
                if live(i, NO):
                    load_dense(i, slot, half)
                q, s, h = back(i, slot, half, NQ)
                if live(q, NQ):
                    wait_past(sp, scan_done, q - 1)
                    sp.dma_start(arow[s], decay_flat[bass.ds(q * QE, QE)].partition_broadcast(P)
                                 ).then_inc(arow_in[s], 16)
                k, s, h = back(i, slot, half, 2)
                if live(k, NO):
                    store_dense(k, s, h)
                q, s, h = back(i, slot, half, NQ + 2)
                if live(q, NQ):
                    store_u(q, s)

            def store_u(q, s):
                sp.wait_ge(u_ready, q + 1)
                sp.dma_start(quad_rows(node_rows, q), U[s]).then_inc(u_stored[s], 16)

            sweep(sp, *A1, step_a1)
            sp.wait_ge(cont_ready, 1)
            sp.dma_start(cont_flat.rearrange("(k j) -> k j", j=256), cont_c[:, :]).then_inc(cont_stored, 16)
            sp.wait_ge(decay_ready, 1)
            sp.dma_start(decay_flat.rearrange("(k j) -> k j", j=256), decay_c[:, :]).then_inc(decay_stored, 16)
            sp.wait_ge(cont_stored, 16)
            sp.wait_ge(decay_stored, 16)
            sweep(sp, *A2, step_a2)
            for s in range(2):
                sp.wait_ge(o_stored[s], 16 * (NO // 2))
                sp.wait_ge(u_stored[s], 16 * ((NQ + 1 - s) // 2))
            sp.sem_inc(a_stored, 1)
            sp.wait_ge(a_done, 3)

            def step_b(q, slot, half):
                wait_past(sp, z1_done, q - 1)
                sp.dma_start(wrow[slot], weight_flat[bass.ds(q * QE, QE)].partition_broadcast(P)
                             ).then_inc(wrow_in[slot], 16)
                wait_past(sp, x1d_ready, q - 1)
                sp.dma_start(Ur[slot], quad_rows(node_rows, q)).then_inc(ur_in[slot], 16)
                wait_past(sp, hm_ready, q - 1)
                if isinstance(q, int) and q == NQ - 1:
                    whole, rest = divmod(E - q * QE, P)
                    for j in range(whole):
                        r = q * QE + j * P
                        sp.dma_start(attr_s[slot][:, j, :], attr[r:r + P, :]).then_inc(attr_in[slot], 16)
                    if rest:
                        sp.dma_start(attr_s[slot][0:rest, whole, :], attr[E - rest:E, :]).then_inc(attr_in[slot], 16)
                else:
                    sp.dma_start(attr_s[slot], quad_rows(attr, q)).then_inc(attr_in[slot], 16)
                wait_past(sp, z3_done, q - 1)
                sp.dma_start(cont[slot], cont_flat[bass.ds(q * QE, QE)].partition_broadcast(P)
                             ).then_inc(cont_in[slot], 16)

            sweep(sp, 0, B[1], max(B[1], (NQ - 1) // 2 * 2), NQ, step_b)

        ATTR_LOADS = -(-(E - (NQ - 1) * QE) // P)

        @block.gpsimd
        def _(pool):
            pool.wait_ge(idx_in, 16)

            def gather(dst, table, idx, t, bound, s):
                nc.gpsimd.indirect_dma_start(dst, None, table, bass.IndirectOffsetOnAxis(ap=idx[:, t:t + 1], axis=0),
                                             bounds_check=bound, oob_is_err=False).then_inc(s, 16)

            for q in range(NQ):
                wait_past(pool, g_in[q % 2], 64 * (q // 2))
                for t in range(QUAD * q, QUAD * q + QUAD):
                    gather(G[:, t, :], x, src_i, t, N - 1, g_in[q % 2])
            pool.wait_ge(idx_ready, 1)
            for q in range(NQ):
                wait_past(pool, u_ready, q - 1)
                wait_past(pool, xd_in[q % 2], 64 * (q // 2))
                for j in range(QUAD):
                    gather(xd[q % 2][:, j, :], x, xd_idx, QUAD * q + j, N - 1, xd_in[q % 2])
            pool.wait_ge(rows_found, 1)
            pool.wait_ge(a_stored, 1)
            for s in range(2):
                pool.wait_ge(g_in[s], 64 * ((NQ + 1 - s) // 2))
            LEAD = 4
            for q in range(NQ + LEAD):
                if q < NQ:
                    wait_past(pool, row_in[q % 2], 64 * (q // 2))
                    for t in range(QUAD * q, QUAD * q + QUAD):
                        gather(G[:, t, :], node_rows, row_idx, t, NT * P - 1, row_in[q % 2])
                if q >= LEAD:
                    k = q - LEAD
                    pool.wait_ge(row_ready, k + 1)
                    wait_past(pool, scattered[k % 2], 64 * (k // 2))
                    for j in range(QUAD):
                        t = QUAD * k + j
                        nc.gpsimd.indirect_dma_start(
                            out, bass.IndirectOffsetOnAxis(ap=out_idx[:, t:t + 1], axis=0), o[k % 2][:, j, :], None,
                            bounds_check=N - 1, oob_is_err=False).then_inc(scattered[k % 2], 16)
            for s in range(2):
                pool.wait_ge(scattered[s], 64 * ((NQ + 1 - s) // 2))

        @block.vector
        def _(dve):
            v = nc.vector
            ch = Chain(dve, setup_dve, 0)
            ch.begin(0)
            ch.add(v.memset(ones[:, :], 1.0))
            ch.add(v.memset(ones3[:, :], 1.0))
            ch.add(v.memset(epst[:, :], EPS))
            ch.add(v.memset(halfpi[:, :], PI / 2))
            ch.add(v.memset(zero_c[:, :], 0.0))
            ch.settle()
            assert ch.n == 5
            dve.wait_ge(idx_in, 16)
            dve.wait_ge(tab_in, 16 * 13)
            ch.add(v.tensor_scalar(xd_idx[:, :], dst_i[:, :], float(N - 1), None, ALU.min))
            ch.add(v.tensor_tensor(tmp_t[:, :], dst_i[:, :], next_i[:, :], ALU.is_equal))
            ch.add(v.tensor_scalar(src21[:, :], src_i[:, :], 2.0, 1.0, ALU.mult, ALU.add))
            ch.settle()
            ch.link(v.scalar_tensor_tensor(out_idx[:, :], tmp_t[:, :], float(SKIP), dst_i[:, :], ALU.mult, ALU.add))
            v.sem_inc(idx_ready, 1)
            for rows_, nxt, code in ((drow_i, dnext_i, dcode), (prow_i, pnext_i, dprev)):
                ch.link(v.tensor_tensor(code[:, :, 0:P], rows_, nxt, ALU.is_equal))
                ch.link(v.tensor_scalar(code[:, :, 0:P], code[:, :, 0:P], -1.0, 1.0, ALU.mult, ALU.add))
                ch.link(v.scalar_tensor_tensor(code[:, :, 0:P], rows_, 2.0, code[:, :, 0:P], ALU.mult, ALU.add))
            ch.link(v.memset(dprev[0:1, 0, 0:P], 0.0))
            ch.add(v.tensor_tensor(dcode[:, :, 0:P], dcode[:, :, 0:P], dprev[:, :, 0:P], ALU.subtract))
            ch.add(v.memset(dcode[:, :, P:P + 1], 1.0))
            ch.add(v.tensor_copy(dfirst.unsqueeze(2), drow_i[:, :, 0:1]))
            ch.settle()
            v.sem_inc(find_setup, 1)
            ch.link(v.tensor_tensor(cont_c[:, :], dst_c[:, :], prev_c[:, :], ALU.is_equal))
            ch.add(v.tensor_scalar(pen_c[:, :], cont_c[:, :], -1.0, BIG, ALU.add, ALU.mult))
            ch.link(v.tensor_reduce(pass_c[:, 0:1], cont_c[:, :], AX.X, ALU.min))
            ch.link(v.tensor_scalar(pass_c[:, 1:2], pass_c[:, 0:1], -1.0, BIG, ALU.add, ALU.mult))
            v.sem_inc(cont_ready, 1)
            ch.link(v.tensor_scalar(tmp_t[:, :], wt[:, :], -ONSET, 1.0 / (CUTOFF - ONSET), ALU.add, ALU.mult))
            ch.link(v.tensor_scalar(tmp_t[:, :], tmp_t[:, :], 0.0, 1.0, ALU.max, ALU.min))
            v.sem_inc(cut_t, 1)
            dve.wait_ge(cut_sin, 1)
            ch.link(v.tensor_scalar(tmp_t[:, :], cut[:, :], 0.5, 0.5, ALU.mult, ALU.add))
            ch.link(v.tensor_scalar(cut[:, :], wt[:, :], ONSET, None, ALU.is_lt))
            ch.link(v.tensor_tensor(tmp_t[:, :], tmp_t[:, :], cut[:, :], ALU.max))
            ch.link(v.tensor_scalar(cut[:, :], wt[:, :], CUTOFF, None, ALU.is_le))
            ch.link(v.tensor_tensor(cut[:, :], cut[:, :], tmp_t[:, :], ALU.mult))
            dve.wait_ge(par_in, 16 * 13)
            ch.add(v.tensor_scalar(nb1[:, :], b1c[:, :], -1.0, None, ALU.mult))
            ch.link(v.tensor_scalar(b1m[:, :], b1c[:, :], -LN2, None, ALU.add))
            v.sem_inc(const_ready, 1)
            dve.wait_ge(setup_pe, 2)
            ch.link(v.tensor_tensor(b2c[:, :], b2c[:, :], E1[:, 0:1], ALU.add))
            ch.add(v.tensor_scalar(nb2[:, :], b2c[:, :], -1.0, None, ALU.mult))
            ch.add(v.tensor_scalar(kb2[:, :], b2c[:, :], -LN2, None, ALU.add))
            dve.wait_ge(setup_act, 3)
            ch.link(v.scalar_tensor_tensor(crow[:, :], E0[:, 0:F], 0.0, ctmp[:, :], ALU.max, ALU.add))
            ch.link(v.tensor_scalar(crow[:, :], crow[:, :], -LN2, None, ALU.add))
            ch.link(v.tensor_reduce(ceps[:, :], crow[:, :], AX.X, ALU.add))
            ch.link(v.tensor_scalar(ceps[:, :], ceps[:, :], -1.0 / F, None, ALU.mult))
            ch.link(v.tensor_scalar(crow[:, :], crow[:, :], ceps[:, :], None, ALU.add))
            ch.link(v.tensor_tensor(ctmp[:, :], crow[:, :], crow[:, :], ALU.mult))
            ch.link(v.tensor_reduce(cneg2[:, :], ctmp[:, :], AX.X, ALU.add))
            ch.link(v.tensor_scalar(ceps[:, :], cneg2[:, :], 1.0 / F, EPS, ALU.mult, ALU.add))
            ch.link(v.tensor_scalar(cneg2[:, :], cneg2[:, :], -1.0, None, ALU.mult))
            ch.link(v.memset(ctmp2[0:3, :], 0.0))
            for k in range(3):
                part = c3[0:3, k, :]
                ch.link(v.tensor_copy(part, crow[0:3, :] if k == 0 else ctmp[0:3, :]))
                ch.link(v.scalar_tensor_tensor(ctmp2[0:3, :], part, ident[0:3, k:k + 1], ctmp2[0:3, :],
                                               ALU.mult, ALU.add))
                ch.link(v.tensor_tensor(ctmp[0:3, :], crow[0:3, :] if k == 0 else ctmp[0:3, :], part, ALU.subtract))
            ch.link(v.tensor_copy(c3[:, :, :], ctmp2[0:3, :].unsqueeze(1).to_broadcast([3, QUAD, F])))
            ch.link(v.tensor_tensor(rhs_sel[:, :, :], ident[0:16, 0:OCT].unsqueeze(2).to_broadcast([16, OCT, F]),
                                    crow[0:16, :].unsqueeze(1).to_broadcast([16, OCT, F]), ALU.mult))
            ch.link(v.tensor_tensor(rhs_sel[:, :, :], rhs_sel[:, :, :],
                                    ident[0:16, OCT:2 * OCT].unsqueeze(2).to_broadcast([16, OCT, F]), ALU.add))
            v.sem_inc(const_ready, 1)

            var, var2, cj = Chain(dve, c_var, VAR_OPS), Chain(dve, c_var2, VAR2_OPS), Chain(dve, c_junk, 8)

            def stats_part(i, s, h):
                dve.wait_ge(x_in[s], 16 * (h + 1))
                for j in range(OCT):
                    ins = v.bn_stats(st[s][:, j, :], xo[s][:, j, :])
                ins.then_inc(bn_done, 1)
                dve.wait_ge(bn_done, i + 1)
                wait_past(dve, d_final, i - 1)
                var.begin(i)
                var.add(v.tensor_tensor(sm[s], st[s][:, :, 1], st[s][:, :, 4], ALU.add))
                var.add(v.tensor_tensor(df[s], st[s][:, :, 1], st[s][:, :, 4], ALU.subtract))
                var.add(v.tensor_tensor(v2[s], st[s][:, :, 2], st[s][:, :, 5], ALU.add))
                var.settle()
                var.add(v.tensor_tensor(dd[s], df[s], df[s], ALU.mult))
                var.add(v.tensor_tensor(q1[s], sm[s], sm[s], ALU.mult))
                var.add(v.tensor_scalar(stats[s][:, OCT:2 * OCT], sm[s], -0.5, None, ALU.mult))
                var.settle()
                var.link(v.scalar_tensor_tensor(V[s], dd[s], float(F) / 4, v2[s], ALU.mult, ALU.add))
                var.link(v.scalar_tensor_tensor(q2[s], q1[s], float(F) / 4, V[s], ALU.mult, ALU.add))
                var.end()

            def second_variance(i, s):
                dve.wait_ge(c_r, 3 * i + 3)
                dve.wait_ge(c_qsum, OCT * i + OCT)
                var2.begin(i)
                var2.add(v.tensor_tensor(t1[s], V[s], rstd[s], ALU.mult))
                var2.add(v.tensor_tensor(t2[s], qsum[s], q2[s], ALU.subtract))
                var2.add(v.tensor_scalar(stats[s][:, 0:OCT], sdev[s], -1.0, None, ALU.add))
                var2.settle()
                var2.link(v.scalar_tensor_tensor(t3[s], t2[s], cneg2[:, :], t1[s], ALU.add, ALU.add))
                var2.link(v.tensor_tensor(t4[s], t3[s], rstd[s], ALU.mult))

            def copy_stats(i, s):
                dve.wait_ge(stat_T, i + 1)
                v.tensor_copy(statsT[s], psT[0:16, 0:P]).then_inc(stat_copied, 1)
                dve.wait_ge(c_r2, 2 * i + 2)
                var2.add(v.tensor_tensor(scale[s], rstd[s], rstd2[s], ALU.mult))
                var2.end()

            def compare_sources(q, s, h):
                dve.wait_ge(srcrow_in[s], 16 * (h + 1))
                wait_past(dve, found, q - 1)
                v.tensor_scalar(ge[s][:, 0, :], srcrow[s], dfirst[:, 0:1], None, ALU.is_ge)
                v.tensor_scalar(ge[s][:, 1, :], srcrow[s], dfirst[:, 1:2], None, ALU.is_ge).then_inc(ge_ready, 1)

            def use_found(q):
                dve.wait_ge(found, q + 1)
                for j in range(QUAD):
                    wait_past(dve, c_junk, cj.base + cj.n - 1)
                    codes = psF[j // 2][:, (j % 2) * (P + 1):(j % 2) * (P + 1) + P]
                    cj.add(v.scalar_tensor_tensor(junk[:, j % 2, :], codes, src21[:, bass.ds(QUAD * q + j, 1)],
                                                  iota[:, :], ALU.is_equal, ALU.mult,
                                                  accum_out=hit[:, bass.ds(QUAD * q + j, 1)]))
                for b in range(2):
                    v.tensor_copy(tile1[:, bass.ds(QUAD * q + 2 * b, 2)], psF[b][:, P:2 * P + 2:P + 1]
                                  ).then_inc(find_used, 1)
                cj.end()

            def scores(q, s, h):
                dve.wait_ge(g_in[s], 64 * (h + 1))
                cj.begin(q)
                for j in range(QUAD):
                    wait_past(dve, c_junk, cj.base + cj.n - 1)
                    cj.add(v.scalar_tensor_tensor(junk[:, j % 2, :], G[:, bass.ds(QUAD * q + j, 1), :], 1.0, w0[:, :],
                                                  ALU.mult, ALU.mult, accum_out=score[:, bass.ds(QUAD * q + j, 1)]))

            def step_a1(i, s, h):
                k, ks, kh = back(i, s, h, 1)
                if live(k, NO):
                    second_variance(k, ks)
                compare_sources(i, s, h)
                if live(k, NO):
                    copy_stats(k, ks)
                stats_part(i, s, h)
                scores(i, s, h)
                use_found(i)

            sweep(dve, *A1, step_a1)

            dve.wait_ge(c_junk, 8 * NQ)
            dve.wait_ge(find_used, 2 * NQ)
            ch.add(v.scalar_tensor_tensor(tmp_t[:, :], tile1[:, :], float(P), hit[:, :], ALU.mult, ALU.add))
            ch.add(v.tensor_scalar(src21[:, :], hit[:, :], 0.0, float(SKIP), ALU.is_equal, ALU.mult))
            ch.settle()
            ch.link(v.scalar_tensor_tensor(row_idx[:, :], tmp_t[:, :], -float(P + 1), src21[:, :], ALU.add, ALU.add))
            v.sem_inc(rows_found, 1)

            soft = Chain(dve, soft_dve, 0)
            soft.begin(0)
            v.sem_inc(soft_dve, 1)
            soft.n = 1
            dve.wait_ge(soft_pe, 2)
            soft.link(v.tensor_copy(score_c[:, :], E0[0:H, 0:256]))
            soft.link(v.tensor_tensor_scan(max_c[:, 1:257], pen_c[:, :], score_c[:, :], -BIG, ALU.add, ALU.max))
            assert soft.n == 3
            dve.wait_ge(soft_pe, 4)
            soft.add(v.tensor_copy(rowbuf[:, :], E1[0:1, 0:2 * P]))
            soft.link(v.memset(carry_row[:, 0:1], -BIG))
            soft.link(v.tensor_tensor_scan(carry_row[0:1, 1:H + 1], rowbuf[0:1, P:P + H], rowbuf[0:1, 0:H], -BIG,
                                           ALU.add, ALU.max))
            assert soft.n == 6
            dve.wait_ge(soft_pe, 5)
            soft.link(v.tensor_copy(max_c[:, 0:1], E2[0:H, 0:1]))
            soft.link(v.tensor_tensor_scan(max_c[:, 1:257], pen_c[:, :], score_c[:, :], max_c[:, 0:1], ALU.add,
                                           ALU.max))
            soft.add(v.tensor_tensor(da_c[:, :], max_c[:, 0:256], pen_c[:, :], ALU.add))
            soft.add(v.tensor_tensor(db_c[:, :], score_c[:, :], max_c[:, 1:257], ALU.subtract))
            soft.settle()
            soft.link(v.tensor_tensor(da_c[:, :], da_c[:, :], max_c[:, 1:257], ALU.subtract))
            assert soft.n == 11
            dve.wait_ge(soft_act, 2)
            soft.add(v.tensor_tensor_scan(den_c[:, :], decay_c[:, :], bw_c[:, :], 0.0, ALU.mult, ALU.add))
            soft.link(v.tensor_tensor_scan(da_c[:, :], decay_c[:, :], zero_c[:, :], 1.0, ALU.mult, ALU.add))
            assert soft.n == 13
            dve.wait_ge(soft_pe, 7)
            soft.add(v.tensor_copy(rowbuf[:, :], E1[0:1, 0:2 * P]))
            soft.link(v.memset(carry_row[:, 0:1], 0.0))
            soft.link(v.tensor_tensor_scan(carry_row[0:1, 1:H + 1], rowbuf[0:1, P:P + H], rowbuf[0:1, 0:H], 0.0,
                                           ALU.mult, ALU.add))
            assert soft.n == 16
            dve.wait_ge(soft_pe, 8)
            soft.link(v.tensor_copy(carry_c[:, :], E2[0:H, 0:1]))
            soft.link(v.tensor_tensor_scan(den_c[:, :], decay_c[:, :], bw_c[:, :], carry_c[:, :], ALU.mult, ALU.add))
            soft.link(v.tensor_scalar(den_c[:, :], den_c[:, :], 1e-20, None, ALU.max))
            soft.link(v.reciprocal(den_c[:, :], den_c[:, :]))
            assert soft.n == 20
            dve.wait_ge(soft_pe, 12)
            for g in range(2):
                soft.add(v.tensor_copy(bw[:, g:NT:2], E0[:, g * H:(g + 1) * H]))
                soft.add(v.tensor_copy(rden[:, g:NT:2], E1[:, g * H:(g + 1) * H]))
            soft.settle()

            def weigh(q, s):
                wait_past(dve, bx_T, q - 1)
                v.tensor_tensor(bx[s], G[:, bass.ds(QUAD * q, QUAD), :],
                                bw[:, bass.ds(QUAD * q, QUAD)].unsqueeze(2).to_broadcast([P, QUAD, F]),
                                ALU.mult).then_inc(bx_ready, 1)

            def running_sum(q, s, h):
                dve.wait_ge(arow_in[s], 16 * (h + 1))
                dve.wait_ge(bx_T, q + 1)
                wait_past(dve, r_T, q - 1)
                if isinstance(q, int) and q == 0:
                    start = 0.0
                else:
                    dve.wait_ge(scan_done, q)
                    start = RT[1 - s][:, QE - 1:QE]
                v.tensor_tensor_scan(RT[s], arow[s], psX[s][:, :], start, ALU.mult, ALU.add).then_inc(scan_done, 1)

            def node_sums(q, s, h):
                dve.wait_ge(r_T, q + 1)
                dve.wait_ge(xd_in[s], 64 * (h + 1))
                wait_past(dve, u_stored[s], 16 * h)
                for j in range(QUAD):
                    ins = v.scalar_tensor_tensor(U[s][:, j, :], psR[:, j * P:(j + 1) * P],
                                                 rden[:, bass.ds(QUAD * q + j, 1)], xd[s][:, j, :],
                                                 ALU.mult, ALU.add)
                ins.then_inc(u_ready, 1)

            def step_a2(i, s, h):
                k, ks, kh = back(i, s, h, 1)
                if live(k, NO):
                    second_variance(k, ks)
                q, qs, qh = back(i, s, h, NQ)
                if live(q, NQ):
                    weigh(q, qs)
                if live(k, NO):
                    copy_stats(k, ks)
                if live(i, NO):
                    stats_part(i, s, h)
                q, qs, qh = back(i, s, h, NQ + 2)
                if live(q, NQ):
                    node_sums(q, qs, qh)
                q, qs, qh = back(i, s, h, NQ + 1)
                if live(q, NQ):
                    running_sum(q, qs, qh)

            sweep(dve, *A2, step_a2)
            dve.wait_ge(u_ready, NQ)
            v.sem_inc(a_done, 1)
            dve.wait_ge(a_done, 3)
            dve.wait_ge(a_stored, 1)

            bvar, bmul, prod_c, yc = (Chain(dve, c_bvar, BVAR_OPS), Chain(dve, c_bmul, 3),
                                      Chain(dve, c_prod, PROD_OPS), Chain(dve, c_y, Y_OPS))

            def variance(c, stat, sm_, df_, v2_, dd_, V_):
                c.add(v.tensor_tensor(sm_, stat[:, :, 1], stat[:, :, 4], ALU.add))
                c.add(v.tensor_tensor(df_, stat[:, :, 1], stat[:, :, 4], ALU.subtract))
                c.add(v.tensor_tensor(v2_, stat[:, :, 2], stat[:, :, 5], ALU.add))
                c.settle()
                c.link(v.tensor_tensor(dd_, df_, df_, ALU.mult))
                c.link(v.scalar_tensor_tensor(V_, dd_, float(F) / 4, v2_, ALU.mult, ALU.add))

            def finish_rows(q, s):
                dve.wait_ge(c_l3, 3 * q + 3)
                dve.wait_ge(x1d_ready, q + 1)
                yc.begin(q)
                yc.link(v.scalar_tensor_tensor(t_, Z3[s][:, :], 0.0, l3, ALU.max, ALU.add))
                wait_past(dve, row_ready, q)
                yc.link(v.scalar_tensor_tensor(y.rearrange("p a b -> p (a b)"), t_, -LN2,
                                               x1d[s].rearrange("p a b -> p (a b)"), ALU.add, ALU.add))
                for j in range(QUAD):
                    yc.add(v.bn_stats(yst[s][:, j, :], y[:, j, :]))
                yc.settle()
                variance(yc, yst[s], ysm[s], ydf[s], yv2[s], ydd[s], yV[s])
                yc.end()

            def norm_factors(q, s):
                dve.wait_ge(c_norm_r, 2 * q + 2)
                wait_past(dve, x1d_ready, q - 1)
                bmul.begin(q)
                bmul.add(v.tensor_tensor(brc[s][:, 0:QUAD], brs[s][:, 0:QUAD], cut[:, bass.ds(QUAD * q, QUAD)],
                                         ALU.mult))
                bmul.add(v.tensor_copy(brc[s][:, QUAD:2 * QUAD], brs[s][:, QUAD:2 * QUAD]))
                bmul.settle()
                bmul.link(v.scalar_tensor_tensor(bnm[s], bsm[s], -0.5, brc[s], ALU.mult, ALU.mult))
                bmul.end()

            def running_product(q, s, h):
                dve.wait_ge(m_T, q + 1)
                dve.wait_ge(bf_ready, q + 1)
                dve.wait_ge(cont_in[s], 16 * (h + 1))
                wait_past(dve, z3_done, q - 1)
                prod_c.begin(q)
                prod_c.link(v.scalar_tensor_tensor(m, bf[s], kb2[:, :], MT[s][:, :], ALU.add, ALU.mult))
                prod_c.link(v.tensor_tensor(d0, m, cont[s], ALU.mult))
                prod_c.link(v.tensor_tensor(d1, m, d0, ALU.subtract))
                start = 1.0 if isinstance(q, int) and q == 0 else prod[1 - s][:, QE - 1:QE]
                prod_c.link(v.tensor_tensor_scan(prod[s], d0, d1, start, ALU.mult, ALU.add))
                prod_c.end()

            def row_stats(q, s, h):
                dve.wait_ge(row_in[s], 64 * (h + 1))
                dve.wait_ge(ur_in[s], 16 * (h + 1))
                wait_past(dve, c_bmul, 3 * (q - 1))
                bvar.begin(q)
                for j in range(QUAD):
                    bvar.add(v.bn_stats(bst[s][:, j, :], G[:, bass.ds(QUAD * q + j, 1), :]))
                    bvar.add(v.bn_stats(bst[s][:, QUAD + j, :], Ur[s][:, j, :]))
                bvar.settle()
                variance(bvar, bst[s], bsm[s], bdf[s], bv2[s], bdd[s], bV[s])
                bvar.end()

            def step_b(i, s, h):
                q, qs, qh = back(i, s, h, 3)
                if live(q, NQ):
                    finish_rows(q, qs)
                q1_, s1_, h1_ = back(i, s, h, 1)
                if live(q1_, NQ):
                    norm_factors(q1_, s1_)
                q2_, s2_, h2_ = back(i, s, h, 2)
                if live(q2_, NQ):
                    running_product(q2_, s2_, h2_)
                if live(i, NQ):
                    row_stats(i, s, h)
                    dve.wait_ge(c_filter, FILTER_OPS * i + L1_AT)
                    wait_past(dve, z2_done, i)
                    v.scalar_tensor_tensor(h1, Z1[s][:, :], nb1[:, :], l1, ALU.max, ALU.add).then_inc(h1_ready, 1)
                if live(q, NQ):
                    dve.wait_ge(c_yr, 2 * q + 2)
                    v.scalar_tensor_tensor(ynm[qs], ysm[qs], -0.5, yrs[qs], ALU.mult, ALU.mult
                                           ).then_inc(ynm_ready, 1)
                if live(q1_, NQ):
                    dve.wait_ge(hn_ready, q1_ + 1)
                    if isinstance(q1_, int) and q1_ == NQ - 1:
                        dve.wait_ge(attr_in[s1_], 16 * (h1_ + ATTR_LOADS))
                    else:
                        dve.wait_ge(attr_in[s1_], 16 * (h1_ + 1))
                    wait_past(dve, m_T, q1_ - 1)
                    v.tensor_tensor(hm[s1_], hn[s1_], attr_s[s1_], ALU.mult).then_inc(hm_ready, 1)
                if live(i, NQ):
                    dve.wait_ge(c_filter, FILTER_OPS * i + L2_AT)
                    v.scalar_tensor_tensor(bf[s], Z2[s][:, :], nb2[:, :], l2, ALU.max, ALU.add).then_inc(bf_ready, 1)

            sweep(dve, *B, step_b)

        @block.scalar
        def _(act):
            a = nc.scalar.activation
            one = ones[:, 0:1]
            act.wait_ge(cut_t, 1)
            a(cut[:, :], tmp_t[:, :], ACT.Sin, bias=halfpi[:, :], scale=-PI).then_inc(cut_sin, 1)
            nc.scalar.preload_act_table_set("natural_log_exp_and_others")
            act.wait_ge(setup_pe, 1)
            setup = Chain(act, setup_act, 3)
            setup.begin(0)
            setup.link(a(ctmp[:, :], E0[:, 0:F], ACT.Abs))
            setup.link(a(ctmp2[:, :], ctmp[:, :], ACT.Exp, scale=-1.0))
            setup.link(a(ctmp[:, :], ctmp2[:, :], ACT.Ln, bias=one))
            setup.end()
            act.wait_ge(const_ready, 2)

            r_c, r2_c, qs_c = Chain(act, c_r, 3), Chain(act, c_r2, 2), Chain(act, c_qsum, OCT)

            def second_rstd(i, s):
                act.wait_ge(c_var2, VAR2_OPS * i + VAR2_AT)
                r2_c.begin(i)
                r2_c.link(a(lnv2[s], t4[s], ACT.Ln, bias=ceps[:, :], scale=1.0 / F))
                r2_c.link(a(rstd2[s], lnv2[s], ACT.Exp, scale=-0.5))
                r2_c.end()

            def square_sums(i, s):
                act.wait_ge(d_filled, i + 1)
                qs_c.begin(i)
                for j in range(OCT):
                    wait_past(act, c_qsum, qs_c.base + qs_c.n - 1)
                    qs_c.add(a(ajunk[:, j % 2, :], D[s][j // QUAD][:, (j % QUAD) * P:(j % QUAD + 1) * P], ACT.Square,
                               accum_out=qsum[s][:, j:j + 1]))
                qs_c.end()

            def first_rstd(i, s):
                act.wait_ge(c_var, VAR_OPS * i + V_AT)
                r_c.begin(i)
                r_c.link(a(lnv[s], V[s], ACT.Ln, bias=epst[:, :], scale=1.0 / F))
                r_c.add(a(rstd[s], lnv[s], ACT.Exp, scale=-0.5))
                r_c.add(a(sdev[s], lnv[s], ACT.Exp, scale=0.5))
                r_c.end()

            def dense_out(i, s, h):
                act.wait_ge(d_final, i + 1)
                act.wait_ge(c_var2, VAR2_OPS * i + SCALE_AT)
                wait_past(act, o_stored[s], 16 * h)
                for j in range(OCT):
                    ins = a(oo[s][:, j, :], D[s][j // QUAD][:, (j % QUAD) * P:(j % QUAD + 1) * P], ACT.Copy,
                            scale=scale[s][:, j:j + 1])
                ins.then_inc(o_ready, 1)

            def dense_step(i, s, h):
                k, ks, kh = back(i, s, h, 1)
                if live(k, NO):
                    second_rstd(k, ks)
                if live(i, NO):
                    square_sums(i, s)
                    first_rstd(i, s)
                if live(k, NO):
                    dense_out(k, ks, kh)

            sweep(act, *A1, dense_step)
            act.wait_ge(soft_dve, 11)
            a(decay_c[:, :], da_c[:, :], ACT.Exp).then_inc(soft_act, 1)
            a(bw_c[:, :], db_c[:, :], ACT.Exp).then_inc(soft_act, 1)
            act.wait_ge(soft_act, 2)
            act.sem_inc(decay_ready, 1)
            sweep(act, *A2, dense_step)
            act.wait_ge(o_ready, NO)
            act.sem_inc(a_done, 1)
            act.wait_ge(a_done, 3)
            act.wait_ge(a_stored, 1)

            fil, norm_c, l3_c, yr_c = (Chain(act, c_filter, FILTER_OPS), Chain(act, c_norm_r, 2), Chain(act, c_l3, 3),
                                       Chain(act, c_yr, 2))

            def step_b(i, s, h):
                q, qs, qh = back(i, s, h, 3)
                q1_, s1_, h1_ = back(i, s, h, 1)
                if live(q, NQ):
                    act.wait_ge(z3_done, q + 1)
                    wait_past(act, c_y, Y_OPS * (q - 1) + 1)
                    l3_c.begin(q)
                    l3_c.link(a(ab, Z3[qs][:, :], ACT.Abs))
                    l3_c.link(a(ab, ab, ACT.Exp, scale=-1.0))
                    l3_c.link(a(l3, ab, ACT.Ln, bias=one))
                    l3_c.end()
                if live(i, NQ):
                    act.wait_ge(wrow_in[s], 16 * (h + 1))
                    fil.begin(i)
                    fil.link(a(sq, wrow[s], ACT.Square, bias=muneg[:, :]))
                    wait_past(act, z1_done, i)
                    fil.link(a(e0, sq, ACT.Exp, scale=-float(F)))
                if live(q1_, NQ):
                    act.wait_ge(c_bmul, 3 * q1_ + 3)
                    wait_past(act, hm_ready, q1_ - 1)
                    for j in range(QUAD):
                        ins = a(hn[s1_][:, j, :], G[:, bass.ds(QUAD * q1_ + j, 1), :], ACT.Identity,
                                bias=bnm[s1_][:, j:j + 1], scale=brc[s1_][:, j:j + 1])
                    ins.then_inc(hn_ready, 1)
                    act.wait_ge(ur_in[s1_], 16 * (h1_ + 1))
                    wait_past(act, c_y, Y_OPS * (q1_ - 2) + 2)
                    for j in range(QUAD):
                        ins = a(x1d[s1_][:, j, :], Ur[s1_][:, j, :], ACT.Identity,
                                bias=bnm[s1_][:, QUAD + j:QUAD + j + 1], scale=brc[s1_][:, QUAD + j:QUAD + j + 1])
                    ins.then_inc(x1d_ready, 1)
                if live(i, NQ):
                    act.wait_ge(z1_done, i + 1)
                    fil.link(a(ab, Z1[s][:, :], ACT.Abs, bias=b1c[:, :]))
                    fil.link(a(ab, ab, ACT.Exp, scale=-1.0))
                    wait_past(act, h1_ready, i)
                    fil.link(a(l1, ab, ACT.Ln, bias=one))
                if live(q, NQ):
                    act.wait_ge(c_y, Y_OPS * q + YV_AT)
                    yr_c.begin(q)
                    yr_c.link(a(yln[qs], yV[qs], ACT.Ln, bias=epst[:, :], scale=1.0 / F))
                    yr_c.link(a(yrs[qs], yln[qs], ACT.Exp, scale=-0.5))
                    yr_c.end()
                if live(i, NQ):
                    act.wait_ge(c_bvar, BVAR_OPS * i + BV_AT)
                    norm_c.begin(i)
                    norm_c.link(a(bln[s], bV[s], ACT.Ln, bias=epst[:, :], scale=1.0 / F))
                    norm_c.link(a(brs[s], bln[s], ACT.Exp, scale=-0.5))
                    norm_c.end()
                if live(q, NQ):
                    act.wait_ge(ynm_ready, q + 1)
                    wait_past(act, scattered[qs], 64 * qh)
                    for j in range(QUAD):
                        ins = a(o[qs][:, j, :], y[:, j, :], ACT.Identity, bias=ynm[qs][:, j:j + 1],
                                scale=yrs[qs][:, j:j + 1])
                    ins.then_inc(row_ready, 1)
                if live(i, NQ):
                    act.wait_ge(z2_done, i + 1)
                    fil.link(a(ab, Z2[s][:, :], ACT.Abs, bias=b2c[:, :]))
                    fil.link(a(ab, ab, ACT.Exp, scale=-1.0))
                    wait_past(act, bf_ready, i)
                    fil.link(a(l2, ab, ACT.Ln, bias=one))
                    fil.end()

            sweep(act, *B, step_b)

        @block.tensor
        def _(pe):
            mm = nc.tensor.matmul
            pe.wait_ge(par_in, 16 * 13)
            pe.wait_ge(setup_dve, 5)
            mm(E0[:, 0:F], ones[:, :], w3[:, :], start=True, stop=False)
            mm(E0[:, 0:F], ones[0:1, :], b3row[0:1, 0, :], start=False, stop=True).then_inc(setup_pe, 1)
            pe.wait_ge(const_ready, 1)
            mm(E1[:, 0:1], w2[:, :], b1m[:, :], start=True, stop=True).then_inc(setup_pe, 1)
            pe.wait_ge(const_ready, 2)

            def fill(i, s, h):
                pe.wait_ge(x_in[s], 16 * (h + 1))
                wait_past(pe, o_ready, i - 1)
                for b in range(2):
                    mm(D[s][b][:, :], ident[:, :], xo[s][:, QUAD * b:QUAD * (b + 1), :], start=True, stop=False)
                    ins = mm(D[s][b][:, :], ones3[:, :], c3[:, :, :], start=False, stop=True)
                ins.then_inc(d_filled, 1)

            def transpose_stats(i, s):
                pe.wait_ge(c_var2, VAR2_OPS * i + S1_AT)
                wait_past(pe, stat_copied, i)
                mm(psT[0:16, 0:P], stats[s], ident[:, :], start=True, stop=True).then_inc(stat_T, 1)

            def add_terms(i, s):
                pe.wait_ge(stat_copied, i + 1)
                pe.wait_ge(c_qsum, OCT * i + OCT)
                for b in range(2):
                    ins = mm(D[s][b][:, :], statsT[s], rhs_sel[:, QUAD * b:QUAD * (b + 1), :], start=False, stop=True,
                             skip_group_check=True)
                ins.then_inc(d_final, 1)

            def find(q, s):
                pe.wait_ge(ge_ready, q + 1)
                wait_past(pe, find_used, 2 * q)
                for j in range(QUAD):
                    for g in range(2):
                        ins = mm(psF[j // 2][:, (j % 2) * (P + 1):(j % 2 + 1) * (P + 1)],
                                 ge[s][:, g, j * P:(j + 1) * P], dcode[:, g, :], start=(g == 0), stop=(g == 1))
                ins.then_inc(found, 1)

            pe.wait_ge(find_setup, 1)

            def step_a1(i, s, h):
                k, ks, kh = back(i, s, h, 1)
                if live(k, NO):
                    transpose_stats(k, ks)
                fill(i, s, h)
                if live(k, NO):
                    add_terms(k, ks)
                find(i, s)

            sweep(pe, *A1, step_a1)

            eh, e1_ = ident[0:H, 0:H], ones[0:1, 0:1]
            pe.wait_ge(soft_dve, 1)
            nc.tensor.transpose(E0[0:H, 0:P], score[:, 0:NT:2], ident[:, :]).then_inc(soft_pe, 1)
            nc.tensor.transpose(E0[0:H, P:2 * P], score[:, 1:NT:2], ident[:, :]).then_inc(soft_pe, 1)
            pe.wait_ge(soft_dve, 3)
            mm(E1[0:1, 0:H], max_c[:, 256:257], eh, start=True, stop=True).then_inc(soft_pe, 1)
            mm(E1[0:1, P:P + H], pass_c[:, 1:2], eh, start=True, stop=True).then_inc(soft_pe, 1)
            pe.wait_ge(soft_dve, 6)
            mm(E2[0:H, 0:1], carry_row[0:1, 0:H], e1_, start=True, stop=True).then_inc(soft_pe, 1)
            pe.wait_ge(soft_dve, 13)
            mm(E1[0:1, 0:H], den_c[:, 255:256], eh, start=True, stop=True).then_inc(soft_pe, 1)
            mm(E1[0:1, P:P + H], da_c[:, 255:256], eh, start=True, stop=True).then_inc(soft_pe, 1)
            pe.wait_ge(soft_dve, 16)
            mm(E2[0:H, 0:1], carry_row[0:1, 0:H], e1_, start=True, stop=True).then_inc(soft_pe, 1)
            pe.wait_ge(soft_dve, 20)
            for bank, src in ((E0, bw_c), (E1, den_c)):
                for g in range(2):
                    nc.tensor.transpose(bank[:, g * H:(g + 1) * H], src[:, g * P:(g + 1) * P], eh
                                        ).then_inc(soft_pe, 1)

            def step_a2(i, s, h):
                k, ks, kh = back(i, s, h, 1)
                if live(k, NO):
                    transpose_stats(k, ks)
                if live(i, NO):
                    fill(i, s, h)
                if live(k, NO):
                    add_terms(k, ks)
                q, qs, qh = back(i, s, h, NQ)
                if live(q, NQ):
                    pe.wait_ge(bx_ready, q + 1)
                    wait_past(pe, scan_done, q - 1)
                    for j in range(QUAD):
                        ins = nc.tensor.transpose(psX[qs][:, j * P:(j + 1) * P], bx[qs][:, j, :], ident[:, :])
                    ins.then_inc(bx_T, 1)
                q, qs, qh = back(i, s, h, NQ + 1)
                if live(q, NQ):
                    pe.wait_ge(scan_done, q + 1)
                    wait_past(pe, u_ready, q)
                    for j in range(QUAD):
                        ins = nc.tensor.transpose(psR[:, j * P:(j + 1) * P], RT[qs][:, j * P:(j + 1) * P],
                                                  ident[:, :])
                    ins.then_inc(r_T, 1)

            sweep(pe, *A2, step_a2)
            pe.wait_ge(r_T, NQ)
            pe.sem_inc(a_done, 1)
            pe.wait_ge(a_done, 3)
            pe.wait_ge(a_stored, 1)

            def step_b(i, s, h):
                if live(i, NQ):
                    pe.wait_ge(c_filter, FILTER_OPS * i + E0_AT)
                    wait_past(pe, h1_ready, i - 1)
                    mm(Z1[s][:, :], w1[:, :], e0, start=True, stop=True).then_inc(z1_done, 1)
                q, qs, qh = back(i, s, h, 2)
                if live(q, NQ):
                    pe.wait_ge(c_prod, PROD_OPS * q + PROD_AT)
                    wait_past(pe, c_y, Y_OPS * (q - 2) + 1)
                    mm(Z3[qs][:, :], ones[0:1, :], b3row[0:1, :, :], start=True, stop=False)
                    for j in range(QUAD):
                        ins = mm(Z3[qs][:, j * P:(j + 1) * P], prod[qs][:, j * P:(j + 1) * P], w3[:, :],
                                 start=False, stop=(j == QUAD - 1))
                    ins.then_inc(z3_done, 1)
                if live(i, NQ):
                    pe.wait_ge(h1_ready, i + 1)
                    wait_past(pe, bf_ready, i - 1)
                    mm(Z2[s][:, :], w2[:, :], h1, start=True, stop=True).then_inc(z2_done, 1)
                q, qs, qh = back(i, s, h, 1)
                if live(q, NQ):
                    pe.wait_ge(hm_ready, q + 1)
                    wait_past(pe, c_prod, PROD_OPS * (q - 2) + 1)
                    for j in range(QUAD):
                        ins = nc.tensor.transpose(MT[qs][:, j * P:(j + 1) * P], hm[qs][:, j, :], ident[:, :])
                    ins.then_inc(m_T, 1)

            sweep(pe, *B, step_b)


def kernel(x, src, dst, edge_attr_128, edge_weight, L0_gnn_W, L1_gnn_W1, L1_gnn_b1, L1_gnn_W2, L1_gnn_b2, L1_gnn_W3,
           L1_gnn_b3):
    import numpy as np
    import concourse.bacc as bacc
    from concourse.bass_utils import run_bass_kernel_spmd

    x, src, dst, attr, weight = (np.ascontiguousarray(a) for a in (x, src, dst, edge_attr_128, edge_weight))
    N, E = x.shape[0], src.shape[0]
    NT = -(-E // QE) * QUAD
    pad = NT * P - E

    def tiles(a):
        return np.ascontiguousarray(a.reshape(NT, P).T)

    src_flat = np.pad(src, (0, pad))
    weight_flat = np.pad(weight, (0, pad), constant_values=2 * CUTOFF)
    dst_flat = np.pad(np.pad(dst, (0, pad), constant_values=N), (P, 1), constant_values=-1)
    arrays = {
        "x": x, "src_tiles": tiles(src_flat), "dst_tiles": tiles(dst_flat[P:-1]), "next_tiles": tiles(dst_flat[P + 1:]),
        "weight_tiles": tiles(weight_flat), "src_flat": src_flat, "dst_flat": dst_flat, "weight_flat": weight_flat,
        "attr": attr, "W0": L0_gnn_W, "W1": L1_gnn_W1, "b1": L1_gnn_b1, "W2": L1_gnn_W2, "b2": L1_gnn_b2,
        "W3": L1_gnn_W3, "b3": L1_gnn_b3, "eye": np.eye(P, dtype=np.float32),
        "iota1": np.ascontiguousarray(np.broadcast_to(np.arange(1, P + 1, dtype=np.float32), (P, P))),
        "mu": -np.linspace(0.0, 1.0, P, dtype=np.float32)[:, None],
    }
    arrays = {f"in_{k}": np.ascontiguousarray(a) for k, a in arrays.items()}
    nc = bacc.Bacc("TRN2", target_bir_lowering=False, num_devices=1)
    args = [nc.dram_tensor(k, a.shape, mybir.dt.from_np(a.dtype), kind="ExternalInput").ap() for k, a in arrays.items()]
    args.append(nc.dram_tensor("out_dram", x.shape, mybir.dt.float32, kind="ExternalOutput").ap())
    gnn_kernel(nc, *args)
    r = run_bass_kernel_spmd(nc, [arrays], core_ids=[0])
    return r.results[0]["out_dram"]
```

```python
import concourse.bass as bass
from concourse import mybir
from contextlib import ExitStack

P = 128
OCT = 8
QUAD = 4
QE = QUAD * P
EPS = 1e-5
BIG = 1e37
SKIP = 1 << 20
LN2 = 0.6931471805599453
ONSET, CUTOFF = 0.8, 1.0
CODE = 8.0
RND = 1.5 * 2.0 ** 34
PI = 3.141592653589793


def live(q, n):
    return not isinstance(q, int) or 0 <= q < n


def wait_past(eng, sem, value):
    if not isinstance(value, int) or value > 0:
        eng.wait_ge(sem, value)


def sweep(eng, start, lo, hi, stop, body):
    for i in range(start, min(lo, stop)):
        body(i, i % 2, i // 2)
    if hi > lo:
        with eng.Fori(lo // 2, hi // 2) as half:
            body(2 * half, 0, half)
            body(2 * half + 1, 1, half)
    for i in range(max(hi, lo), stop):
        body(i, i % 2, i // 2)


def back(i, slot, half, k):
    return i - k, (slot - k) % 2, half + (slot - k) // 2


class Chain:

    def __init__(self, eng, sem, size):
        self.eng, self.sem, self.size = eng, sem, size

    def begin(self, q):
        self.base, self.n = self.size * q, 0

    def add(self, ins):
        self.n += 1
        ins.then_inc(self.sem, 1)

    def settle(self):
        self.eng.wait_ge(self.sem, self.base + self.n)

    def link(self, ins):
        self.add(ins)
        self.settle()

    def end(self):
        assert self.n == self.size, (self.n, self.size)


def gnn_kernel(nc, x, src_tiles, dst_tiles, next_tiles, weight_tiles, src_flat, dst_flat, weight_flat, attr,
               W0, W1, b1, W2, b2, W3, b3, eye, iota1, mu, out):
    F32, BF16, F16, I32 = mybir.dt.float32, mybir.dt.bfloat16, mybir.dt.float16, mybir.dt.int32
    ALU, ACT, AX = mybir.AluOpType, mybir.ActivationFunctionType, mybir.AxisListType

    N, F = x.shape
    E = attr.shape[0]
    NT = src_tiles.shape[1]
    NQ = NT // QUAD
    H = NT // 2
    OROWS = OCT * P
    NO = -(-N // OROWS)
    assert (2 * N + 4096) / CODE < 65504
    TERMS = 3 * 4 * OCT
    assert NO == 2 * NQ and H <= P and F == P and N >= OROWS

    node_rows = nc.dram_tensor("node_rows", [NT * P, F], F32).ap()
    decay_flat = nc.dram_tensor("decay_flat", [NT * P], F32).ap()
    cont_flat = nc.dram_tensor("cont_flat", [NT * P], F32).ap()

    ctx = ExitStack()
    with ctx:
        def sb(name, shape, dt=F32):
            return ctx.enter_context(nc.sbuf_tensor(name, shape, dt))

        def sem(name):
            return ctx.enter_context(nc.semaphore(name))

        def sem2(name):
            return [sem(name + "_0"), sem(name + "_1")]

        G = sb("gathered", [P, NT, F])
        src_i = sb("src_i", [P, NT], I32)
        dst_i = sb("dst_i", [P, NT], I32)
        next_i = sb("next_i", [P, NT], I32)
        xd_idx = sb("xd_idx", [P, NT], I32)
        out_idx = sb("out_idx", [P, NT], I32)
        row_idx = sb("row_idx", [P, NT], I32)
        src_code = sb("src_code", [P, NT])
        wt = sb("wt", [P, NT])
        cut = sb("cut", [P, NT])
        score = sb("score", [P, NT])
        hit = sb("hit", [P, NT])
        tile1 = sb("tile1", [P, NT])
        tmp_t = sb("tmp_t", [P, NT])
        bw = sb("bw", [P, NT])
        rden = sb("rden", [P, NT])
        rnode = sb("rnode", [P, NT])
        ident = sb("ident", [P, P])
        iota = sb("iota", [P, P])
        ones = sb("ones", [P, P])
        w0 = sb("w0", [P, P])
        w1, w2, w3 = (sb(n, [P, P]) for n in ("w1s", "w2s", "w3s"))
        muneg = sb("muneg", [P, 1])
        b1c, b2c, nb1, nb2, kb2, b1m = (sb(n, [P, 1]) for n in ("b1c", "b2c", "nb1", "nb2", "kb2", "b1m"))
        b3row = sb("b3row", [1, F])
        b3all, b3sum = sb("b3all", [3, F]), sb("b3sum", [3, F])
        b3part = sb("b3part", [3, F], BF16)
        b3parts = sb("b3parts", [3, QUAD, F], BF16)
        epst = sb("epst", [P, 1])
        halfpi = sb("halfpi", [P, 1])
        crow = sb("crow", [P, F])
        ctmp = sb("ctmp", [P, F])
        ctmp2 = sb("ctmp2", [P, F])
        cstat = sb("cstat", [P, 6])
        cneg2 = sb("cneg2", [P, 1])
        ceps = sb("ceps", [P, 1])
        c3 = sb("c3", [3, QUAD, F], BF16)
        ones3 = sb("ones3", [3, P], BF16)
        ident_bf = sb("ident_bf", [P, P], BF16)
        rhs_sel = sb("rhs_sel", [TERMS, OCT, F], BF16)
        blk, kind, kind12, cterm = (sb(n, [TERMS, k]) for n, k in (("blk", OCT), ("kind", 4), ("kind12", 12),
                                                                   ("cterm", F)))
        junk = sb("junk", [P, 4, F])
        ajunk = sb("ajunk", [P, 2, F])

        dst_c, prev_c = (sb(n, [H, 256], I32) for n in ("dst_c", "prev_c"))
        cont_c, pen_c, score_c, da_c, db_c, decay_c, bw_c, den_c = (
            sb(n, [H, 256]) for n in ("cont_c", "pen_c", "score_c", "da_c", "db_c", "decay_c", "bw_c", "den_c"))
        max_c = sb("max_c", [H, 257])
        zero_c = sb("zero_c", [H, 256])
        pass_c = sb("pass_c", [H, 2])
        rowbuf = sb("rowbuf", [1, 2 * P])
        carry_row = sb("carry_row", [1, P + 1])
        carry_c = sb("carry_c", [H, 1])

        WORK = 33 * QE
        work = sb("work", [P, WORK])
        used = [0]

        def take(*free, parts=P, dt=F32):
            n = 1
            for f in free:
                n *= f
            v = work[0:parts, used[0]:used[0] + n]
            used[0] += n
            assert used[0] <= WORK
            if dt is not F32:
                v = v.bitcast(dt)
            return v.rearrange("p (a b) -> p a b", b=free[1]) if len(free) == 2 else v

        def take2(*free, **kw):
            return [take(*free, **kw) for _ in range(2)]

        xo, oo = take2(OCT, F), take2(OCT, F)
        st = take2(OCT, 6)
        (sm, df, v2, dd, V, q1, q2, t1, t2, t3, t4, lnv, rstd, sdev, lnv2, rstd2, scale, qsum) = (
            take2(OCT) for _ in range(18))
        stats = take2(4, OCT)
        rest1, rest2 = take2(4 * OCT), take2(4 * OCT)
        parts = take2(TERMS // 2, dt=BF16)
        statsT = take2(P // 2, parts=TERMS, dt=BF16)
        srcrow = take2(QE, parts=H, dt=I32)
        ge = [take(QE, parts=H, dt=F16).rearrange("p (g e) -> p g e", g=2) for _ in range(2)]
        drow_i, dnext_i, prow_i, pnext_i = (take(2, P, parts=H, dt=I32) for _ in range(4))
        dfirst = take(2, parts=H)
        dcode, dprev, dlow = (take(2, P + 1, parts=H) for _ in range(3))
        dhigh, drest = [take(P + 2, parts=H, dt=F16).rearrange("p (g e) -> p g e", g=2) for _ in range(2)]
        arow, bx, RT, xd, U = take2(QE), take2(QUAD, F), take2(QE), take2(QUAD, F), take2(QUAD, F)
        used[0] = 0
        wrow, attr_s, first_nodes, cont = take2(QE), take2(QUAD, F), take2(QUAD, F), take2(QE)
        e0 = take(QE)
        l1, l2, l3 = take(QE), take(QE), take(QE)
        h1 = take(QE)
        bf = take2(QE)
        hn, hm = take2(QUAD, F), take2(QUAD, F)
        m, d0, d1 = take(QE), take(QE), take(QE)
        prod = take2(QE)
        t_, y = take(QE), take(QUAD, F)
        o = take2(QUAD, F)
        bst = take2(2 * QUAD, 6)
        (bsm, bdf, bv2, bdd, bV, bln, brs) = (take2(2 * QUAD) for _ in range(7))
        brc, bnm = take2(QUAD), take2(QUAD)
        yst = take2(QUAD, 6)
        (ysm, ydf, yv2, ydd, yV, yln, yrs, ynm) = (take2(QUAD) for _ in range(8))

        banks = [ctx.enter_context(nc.psum_tensor(f"bank{i}", [P, 512], F32)) for i in range(8)]
        D = [banks[0:2], banks[2:4]]
        psT = banks[4]
        psF = banks[5:7]
        psX = banks[5:7]
        psR = banks[7]
        E0, E1, E2 = banks[5], banks[6], banks[7]
        Z1, Z2, MT, Z3 = banks[0:2], banks[2:4], banks[4:6], banks[6:8]

        idx_in, tab_in, par_in = sem("idx_in"), sem("tab_in"), sem("par_in")
        setup_dve, setup_pe, setup_act = sem("setup_dve"), sem("setup_pe"), sem("setup_act")
        idx_ready, find_setup, cont_ready, cut_t, cut_sin, const_ready = (
            sem(n) for n in ("idx_ready", "find_setup", "cont_ready", "cut_t", "cut_sin", "const_ready"))
        x_in, o_stored = sem2("x_in"), sem2("o_stored")
        d_filled, o_ready = sem2("d_filled"), sem2("o_ready")
        bn_done, stat_T, stat_copied, d_final = (sem(n) for n in ("bn_done", "stat_T", "stat_copied", "d_final"))
        c_split = sem("c_split")
        c_var, c_var2, c_r, c_r2, c_found, c_score, c_qsum = (
            sem(n) for n in ("c_var", "c_var2", "c_r", "c_r2", "c_found", "c_score", "c_qsum"))
        g_in, srcrow_in = sem2("g_in"), sem2("srcrow_in")
        ge_ready, found, find_used, rows_found = (sem(n) for n in ("ge_ready", "found", "find_used", "rows_found"))
        soft_dve, soft_pe, soft_act, decay_ready, decay_stored, cont_stored = (
            sem(n) for n in ("soft_dve", "soft_pe", "soft_act", "decay_ready", "decay_stored", "cont_stored"))
        arow_in, xd_in, u_stored = sem2("arow_in"), sem2("xd_in"), sem2("u_stored")
        bx_ready, bx_T, scan_done, r_T, u_ready = (sem(n) for n in ("bx_ready", "bx_T", "scan_done", "r_T", "u_ready"))
        a_done, a_stored = sem("a_done"), sem("a_stored")
        wrow_in, attr_in, ur_in, cont_in = sem2("wrow_in"), sem2("attr_in"), sem2("ur_in"), sem2("cont_in")
        row_in, scattered = sem2("row_in"), sem2("scattered")
        c_basis, c_l1, c_l2, c_norm_r, c_bvar, c_bmul = (
            sem(n) for n in ("c_basis", "c_l1", "c_l2", "c_norm_r", "c_bvar", "c_bmul"))
        z1_done, h1_ready, z2_done, bf_ready, hn_ready, hm_ready, m_T = (
            sem(n) for n in ("z1_done", "h1_ready", "z2_done", "bf_ready", "hn_ready", "hm_ready", "m_T"))
        c_prod, z3_done, c_l3, c_y, c_yr, ynm_ready, row_ready = (
            sem(n) for n in ("c_prod", "z3_done", "c_l3", "c_y", "c_yr", "ynm_ready", "row_ready"))

        def octet_rows(i):
            return x[bass.ds(i * OROWS, OROWS), :].rearrange("(p j) f -> p j f", j=OCT)

        def quad_rows(t, q):
            return t[bass.ds(q * QE, QE), :].rearrange("(j p) f -> p j f", p=P)

        def node_tiles(q):
            return first_nodes[q] if isinstance(q, int) and q < 2 else G[:, bass.ds(QUAD * (q - 2), QUAD), :]

        LAST = N - OROWS
        FRESH = (NO - 1) * OROWS - LAST
        assert FRESH % OCT == 0

        VAR_OPS, V_AT = 8, 7
        VAR2_OPS, VAR2_AT, SCALE_AT = 5, 4, 5
        SPLIT_OPS = 6
        BVAR_OPS, BV_AT = 13, 13
        PROD_OPS, PROD_AT = 4, 4
        Y_OPS, YV_AT = 14, 14

        A1 = (0, 4, 4 + (NQ - 4) // 2 * 2, NQ)
        a2lo = NQ + 4 + NQ % 2
        A2 = (NQ, a2lo, max(a2lo, NO - 2), NO + 2)
        blo = 6
        B = (0, blo, max(blo, NQ // 2 * 2), NQ + 3)

        block = ctx.enter_context(nc.Block())

        @block.sync
        def _(sp):
            sp.dma_start(src_i[:, :], src_tiles).then_inc(idx_in, 16)
            for dst, src in ((dst_i, dst_tiles), (next_i, next_tiles), (wt, weight_tiles)):
                sp.dma_start(dst[:, :], src).then_inc(tab_in, 16)
            rows = "(k g j) -> k g j"
            base = P
            for dst, off in ((drow_i, 0), (dnext_i, 1), (prow_i, -P), (pnext_i, 1 - P)):
                for g in range(2):
                    v = dst_flat[base + off + g * H * P:base + off + (g + 1) * H * P].rearrange("(k j) -> k j", j=P)
                    sp.dma_start(dst[:, g, :], v).then_inc(tab_in, 16)
            for dst, off in ((dst_c, 0), (prev_c, -1)):
                sp.dma_start(dst[:, :], dst_flat[base + off:base + off + NT * P].rearrange("(k j) -> k j", j=256)
                             ).then_inc(tab_in, 16)
            for dst, src in ((ident, eye), (iota, iota1), (w1, W1), (w2, W2), (w3, W3), (muneg, mu),
                             (b1c, b1.rearrange("(p a) -> p a", a=1)), (b2c, b2.rearrange("(p a) -> p a", a=1))):
                sp.dma_start(dst[:, :], src).then_inc(par_in, 16)
            sp.dma_start(w0[:, :], W0[0, :].partition_broadcast(P)).then_inc(par_in, 16)
            sp.dma_start(b3row[:, :], b3.rearrange("(a f) -> a f", a=1)).then_inc(par_in, 16)
            sp.dma_start(b3all[:, :], b3.partition_broadcast(3)).then_inc(par_in, 16)

            def load_dense(i, slot, half):
                wait_past(sp, bn_done, i - 1)
                wait_past(sp, d_filled[1], i - 1)
                if isinstance(i, int) and i == NO - 1:
                    rows_ = x[LAST:N, :].rearrange("(p j) f -> p j f", j=OCT)
                else:
                    rows_ = octet_rows(i)
                sp.dma_start(xo[slot], rows_).then_inc(x_in[slot], 16)

            def store_dense(i, slot, half):
                sp.wait_ge(o_ready[1], i + 1)
                if isinstance(i, int) and i == NO - 1:
                    skip = FRESH // OCT
                    rows_ = out[(NO - 1) * OROWS:N, :].rearrange("(p j) f -> p j f", j=OCT)
                    sp.dma_start(rows_, oo[slot][skip:P]).then_inc(o_stored[slot], 16)
                else:
                    rows_ = out[bass.ds(i * OROWS, OROWS), :].rearrange("(p j) f -> p j f", j=OCT)
                    sp.dma_start(rows_, oo[slot]).then_inc(o_stored[slot], 16)

            def ahead(i, slot, half):
                return i + 1, 1 - slot, half + slot

            def load_sources(i, slot, half):
                wait_past(sp, ge_ready, i - 1)
                sp.dma_start(srcrow[slot], src_flat[bass.ds(i * QE, QE)].partition_broadcast(H)
                             ).then_inc(srcrow_in[slot], 16)

            def step_a1(i, slot, half):
                n, s, h = ahead(i, slot, half)
                if live(n, NQ):
                    load_sources(n, s, h)
                load_dense(n, s, h)
                k, s, h = back(i, slot, half, 2)
                if live(k, NO):
                    store_dense(k, s, h)

            def step_a2(i, slot, half):
                n, s, h = ahead(i, slot, half)
                if live(n, NO):
                    load_dense(n, s, h)
                q, s, h = back(i, slot, half, NQ)
                if live(q, NQ):
                    wait_past(sp, scan_done, q - 1)
                    sp.dma_start(arow[s], decay_flat[bass.ds(q * QE, QE)].partition_broadcast(P)
                                 ).then_inc(arow_in[s], 16)
                k, s, h = back(i, slot, half, 2)
                if live(k, NO):
                    store_dense(k, s, h)
                q, s, h = back(i, slot, half, NQ + 2)
                if live(q, NQ):
                    store_u(q, s)

            def store_u(q, s):
                sp.wait_ge(u_ready, q + 1)
                sp.dma_start(quad_rows(node_rows, q), U[s]).then_inc(u_stored[s], 16)

            load_sources(0, 0, 0)
            load_dense(0, 0, 0)
            sweep(sp, *A1, step_a1)
            sp.wait_ge(cont_ready, 1)
            sp.dma_start(cont_flat.rearrange("(k j) -> k j", j=256), cont_c[:, :]).then_inc(cont_stored, 16)
            sp.wait_ge(decay_ready, 1)
            sp.dma_start(decay_flat.rearrange("(k j) -> k j", j=256), decay_c[:, :]).then_inc(decay_stored, 16)
            sp.wait_ge(cont_stored, 16)
            sp.wait_ge(decay_stored, 16)
            sweep(sp, *A2, step_a2)
            for s in range(2):
                sp.wait_ge(o_stored[s], 16 * (NO // 2))
                sp.wait_ge(u_stored[s], 16 * ((NQ + 1 - s) // 2))
            sp.sem_inc(a_stored, 1)
            sp.wait_ge(a_done, 3)

            def step_b(q, slot, half):
                wait_past(sp, z1_done, q - 1)
                sp.dma_start(wrow[slot], weight_flat[bass.ds(q * QE, QE)].partition_broadcast(P)
                             ).then_inc(wrow_in[slot], 16)
                wait_past(sp, hn_ready, q - 1)
                sp.dma_start(node_tiles(q), quad_rows(node_rows, q)).then_inc(ur_in[slot], 16)
                wait_past(sp, hm_ready, q - 1)
                if isinstance(q, int) and q == NQ - 1:
                    whole, rest = divmod(E - q * QE, P)
                    for j in range(whole):
                        r = q * QE + j * P
                        sp.dma_start(attr_s[slot][:, j, :], attr[r:r + P, :]).then_inc(attr_in[slot], 16)
                    if rest:
                        sp.dma_start(attr_s[slot][0:rest, whole, :], attr[E - rest:E, :]).then_inc(attr_in[slot], 16)
                else:
                    sp.dma_start(attr_s[slot], quad_rows(attr, q)).then_inc(attr_in[slot], 16)
                k, s, h = back(q, slot, half, 1)
                if live(k, NQ):
                    load_flags(k, s)

            def load_flags(q, slot):
                wait_past(sp, z3_done, q - 1)
                sp.dma_start(cont[slot], cont_flat[bass.ds(q * QE, QE)].partition_broadcast(P)
                             ).then_inc(cont_in[slot], 16)

            sweep(sp, 0, B[1], max(B[1], (NQ - 1) // 2 * 2), NQ, step_b)
            load_flags(NQ - 1, (NQ - 1) % 2)

        ATTR_LOADS = -(-(E - (NQ - 1) * QE) // P)

        @block.gpsimd
        def _(pool):
            pool.wait_ge(idx_in, 16)

            def gather(dst, table, idx, t, bound, s):
                nc.gpsimd.indirect_dma_start(dst, None, table, bass.IndirectOffsetOnAxis(ap=idx[:, t:t + 1], axis=0),
                                             bounds_check=bound, oob_is_err=False).then_inc(s, 16)

            for q in range(NQ):
                wait_past(pool, g_in[q % 2], 64 * (q // 2))
                for t in range(QUAD * q, QUAD * q + QUAD):
                    gather(G[:, t, :], x, src_i, t, N - 1, g_in[q % 2])
            pool.wait_ge(idx_ready, 1)
            for q in range(NQ):
                wait_past(pool, u_ready, q - 1)
                wait_past(pool, xd_in[q % 2], 64 * (q // 2))
                for j in range(QUAD):
                    gather(xd[q % 2][:, j, :], x, xd_idx, QUAD * q + j, N - 1, xd_in[q % 2])
            pool.wait_ge(rows_found, 1)
            pool.wait_ge(a_stored, 1)
            for s in range(2):
                pool.wait_ge(g_in[s], 64 * ((NQ + 1 - s) // 2))
            LEAD = 6
            for q in range(NQ + LEAD):
                if q < NQ:
                    wait_past(pool, row_in[q % 2], 64 * (q // 2))
                    for t in range(QUAD * q, QUAD * q + QUAD):
                        gather(G[:, t, :], node_rows, row_idx, t, NT * P - 1, row_in[q % 2])
                if q >= LEAD:
                    k = q - LEAD
                    pool.wait_ge(row_ready, k + 1)
                    wait_past(pool, scattered[k % 2], 64 * (k // 2))
                    for j in range(QUAD):
                        t = QUAD * k + j
                        nc.gpsimd.indirect_dma_start(
                            out, bass.IndirectOffsetOnAxis(ap=out_idx[:, t:t + 1], axis=0), o[k % 2][:, j, :], None,
                            bounds_check=N - 1, oob_is_err=False).then_inc(scattered[k % 2], 16)
            for s in range(2):
                pool.wait_ge(scattered[s], 64 * ((NQ + 1 - s) // 2))

        @block.vector
        def _(dve):
            v = nc.vector
            ch = Chain(dve, setup_dve, 0)
            ch.begin(0)
            ch.add(v.memset(ones[:, :], 1.0))
            ch.add(v.memset(ones3[:, :], 1.0))
            ch.add(v.memset(epst[:, :], EPS))
            ch.add(v.memset(halfpi[:, :], PI / 2))
            ch.add(v.memset(zero_c[:, :], 0.0))
            ch.settle()
            assert ch.n == 5
            dve.wait_ge(idx_in, 16)
            dve.wait_ge(tab_in, 16 * 13)
            ch.add(v.tensor_scalar(xd_idx[:, :], dst_i[:, :], float(N - 1), None, ALU.min))
            ch.add(v.tensor_tensor(tmp_t[:, :], dst_i[:, :], next_i[:, :], ALU.is_equal))
            ch.add(v.tensor_scalar(src_code[:, :], src_i[:, :], 2.0 / CODE, 1.0 / CODE, ALU.mult, ALU.add))
            ch.settle()
            ch.link(v.scalar_tensor_tensor(out_idx[:, :], tmp_t[:, :], float(SKIP), dst_i[:, :], ALU.mult, ALU.add))
            v.sem_inc(idx_ready, 1)
            for rows_, nxt, code in ((drow_i, dnext_i, dcode), (prow_i, pnext_i, dprev)):
                ch.link(v.tensor_tensor(code[:, :, 0:P], rows_, nxt, ALU.is_equal))
                ch.link(v.tensor_scalar(code[:, :, 0:P], code[:, :, 0:P], -1.0, 1.0, ALU.mult, ALU.add))
                ch.link(v.scalar_tensor_tensor(code[:, :, 0:P], rows_, 2.0, code[:, :, 0:P], ALU.mult, ALU.add))
            ch.link(v.memset(dprev[0:1, 0, 0:P], 0.0))
            ch.link(v.tensor_tensor(dcode[:, :, 0:P], dcode[:, :, 0:P], dprev[:, :, 0:P], ALU.subtract))
            ch.link(v.tensor_scalar(dprev[:, :, 0:P], dcode[:, :, 0:P], RND, None, ALU.add))
            ch.link(v.tensor_scalar(dprev[:, :, 0:P], dprev[:, :, 0:P], -RND, None, ALU.add))
            ch.link(v.tensor_tensor(dlow[:, :, 0:P], dcode[:, :, 0:P], dprev[:, :, 0:P], ALU.subtract))
            for part, of in ((dhigh, dprev), (drest, dlow)):
                ch.add(v.tensor_scalar(part[:, :, 0:P], of[:, :, 0:P], 1.0 / CODE, None, ALU.mult))
            ch.add(v.memset(dhigh[:, :, P:P + 1], 1.0))
            ch.add(v.memset(drest[:, :, P:P + 1], 0.0))
            ch.add(v.tensor_copy(dfirst.unsqueeze(2), drow_i[:, :, 0:1]))
            ch.settle()
            v.sem_inc(find_setup, 1)
            ch.link(v.tensor_tensor(cont_c[:, :], dst_c[:, :], prev_c[:, :], ALU.is_equal))
            ch.add(v.tensor_scalar(pen_c[:, :], cont_c[:, :], -1.0, BIG, ALU.add, ALU.mult))
            ch.link(v.tensor_reduce(pass_c[:, 0:1], cont_c[:, :], AX.X, ALU.min))
            ch.link(v.tensor_scalar(pass_c[:, 1:2], pass_c[:, 0:1], -1.0, BIG, ALU.add, ALU.mult))
            v.sem_inc(cont_ready, 1)
            ch.link(v.tensor_scalar(tmp_t[:, :], wt[:, :], -ONSET, 1.0 / (CUTOFF - ONSET), ALU.add, ALU.mult))
            ch.link(v.tensor_scalar(tmp_t[:, :], tmp_t[:, :], 0.0, 1.0, ALU.max, ALU.min))
            v.sem_inc(cut_t, 1)
            dve.wait_ge(cut_sin, 1)
            ch.link(v.tensor_scalar(tmp_t[:, :], cut[:, :], 0.5, 0.5, ALU.mult, ALU.add))
            ch.link(v.tensor_scalar(cut[:, :], wt[:, :], ONSET, None, ALU.is_lt))
            ch.link(v.tensor_tensor(tmp_t[:, :], tmp_t[:, :], cut[:, :], ALU.max))
            ch.link(v.tensor_scalar(cut[:, :], wt[:, :], CUTOFF, None, ALU.is_le))
            ch.link(v.tensor_tensor(cut[:, :], cut[:, :], tmp_t[:, :], ALU.mult))
            dve.wait_ge(par_in, 16 * 11)
            ch.add(v.tensor_scalar(nb1[:, :], b1c[:, :], -1.0, None, ALU.mult))
            ch.link(v.tensor_scalar(b1m[:, :], b1c[:, :], -LN2, None, ALU.add))
            v.sem_inc(const_ready, 1)
            dve.wait_ge(setup_pe, 2)
            ch.link(v.tensor_tensor(b2c[:, :], b2c[:, :], E1[:, 0:1], ALU.add))
            ch.add(v.tensor_scalar(nb2[:, :], b2c[:, :], -1.0, None, ALU.mult))
            ch.add(v.tensor_scalar(kb2[:, :], b2c[:, :], -LN2, None, ALU.add))
            dve.wait_ge(setup_act, 3)
            ch.link(v.scalar_tensor_tensor(crow[:, :], E0[:, 0:F], 0.0, ctmp[:, :], ALU.max, ALU.add))
            ch.link(v.tensor_scalar(crow[:, :], crow[:, :], -LN2, None, ALU.add))
            ch.link(v.tensor_reduce(ceps[:, :], crow[:, :], AX.X, ALU.add))
            ch.link(v.tensor_scalar(ceps[:, :], ceps[:, :], -1.0 / F, None, ALU.mult))
            ch.link(v.tensor_scalar(crow[:, :], crow[:, :], ceps[:, :], None, ALU.add))
            ch.link(v.tensor_tensor(ctmp[:, :], crow[:, :], crow[:, :], ALU.mult))
            ch.link(v.tensor_reduce(cneg2[:, :], ctmp[:, :], AX.X, ALU.add))
            ch.link(v.tensor_scalar(ceps[:, :], cneg2[:, :], 1.0 / F, EPS, ALU.mult, ALU.add))
            ch.link(v.tensor_scalar(cneg2[:, :], cneg2[:, :], -1.0, None, ALU.mult))
            rows_ = ident[0:TERMS, 0:TERMS]
            ch.add(v.tensor_reduce(blk[:, :], rows_.rearrange("k (g b) -> k b g", b=OCT), AX.X, ALU.add))
            ch.add(v.tensor_reduce(kind12[:, :], rows_.rearrange("k (g b) -> k g b", b=OCT), AX.X, ALU.add))
            ch.add(v.tensor_copy(ident_bf[:, :], ident[:, :]))
            ch.add(v.memset(ctmp2[0:3, :], 0.0))
            ch.settle()
            ch.link(v.tensor_reduce(kind[:, :], kind12[:, :].rearrange("k (p c) -> k c p", c=4), AX.X, ALU.add))
            ch.link(v.tensor_scalar(cterm[:, :], ones[0:TERMS, :], kind[:, 3:4], None, ALU.mult))
            for k in range(3):
                part, left = rhs_sel[:, k, :], crow if k == 0 else ctmp
                ch.link(v.tensor_copy(part, left[0:TERMS, :]))
                ch.add(v.scalar_tensor_tensor(ctmp2[0:3, :], part[0:3, :], ident[0:3, k:k + 1], ctmp2[0:3, :],
                                              ALU.mult, ALU.add))
                ch.add(v.scalar_tensor_tensor(cterm[:, :], part, kind[:, k:k + 1], cterm[:, :], ALU.mult, ALU.add))
                ch.link(v.tensor_tensor(ctmp[0:TERMS, :], left[0:TERMS, :], part, ALU.subtract))
            ch.link(v.memset(b3sum[:, :], 0.0))
            for k in range(3):
                ch.link(v.tensor_copy(b3part[:, :], b3all[:, :]))
                ch.add(v.scalar_tensor_tensor(b3sum[:, :], b3part[:, :], ident[0:3, k:k + 1], b3sum[:, :],
                                              ALU.mult, ALU.add))
                ch.link(v.tensor_tensor(b3all[:, :], b3all[:, :], b3part[:, :], ALU.subtract))
            ch.add(v.tensor_copy(b3parts[:, :, :], b3sum[:, :].unsqueeze(1).to_broadcast([3, QUAD, F])))
            ch.link(v.tensor_copy(c3[:, :, :], ctmp2[0:3, :].unsqueeze(1).to_broadcast([3, QUAD, F])))
            ch.link(v.tensor_tensor(rhs_sel[:, :, :], blk[:, :].unsqueeze(2).to_broadcast([TERMS, OCT, F]),
                                    cterm[:, :].unsqueeze(1).to_broadcast([TERMS, OCT, F]), ALU.mult))
            v.sem_inc(const_ready, 1)

            var, var2 = Chain(dve, c_var, VAR_OPS), Chain(dve, c_var2, VAR2_OPS)
            split = Chain(dve, c_split, SPLIT_OPS)
            cf, cs = Chain(dve, c_found, QUAD), Chain(dve, c_score, QUAD)

            def stats_part(i, s, h, between):
                dve.wait_ge(x_in[s], 16 * (h + 1))
                for j in range(OCT):
                    ins = v.bn_stats(st[s][:, j, :], xo[s][:, j, :])
                ins.then_inc(bn_done, 1)
                between(0)
                dve.wait_ge(bn_done, i + 1)
                var.begin(i)
                var.add(v.tensor_tensor(sm[s], st[s][:, :, 1], st[s][:, :, 4], ALU.add))
                var.add(v.tensor_tensor(df[s], st[s][:, :, 1], st[s][:, :, 4], ALU.subtract))
                var.add(v.tensor_tensor(v2[s], st[s][:, :, 2], st[s][:, :, 5], ALU.add))
                between(1)
                var.settle()
                var.add(v.tensor_tensor(dd[s], df[s], df[s], ALU.mult))
                var.add(v.tensor_tensor(q1[s], sm[s], sm[s], ALU.mult))
                var.add(v.tensor_scalar(stats[s][:, 3, :], sm[s], -0.5, None, ALU.mult))
                between(2)
                var.settle()
                var.add(v.scalar_tensor_tensor(V[s], dd[s], float(F) / 4, v2[s], ALU.mult, ALU.add))
                between(3)
                var.settle()
                var.add(v.scalar_tensor_tensor(q2[s], q1[s], float(F) / 4, V[s], ALU.mult, ALU.add))
                var.end()

            def second_variance(i, s, between):
                dve.wait_ge(c_r, 3 * i + 3)
                dve.wait_ge(c_var, VAR_OPS * (i + 1))
                dve.wait_ge(c_qsum, OCT * i + OCT)
                var2.begin(i)
                var2.add(v.tensor_tensor(t1[s], V[s], rstd[s], ALU.mult))
                var2.add(v.tensor_tensor(t2[s], qsum[s], q2[s], ALU.subtract))
                between(0)
                var2.settle()
                var2.add(v.scalar_tensor_tensor(t3[s], t2[s], cneg2[:, :], t1[s], ALU.add, ALU.add))
                between(1)
                var2.settle()
                var2.add(v.tensor_tensor(t4[s], t3[s], rstd[s], ALU.mult))

            def second_scale(i, s):
                dve.wait_ge(c_r2, 2 * i + 2)
                var2.add(v.tensor_tensor(scale[s], rstd[s], rstd2[s], ALU.mult))
                var2.end()

            def split_stats(i, s, between):
                dve.wait_ge(c_r, 3 * i + 3)
                dve.wait_ge(c_var, VAR_OPS * (i + 1))
                wait_past(dve, stat_T, i - 1)
                split.begin(i)
                split.add(v.tensor_scalar(stats[s][:, 0:3, :], sdev[s].unsqueeze(1).to_broadcast([P, 3, OCT]), -1.0,
                                          None, ALU.add))
                n = 4 * OCT
                a0, a1, a2 = (parts[s][:, k * n:(k + 1) * n] for k in range(3))
                whole = stats[s].rearrange("p a b -> p (a b)")
                between(0)
                split.settle()
                split.add(v.tensor_copy(a0, whole))
                between(1)
                split.settle()
                split.add(v.tensor_tensor(rest1[s], whole, a0, ALU.subtract))
                between(2)
                split.settle()
                split.add(v.tensor_copy(a1, rest1[s]))
                between(3)
                split.settle()
                split.add(v.tensor_tensor(rest2[s], rest1[s], a1, ALU.subtract))
                between(4)
                split.settle()
                split.add(v.tensor_copy(a2, rest2[s]))
                split.end()

            def copy_stats(i, s):
                dve.wait_ge(stat_T, i + 1)
                wait_past(dve, d_final, i - 1)
                v.tensor_copy(statsT[s], psT[0:TERMS, 0:P]).then_inc(stat_copied, 1)

            def compare_sources(q, s, h, g):
                if g == 0:
                    dve.wait_ge(srcrow_in[s], 16 * (h + 1))
                    wait_past(dve, found, 2 * (q - 1))
                ins = v.tensor_scalar(ge[s][:, g, :], srcrow[s], dfirst[:, g:g + 1], None, ALU.is_ge)
                if g == 1:
                    ins.then_inc(ge_ready, 1)

            def use_found(q, j):
                if j == 0:
                    dve.wait_ge(found, 2 * q + 2)
                    cf.begin(q)
                wait_past(dve, c_found, cf.base + cf.n - 1)
                codes = psF[j // 2][:, (j % 2) * (P + 1):(j % 2) * (P + 1) + P]
                cf.add(v.scalar_tensor_tensor(junk[:, j % 2, :], codes, src_code[:, bass.ds(QUAD * q + j, 1)],
                                              iota[:, :], ALU.is_equal, ALU.mult,
                                              accum_out=hit[:, bass.ds(QUAD * q + j, 1)]))
                if j % 2:
                    v.tensor_copy(tile1[:, bass.ds(QUAD * q + j - 1, 2)], psF[j // 2][:, P:2 * P + 2:P + 1]
                                  ).then_inc(find_used, 1)

            def scores(q, s, h, j):
                if j == 0:
                    dve.wait_ge(g_in[s], 64 * (h + 1))
                    cs.begin(q)
                wait_past(dve, c_score, cs.base + cs.n - 1)
                cs.add(v.scalar_tensor_tensor(junk[:, 2 + j % 2, :], G[:, bass.ds(QUAD * q + j, 1), :], 1.0, w0[:, :],
                                              ALU.mult, ALU.mult, accum_out=score[:, bass.ds(QUAD * q + j, 1)]))

            def nothing(k):
                pass

            def step_a1(i, s, h):
                k, ks, kh = back(i, s, h, 1)
                if live(k, NO):
                    second_variance(k, ks, lambda n: compare_sources(i, s, h, n))
                else:
                    compare_sources(i, s, h, 0)
                    compare_sources(i, s, h, 1)
                split_stats(i, s, lambda n: use_found(k, n) if n < QUAD and live(k, NO) else None)
                if live(k, NO):
                    second_scale(k, ks)
                stats_part(i + 1, 1 - s, h + s, lambda n: scores(i, s, h, n))
                copy_stats(i, s)

            stats_part(0, 0, 0, nothing)
            sweep(dve, *A1, step_a1)
            for j in range(QUAD):
                use_found(NQ - 1, j)

            dve.wait_ge(c_found, QUAD * NQ)
            dve.wait_ge(c_score, QUAD * NQ)
            dve.wait_ge(find_used, 2 * NQ)
            ch.add(v.scalar_tensor_tensor(tmp_t[:, :], tile1[:, :], float(P), hit[:, :], ALU.mult, ALU.add))
            ch.add(v.tensor_scalar(src_code[:, :], hit[:, :], 0.0, float(SKIP), ALU.is_equal, ALU.mult))
            ch.settle()
            ch.link(v.scalar_tensor_tensor(row_idx[:, :], tmp_t[:, :], -float(P + 1), src_code[:, :], ALU.add, ALU.add))
            v.sem_inc(rows_found, 1)

            soft = Chain(dve, soft_dve, 0)
            soft.begin(0)
            v.sem_inc(soft_dve, 1)
            soft.n = 1
            dve.wait_ge(soft_pe, 2)
            soft.link(v.tensor_copy(score_c[:, :], E0[0:H, 0:256]))
            soft.link(v.tensor_tensor_scan(max_c[:, 1:257], pen_c[:, :], score_c[:, :], -BIG, ALU.add, ALU.max))
            assert soft.n == 3
            dve.wait_ge(soft_pe, 4)
            soft.add(v.tensor_copy(rowbuf[:, :], E1[0:1, 0:2 * P]))
            soft.link(v.memset(carry_row[:, 0:1], -BIG))
            soft.link(v.tensor_tensor_scan(carry_row[0:1, 1:H + 1], rowbuf[0:1, P:P + H], rowbuf[0:1, 0:H], -BIG,
                                           ALU.add, ALU.max))
            assert soft.n == 6
            dve.wait_ge(soft_pe, 5)
            soft.link(v.tensor_copy(max_c[:, 0:1], E2[0:H, 0:1]))
            soft.link(v.tensor_tensor_scan(max_c[:, 1:257], pen_c[:, :], score_c[:, :], max_c[:, 0:1], ALU.add,
                                           ALU.max))
            soft.add(v.tensor_tensor(da_c[:, :], max_c[:, 0:256], pen_c[:, :], ALU.add))
            soft.add(v.tensor_tensor(db_c[:, :], score_c[:, :], max_c[:, 1:257], ALU.subtract))
            soft.settle()
            soft.link(v.tensor_tensor(da_c[:, :], da_c[:, :], max_c[:, 1:257], ALU.subtract))
            assert soft.n == 11
            dve.wait_ge(soft_act, 2)
            soft.add(v.tensor_tensor_scan(den_c[:, :], decay_c[:, :], bw_c[:, :], 0.0, ALU.mult, ALU.add))
            soft.link(v.tensor_tensor_scan(da_c[:, :], decay_c[:, :], zero_c[:, :], 1.0, ALU.mult, ALU.add))
            assert soft.n == 13
            dve.wait_ge(soft_pe, 7)
            soft.add(v.tensor_copy(rowbuf[:, :], E1[0:1, 0:2 * P]))
            soft.link(v.memset(carry_row[:, 0:1], 0.0))
            soft.link(v.tensor_tensor_scan(carry_row[0:1, 1:H + 1], rowbuf[0:1, P:P + H], rowbuf[0:1, 0:H], 0.0,
                                           ALU.mult, ALU.add))
            assert soft.n == 16
            dve.wait_ge(soft_pe, 8)
            soft.link(v.tensor_copy(carry_c[:, :], E2[0:H, 0:1]))
            soft.link(v.tensor_tensor_scan(den_c[:, :], decay_c[:, :], bw_c[:, :], carry_c[:, :], ALU.mult, ALU.add))
            soft.link(v.tensor_scalar(den_c[:, :], den_c[:, :], 1e-20, None, ALU.max))
            soft.link(v.reciprocal(den_c[:, :], den_c[:, :]))
            assert soft.n == 20
            dve.wait_ge(soft_pe, 12)
            for g in range(2):
                soft.add(v.tensor_copy(bw[:, g:NT:2], E0[:, g * H:(g + 1) * H]))
                soft.add(v.tensor_copy(rden[:, g:NT:2], E1[:, g * H:(g + 1) * H]))
            soft.settle()

            def weigh(q, s):
                wait_past(dve, bx_T, q - 1)
                v.tensor_tensor(bx[s], G[:, bass.ds(QUAD * q, QUAD), :],
                                bw[:, bass.ds(QUAD * q, QUAD)].unsqueeze(2).to_broadcast([P, QUAD, F]),
                                ALU.mult).then_inc(bx_ready, 1)

            def running_sum(q, s, h):
                dve.wait_ge(arow_in[s], 16 * (h + 1))
                dve.wait_ge(bx_T, q + 1)
                wait_past(dve, r_T, q - 1)
                if isinstance(q, int) and q == 0:
                    start = 0.0
                else:
                    dve.wait_ge(scan_done, q)
                    start = RT[1 - s][:, QE - 1:QE]
                v.tensor_tensor_scan(RT[s], arow[s], psX[s][:, :], start, ALU.mult, ALU.add).then_inc(scan_done, 1)

            def node_sums(q, s, h, j):
                if j == 0:
                    dve.wait_ge(r_T, q + 1)
                    dve.wait_ge(xd_in[s], 64 * (h + 1))
                    wait_past(dve, u_stored[s], 16 * h)
                ins = v.scalar_tensor_tensor(U[s][:, j, :], psR[:, j * P:(j + 1) * P],
                                             rden[:, bass.ds(QUAD * q + j, 1)], xd[s][:, j, :],
                                             ALU.mult, ALU.add)
                if j == QUAD - 1:
                    ins.then_inc(u_ready, 1)

            def step_a2(i, s, h):
                k, ks, kh = back(i, s, h, 1)
                qw, sw, hw = back(i, s, h, NQ)
                qr, sr, hr = back(i, s, h, NQ + 1)
                qn, sn, hn_ = back(i, s, h, NQ + 2)

                def sums(n):
                    if n == 0 and live(qw, NQ):
                        weigh(qw, sw)
                    if n == 1 and live(qn, NQ):
                        for j in range(2):
                            node_sums(qn, sn, hn_, j)

                def more(n):
                    if n < 2 and live(qn, NQ):
                        node_sums(qn, sn, hn_, n + 2)
                    if n == 2 and live(qr, NQ):
                        running_sum(qr, sr, hr)

                if live(k, NO):
                    second_variance(k, ks, sums)
                else:
                    sums(0)
                    sums(1)
                if live(i, NO):
                    split_stats(i, s, more)
                else:
                    for n in range(3):
                        more(n)
                if live(k, NO):
                    second_scale(k, ks)
                if live(i + 1, NO):
                    stats_part(i + 1, 1 - s, h + s, nothing)
                if live(i, NO):
                    copy_stats(i, s)

            sweep(dve, *A2, step_a2)
            dve.wait_ge(u_ready, NQ)
            v.sem_inc(a_done, 1)
            dve.wait_ge(a_done, 3)
            dve.wait_ge(a_stored, 1)

            bvar, bmul, prod_c, yc = (Chain(dve, c_bvar, BVAR_OPS), Chain(dve, c_bmul, 3),
                                      Chain(dve, c_prod, PROD_OPS), Chain(dve, c_y, Y_OPS))

            def variance(c, stat, sm_, df_, v2_, dd_, V_, between):
                c.add(v.tensor_tensor(sm_, stat[:, :, 1], stat[:, :, 4], ALU.add))
                c.add(v.tensor_tensor(df_, stat[:, :, 1], stat[:, :, 4], ALU.subtract))
                c.add(v.tensor_tensor(v2_, stat[:, :, 2], stat[:, :, 5], ALU.add))
                between(1)
                c.settle()
                c.add(v.tensor_tensor(dd_, df_, df_, ALU.mult))
                between(2)
                c.settle()
                c.add(v.scalar_tensor_tensor(V_, dd_, float(F) / 4, v2_, ALU.mult, ALU.add))

            def finish_rows(q, s, between):
                dve.wait_ge(c_l3, 3 * q + 3)
                yc.begin(q)
                yc.add(v.scalar_tensor_tensor(t_, Z3[s][:, :], 0.0, l3, ALU.max, ALU.add))
                between(-1)
                yc.settle()
                wait_past(dve, row_ready, q)
                for j in range(QUAD):
                    yc.add(v.scalar_tensor_tensor(y[:, j, :], node_tiles(q)[:, j, :],
                                                  rnode[:, bass.ds(QUAD * q + j, 1)], t_[:, j * P:(j + 1) * P],
                                                  ALU.mult, ALU.add))
                between(0)
                yc.settle()
                for j in range(QUAD):
                    yc.add(v.bn_stats(yst[s][:, j, :], y[:, j, :]))
                between(3)
                yc.settle()
                variance(yc, yst[s], ysm[s], ydf[s], yv2[s], ydd[s], yV[s], between)
                yc.end()

            def norm_factors(q, s, n):
                if n == 0:
                    dve.wait_ge(c_norm_r, 2 * q + 2)
                    wait_past(dve, hn_ready, q - 1)
                    bmul.begin(q)
                    bmul.add(v.tensor_tensor(brc[s], brs[s][:, 0:QUAD], cut[:, bass.ds(QUAD * q, QUAD)], ALU.mult))
                    bmul.add(v.tensor_copy(rnode[:, bass.ds(QUAD * q, QUAD)], brs[s][:, QUAD:2 * QUAD]))
                    return
                bmul.settle()
                bmul.add(v.scalar_tensor_tensor(bnm[s], bsm[s][:, 0:QUAD], -0.5, brc[s], ALU.mult, ALU.mult))
                bmul.end()

            def running_product(q, s, h, n):
                if n == 0:
                    dve.wait_ge(m_T, q + 1)
                    dve.wait_ge(bf_ready, q + 1)
                    prod_c.begin(q)
                    prod_c.add(v.scalar_tensor_tensor(m, bf[s], kb2[:, :], MT[s][:, :], ALU.add, ALU.mult))
                    return
                prod_c.settle()
                if n == 1:
                    dve.wait_ge(cont_in[s], 16 * (h + 1))
                    prod_c.add(v.tensor_tensor(d0, m, cont[s], ALU.mult))
                if n == 2:
                    prod_c.add(v.tensor_tensor(d1, m, d0, ALU.subtract))
                if n == 3:
                    wait_past(dve, z3_done, q - 1)
                    start = 1.0 if isinstance(q, int) and q == 0 else prod[1 - s][:, QE - 1:QE]
                    prod_c.add(v.tensor_tensor_scan(prod[s], d0, d1, start, ALU.mult, ALU.add))
                    prod_c.end()

            def row_stats(q, s, h, between):
                dve.wait_ge(row_in[s], 64 * (h + 1))
                dve.wait_ge(ur_in[s], 16 * (h + 1))
                wait_past(dve, c_bmul, 3 * (q - 1))
                wait_past(dve, c_norm_r, 2 * (q - 1))
                bvar.begin(q)
                for j in range(QUAD):
                    bvar.add(v.bn_stats(bst[s][:, j, :], G[:, bass.ds(QUAD * q + j, 1), :]))
                    bvar.add(v.bn_stats(bst[s][:, QUAD + j, :], node_tiles(q)[:, j, :]))
                between(0)
                bvar.settle()
                variance(bvar, bst[s], bsm[s], bdf[s], bv2[s], bdd[s], bV[s], between)
                bvar.end()

            def hidden(q, s):
                dve.wait_ge(c_l1, 3 * q + 3)
                wait_past(dve, z2_done, q)
                v.scalar_tensor_tensor(h1, Z1[s][:, :], nb1[:, :], l1, ALU.max, ALU.add).then_inc(h1_ready, 1)

            def filters(q, s):
                dve.wait_ge(c_l2, 3 * q + 3)
                wait_past(dve, c_prod, PROD_OPS * (q - 2) + 1)
                v.scalar_tensor_tensor(bf[s], Z2[s][:, :], nb2[:, :], l2, ALU.max, ALU.add).then_inc(bf_ready, 1)

            def attributed(q, s, h):
                dve.wait_ge(hn_ready, q + 1)
                if isinstance(q, int) and q == NQ - 1:
                    dve.wait_ge(attr_in[s], 16 * (h + ATTR_LOADS))
                else:
                    dve.wait_ge(attr_in[s], 16 * (h + 1))
                wait_past(dve, m_T, q - 1)
                v.tensor_tensor(hm[s], hn[s], attr_s[s], ALU.mult).then_inc(hm_ready, 1)

            def step_b(i, s, h):
                q1_, s1_, h1_ = back(i, s, h, 1)
                q2_, s2_, h2_ = back(i, s, h, 2)
                q, qs, qh = back(i, s, h, 3)

                def product(n):
                    if live(q2_, NQ):
                        running_product(q2_, s2_, h2_, n)

                def beside_stats(n):
                    if n < 2:
                        product(n)
                    elif live(q1_, NQ):
                        hidden(q1_, s1_)

                def beside_rows(n):
                    if n == -1:
                        product(3)
                    if n == 0 and live(q1_, NQ):
                        attributed(q1_, s1_, h1_)
                    if n in (3, 1) and live(i, NQ):
                        norm_factors(i, s, 0 if n == 3 else 1)

                if live(i, NQ):
                    row_stats(i, s, h, beside_stats)
                else:
                    for n in range(3):
                        beside_stats(n)
                product(2)
                if live(q, NQ):
                    finish_rows(q, qs, beside_rows)
                else:
                    for n in (-1, 0, 3, 1):
                        beside_rows(n)
                if live(q1_, NQ):
                    filters(q1_, s1_)
                if live(q, NQ):
                    dve.wait_ge(c_yr, 2 * q + 2)
                    v.scalar_tensor_tensor(ynm[qs], ysm[qs], -0.5, yrs[qs], ALU.mult, ALU.mult
                                           ).then_inc(ynm_ready, 1)
            sweep(dve, *B, step_b)

        @block.scalar
        def _(act):
            a = nc.scalar.activation
            one = ones[:, 0:1]
            act.wait_ge(cut_t, 1)
            a(cut[:, :], tmp_t[:, :], ACT.Sin, bias=halfpi[:, :], scale=-PI).then_inc(cut_sin, 1)
            nc.scalar.preload_act_table_set("natural_log_exp_and_others")
            act.wait_ge(setup_pe, 1)
            setup = Chain(act, setup_act, 3)
            setup.begin(0)
            setup.link(a(ctmp[:, :], E0[:, 0:F], ACT.Abs))
            setup.link(a(ctmp2[:, :], ctmp[:, :], ACT.Exp, scale=-1.0))
            setup.link(a(ctmp[:, :], ctmp2[:, :], ACT.Ln, bias=one))
            setup.end()
            act.wait_ge(const_ready, 2)

            r_c, r2_c, qs_c = Chain(act, c_r, 3), Chain(act, c_r2, 2), Chain(act, c_qsum, OCT)

            def second_rstd(i, s):
                act.wait_ge(c_var2, VAR2_OPS * i + VAR2_AT)
                r2_c.begin(i)
                r2_c.link(a(lnv2[s], t4[s], ACT.Ln, bias=ceps[:, :], scale=1.0 / F))
                r2_c.link(a(rstd2[s], lnv2[s], ACT.Exp, scale=-0.5))
                r2_c.end()

            def square_sums(i, s):
                qs_c.begin(i)
                for j in range(OCT):
                    if j % QUAD == 0:
                        act.wait_ge(d_filled[j // QUAD], i + 1)
                    wait_past(act, c_qsum, qs_c.base + qs_c.n - 1)
                    qs_c.add(a(ajunk[:, j % 2, :], D[s][j // QUAD][:, (j % QUAD) * P:(j % QUAD + 1) * P], ACT.Square,
                               accum_out=qsum[s][:, j:j + 1]))
                qs_c.end()

            def first_rstd(i, s):
                act.wait_ge(c_var, VAR_OPS * i + V_AT)
                r_c.begin(i)
                r_c.link(a(lnv[s], V[s], ACT.Ln, bias=epst[:, :], scale=1.0 / F))
                r_c.add(a(rstd[s], lnv[s], ACT.Exp, scale=-0.5))
                r_c.add(a(sdev[s], lnv[s], ACT.Exp, scale=0.5))
                r_c.end()

            def dense_out(i, s, h, b):
                act.wait_ge(d_final, i + 1)
                act.wait_ge(c_var2, VAR2_OPS * i + SCALE_AT)
                wait_past(act, o_stored[s], 16 * h)
                for j in range(QUAD * b, QUAD * b + QUAD):
                    ins = a(oo[s][:, j, :], D[s][b][:, (j % QUAD) * P:(j % QUAD + 1) * P], ACT.Copy,
                            scale=scale[s][:, j:j + 1])
                ins.then_inc(o_ready[b], 1)

            def dense_step(i, s, h):
                k, ks, kh = back(i, s, h, 2)
                if live(k, NO):
                    dense_out(k, ks, kh, 0)
                if live(i, NO):
                    first_rstd(i, s)
                if live(k, NO):
                    dense_out(k, ks, kh, 1)
                k, ks, kh = back(i, s, h, 1)
                if live(k, NO):
                    second_rstd(k, ks)
                if live(i, NO):
                    square_sums(i, s)

            sweep(act, *A1, dense_step)
            act.wait_ge(soft_dve, 11)
            a(decay_c[:, :], da_c[:, :], ACT.Exp).then_inc(soft_act, 1)
            a(bw_c[:, :], db_c[:, :], ACT.Exp).then_inc(soft_act, 1)
            act.wait_ge(soft_act, 2)
            act.sem_inc(decay_ready, 1)
            sweep(act, *A2, dense_step)
            act.wait_ge(o_ready[1], NO)
            act.sem_inc(a_done, 1)
            act.wait_ge(a_done, 3)
            act.wait_ge(a_stored, 1)

            basis_c, l1_c, l2_c, l3_c = (Chain(act, sem_, n) for sem_, n in ((c_basis, 2), (c_l1, 3), (c_l2, 3),
                                                                              (c_l3, 3)))
            norm_c, yr_c = Chain(act, c_norm_r, 2), Chain(act, c_yr, 2)

            def log_term(chain, q, l, z, bias, n):
                if n == 0:
                    chain.begin(q)
                    chain.add(a(l, z, ACT.Abs, bias=bias))
                    return
                chain.settle()
                if n == 1:
                    chain.add(a(l, l, ACT.Exp, scale=-1.0))
                if n == 2:
                    chain.add(a(l, l, ACT.Ln, bias=one))
                    chain.end()

            def inverse_deviation(chain, q, ln_, r, V_):
                chain.begin(q)
                chain.link(a(ln_, V_, ACT.Ln, bias=epst[:, :], scale=1.0 / F))
                chain.link(a(r, ln_, ACT.Exp, scale=-0.5))
                chain.end()

            def step_b(i, s, h):
                q, qs, qh = back(i, s, h, 3)
                q1_, s1_, h1_ = back(i, s, h, 1)
                if live(q, NQ):
                    act.wait_ge(z3_done, q + 1)
                    wait_past(act, c_y, Y_OPS * (q - 1) + 1)
                if live(q1_, NQ):
                    act.wait_ge(z1_done, q1_ + 1)
                    wait_past(act, h1_ready, q1_)
                for n in range(3):
                    if live(q1_, NQ):
                        log_term(l1_c, q1_, l1, Z1[s1_][:, :], b1c[:, :], n)
                    if live(q, NQ):
                        log_term(l3_c, q, l3, Z3[qs][:, :], 0.0, n)
                if live(q1_, NQ):
                    act.wait_ge(c_bmul, 3 * q1_ + 3)
                    wait_past(act, hm_ready, q1_ - 1)
                    for j in range(QUAD):
                        ins = a(hn[s1_][:, j, :], G[:, bass.ds(QUAD * q1_ + j, 1), :], ACT.Identity,
                                bias=bnm[s1_][:, j:j + 1], scale=brc[s1_][:, j:j + 1])
                    ins.then_inc(hn_ready, 1)
                if live(i, NQ):
                    act.wait_ge(c_bvar, BVAR_OPS * i + BV_AT)
                    inverse_deviation(norm_c, i, bln[s], brs[s], bV[s])
                    act.wait_ge(wrow_in[s], 16 * (h + 1))
                    wait_past(act, z1_done, i)
                    basis_c.begin(i)
                    basis_c.add(a(e0, wrow[s], ACT.Square, bias=muneg[:, :]))
                if live(q1_, NQ):
                    act.wait_ge(z2_done, q1_ + 1)
                    wait_past(act, bf_ready, q1_)
                    log_term(l2_c, q1_, l2, Z2[s1_][:, :], b2c[:, :], 0)
                if live(i, NQ):
                    basis_c.settle()
                    basis_c.add(a(e0, e0, ACT.Exp, scale=-float(F)))
                    basis_c.end()
                if live(q1_, NQ):
                    log_term(l2_c, q1_, l2, Z2[s1_][:, :], b2c[:, :], 1)
                    log_term(l2_c, q1_, l2, Z2[s1_][:, :], b2c[:, :], 2)
                if live(q, NQ):
                    act.wait_ge(c_y, Y_OPS * q + YV_AT)
                    inverse_deviation(yr_c, q, yln[qs], yrs[qs], yV[qs])
                if live(q, NQ):
                    act.wait_ge(ynm_ready, q + 1)
                    wait_past(act, scattered[qs], 64 * qh)
                    for j in range(QUAD):
                        ins = a(o[qs][:, j, :], y[:, j, :], ACT.Identity, bias=ynm[qs][:, j:j + 1],
                                scale=yrs[qs][:, j:j + 1])
                    ins.then_inc(row_ready, 1)

            sweep(act, *B, step_b)

        @block.tensor
        def _(pe):
            mm = nc.tensor.matmul
            pe.wait_ge(par_in, 16 * 11)
            pe.wait_ge(setup_dve, 5)
            mm(E0[:, 0:F], ones[:, :], w3[:, :], start=True, stop=False)
            mm(E0[:, 0:F], ones[0:1, :], b3row[:, :], start=False, stop=True).then_inc(setup_pe, 1)
            pe.wait_ge(const_ready, 1)
            mm(E1[:, 0:1], w2[:, :], b1m[:, :], start=True, stop=True).then_inc(setup_pe, 1)
            pe.wait_ge(const_ready, 2)

            def fill(i, s, h):
                pe.wait_ge(x_in[s], 16 * (h + 1))
                for b in range(2):
                    wait_past(pe, o_ready[b], i - 1)
                    mm(D[s][b][:, :], ident[:, :], xo[s][:, QUAD * b:QUAD * (b + 1), :], start=True, stop=False)
                    mm(D[s][b][:, :], ones3[:, :], c3[:, :, :], start=False, stop=True).then_inc(d_filled[b], 1)

            def transpose_stats(i, s):
                pe.wait_ge(c_split, SPLIT_OPS * (i + 1))
                wait_past(pe, stat_copied, i)
                mm(psT[0:TERMS, 0:P], parts[s], ident_bf[:, :], start=True, stop=True).then_inc(stat_T, 1)

            def add_terms(i, s):
                pe.wait_ge(stat_copied, i + 1)
                pe.wait_ge(c_qsum, OCT * i + OCT)
                for b in range(2):
                    ins = mm(D[s][b][:, :], statsT[s], rhs_sel[:, QUAD * b:QUAD * (b + 1), :], start=False, stop=True,
                             skip_group_check=True)
                ins.then_inc(d_final, 1)

            def find(q, s, b):
                pe.wait_ge(ge_ready, q + 1)
                wait_past(pe, find_used, 2 * q)
                for j in (2 * b, 2 * b + 1):
                    for g, part in ((0, dhigh), (0, drest), (1, dhigh), (1, drest)):
                        ins = mm(psF[b][:, (j % 2) * (P + 1):(j % 2 + 1) * (P + 1)],
                                 ge[s][:, g, j * P:(j + 1) * P], part[:, g, 0:P + 1],
                                 start=(g == 0 and part is dhigh), stop=(g == 1 and part is drest))
                ins.then_inc(found, 1)

            pe.wait_ge(find_setup, 1)

            def step_a1(i, s, h):
                fill(i, s, h)
                k, ks, kh = back(i, s, h, 1)
                if live(k, NO):
                    add_terms(k, ks)
                find(i, s, 0)
                find(i, s, 1)
                transpose_stats(i, s)

            sweep(pe, *A1, step_a1)

            eh, e1_ = ident[0:H, 0:H], ones[0:1, 0:1]
            pe.wait_ge(soft_dve, 1)
            nc.tensor.transpose(E0[0:H, 0:P], score[:, 0:NT:2], ident[:, :]).then_inc(soft_pe, 1)
            nc.tensor.transpose(E0[0:H, P:2 * P], score[:, 1:NT:2], ident[:, :]).then_inc(soft_pe, 1)
            pe.wait_ge(soft_dve, 3)
            mm(E1[0:1, 0:H], max_c[:, 256:257], eh, start=True, stop=True).then_inc(soft_pe, 1)
            mm(E1[0:1, P:P + H], pass_c[:, 1:2], eh, start=True, stop=True).then_inc(soft_pe, 1)
            pe.wait_ge(soft_dve, 6)
            mm(E2[0:H, 0:1], carry_row[0:1, 0:H], e1_, start=True, stop=True).then_inc(soft_pe, 1)
            pe.wait_ge(soft_dve, 13)
            mm(E1[0:1, 0:H], den_c[:, 255:256], eh, start=True, stop=True).then_inc(soft_pe, 1)
            mm(E1[0:1, P:P + H], da_c[:, 255:256], eh, start=True, stop=True).then_inc(soft_pe, 1)
            pe.wait_ge(soft_dve, 16)
            mm(E2[0:H, 0:1], carry_row[0:1, 0:H], e1_, start=True, stop=True).then_inc(soft_pe, 1)
            pe.wait_ge(soft_dve, 20)
            for bank, src in ((E0, bw_c), (E1, den_c)):
                for g in range(2):
                    nc.tensor.transpose(bank[:, g * H:(g + 1) * H], src[:, g * P:(g + 1) * P], eh
                                        ).then_inc(soft_pe, 1)

            def step_a2(i, s, h):
                k, ks, kh = back(i, s, h, 1)
                if live(i, NO):
                    fill(i, s, h)
                if live(k, NO):
                    add_terms(k, ks)
                q, qs, qh = back(i, s, h, NQ)
                if live(q, NQ):
                    pe.wait_ge(bx_ready, q + 1)
                    wait_past(pe, scan_done, q - 1)
                    for j in range(QUAD):
                        ins = nc.tensor.transpose(psX[qs][:, j * P:(j + 1) * P], bx[qs][:, j, :], ident[:, :])
                    ins.then_inc(bx_T, 1)
                q, qs, qh = back(i, s, h, NQ + 1)
                if live(q, NQ):
                    pe.wait_ge(scan_done, q + 1)
                    wait_past(pe, u_ready, q)
                    for j in range(QUAD):
                        ins = nc.tensor.transpose(psR[:, j * P:(j + 1) * P], RT[qs][:, j * P:(j + 1) * P],
                                                  ident[:, :])
                    ins.then_inc(r_T, 1)
                if live(i, NO):
                    transpose_stats(i, s)

            sweep(pe, *A2, step_a2)
            pe.wait_ge(r_T, NQ)
            pe.sem_inc(a_done, 1)
            pe.wait_ge(a_done, 3)
            pe.wait_ge(a_stored, 1)

            def step_b(i, s, h):
                q, qs, qh = back(i, s, h, 1)
                if live(q, NQ):
                    pe.wait_ge(h1_ready, q + 1)
                    wait_past(pe, bf_ready, q - 1)
                    mm(Z2[qs][:, :], w2[:, :], h1, start=True, stop=True).then_inc(z2_done, 1)
                q, qs, qh = back(i, s, h, 2)
                if live(q, NQ):
                    pe.wait_ge(c_prod, PROD_OPS * q + PROD_AT)
                    wait_past(pe, c_y, Y_OPS * (q - 2) + 1)
                    mm(Z3[qs][:, :], ones3[:, :], b3parts[:, :, :], start=True, stop=False)
                    for j in range(QUAD):
                        ins = mm(Z3[qs][:, j * P:(j + 1) * P], prod[qs][:, j * P:(j + 1) * P], w3[:, :],
                                 start=False, stop=(j == QUAD - 1))
                    ins.then_inc(z3_done, 1)
                if live(i, NQ):
                    pe.wait_ge(c_basis, 2 * i + 2)
                    wait_past(pe, h1_ready, i - 1)
                    mm(Z1[s][:, :], w1[:, :], e0, start=True, stop=True).then_inc(z1_done, 1)
                q, qs, qh = back(i, s, h, 1)
                if live(q, NQ):
                    pe.wait_ge(hm_ready, q + 1)
                    wait_past(pe, c_prod, PROD_OPS * (q - 2) + 1)
                    for j in range(QUAD):
                        ins = nc.tensor.transpose(MT[qs][:, j * P:(j + 1) * P], hm[qs][:, j, :], ident[:, :])
                    ins.then_inc(m_T, 1)

            sweep(pe, *B, step_b)


def kernel(x, src, dst, edge_attr_128, edge_weight, L0_gnn_W, L1_gnn_W1, L1_gnn_b1, L1_gnn_W2, L1_gnn_b2, L1_gnn_W3,
           L1_gnn_b3):
    import numpy as np
    import concourse.bacc as bacc
    from concourse.bass_utils import run_bass_kernel_spmd

    x, src, dst, attr, weight = (np.ascontiguousarray(a) for a in (x, src, dst, edge_attr_128, edge_weight))
    N, E = x.shape[0], src.shape[0]
    NT = -(-E // QE) * QUAD
    pad = NT * P - E

    def tiles(a):
        return np.ascontiguousarray(a.reshape(NT, P).T)

    src_flat = np.pad(src, (0, pad))
    weight_flat = np.pad(weight, (0, pad), constant_values=2 * CUTOFF)
    dst_flat = np.pad(np.pad(dst, (0, pad), constant_values=N), (P, 1), constant_values=-1)
    arrays = {
        "x": x, "src_tiles": tiles(src_flat), "dst_tiles": tiles(dst_flat[P:-1]), "next_tiles": tiles(dst_flat[P + 1:]),
        "weight_tiles": tiles(weight_flat), "src_flat": src_flat, "dst_flat": dst_flat, "weight_flat": weight_flat,
        "attr": attr, "W0": L0_gnn_W, "W1": L1_gnn_W1, "b1": L1_gnn_b1, "W2": L1_gnn_W2, "b2": L1_gnn_b2,
        "W3": L1_gnn_W3, "b3": L1_gnn_b3, "eye": np.eye(P, dtype=np.float32),
        "iota1": np.ascontiguousarray(np.broadcast_to(np.arange(1, P + 1, dtype=np.float32), (P, P))),
        "mu": -np.linspace(0.0, 1.0, P, dtype=np.float32)[:, None],
    }
    arrays = {f"in_{k}": np.ascontiguousarray(a) for k, a in arrays.items()}
    nc = bacc.Bacc("TRN2", target_bir_lowering=False, num_devices=1)
    args = [nc.dram_tensor(k, a.shape, mybir.dt.from_np(a.dtype), kind="ExternalInput").ap() for k, a in arrays.items()]
    args.append(nc.dram_tensor("out_dram", x.shape, mybir.dt.float32, kind="ExternalOutput").ap())
    gnn_kernel(nc, *args)
    r = run_bass_kernel_spmd(nc, [arrays], core_ids=[0])
    return r.results[0]["out_dram"]
```

```python
import concourse.bass as bass
from concourse import mybir
from contextlib import ExitStack

P = 128
OCT = 8
QUAD = 4
QE = QUAD * P
EPS = 1e-5
BIG = 1e37
SKIP = 1 << 20
LN2 = 0.6931471805599453
ONSET, CUTOFF = 0.8, 1.0
CODE = 8.0
RND = 1.5 * 2.0 ** 34
PI = 3.141592653589793


def live(q, n):
    return not isinstance(q, int) or 0 <= q < n


def wait_past(eng, sem, value):
    if not isinstance(value, int) or value > 0:
        eng.wait_ge(sem, value)


def sweep(eng, start, lo, hi, stop, body):
    for i in range(start, min(lo, stop)):
        body(i, i % 2, i // 2)
    if hi > lo:
        with eng.Fori(lo // 2, hi // 2) as half:
            body(2 * half, 0, half)
            body(2 * half + 1, 1, half)
    for i in range(max(hi, lo), stop):
        body(i, i % 2, i // 2)


def straight(start, stop, body):
    for i in range(start, stop):
        body(i, i % 2, i // 2)


def back(i, slot, half, k):
    return i - k, (slot - k) % 2, half + (slot - k) // 2


class Chain:

    def __init__(self, eng, sem, size):
        self.eng, self.sem, self.size = eng, sem, size

    def begin(self, q):
        self.base, self.n = self.size * q, 0

    def add(self, ins):
        self.n += 1
        ins.then_inc(self.sem, 1)

    def settle(self):
        self.eng.wait_ge(self.sem, self.base + self.n)

    def link(self, ins):
        self.add(ins)
        self.settle()

    def end(self):
        assert self.n == self.size, (self.n, self.size)


def gnn_kernel(nc, x, src_tiles, dst_tiles, next_tiles, weight_tiles, src_flat, dst_flat, weight_flat, attr,
               W0, W1, b1, W2, b2, W3, b3, eye, iota1, mu, out):
    F32, BF16, F16, I32 = mybir.dt.float32, mybir.dt.bfloat16, mybir.dt.float16, mybir.dt.int32
    ALU, ACT, AX = mybir.AluOpType, mybir.ActivationFunctionType, mybir.AxisListType

    N, F = x.shape
    E = attr.shape[0]
    NT = src_tiles.shape[1]
    NQ = NT // QUAD
    H = NT // 2
    OROWS = OCT * P
    NO = -(-N // OROWS)
    assert (2 * N + 4096) / CODE < 65504
    TERMS = 3 * 4 * OCT
    assert NO == 2 * NQ and H <= P and F == P and N >= OROWS

    node_rows = nc.dram_tensor("node_rows", [NT * P, F], F32).ap()
    decay_flat = nc.dram_tensor("decay_flat", [NT * P], F32).ap()
    cont_flat = nc.dram_tensor("cont_flat", [NT * P], F32).ap()

    ctx = ExitStack()
    with ctx:
        def sb(name, shape, dt=F32):
            return ctx.enter_context(nc.sbuf_tensor(name, shape, dt))

        def sem(name):
            return ctx.enter_context(nc.semaphore(name))

        def sem2(name):
            return [sem(name + "_0"), sem(name + "_1")]

        G = sb("gathered", [P, NT, F])
        src_i = sb("src_i", [P, NT], I32)
        dst_i = sb("dst_i", [P, NT], I32)
        next_i = sb("next_i", [P, NT], I32)
        xd_idx = sb("xd_idx", [P, NT], I32)
        out_idx = sb("out_idx", [P, NT], I32)
        row_idx = sb("row_idx", [P, NT], I32)
        src_code = sb("src_code", [P, NT])
        wt = sb("wt", [P, NT])
        cut = sb("cut", [P, NT])
        score = sb("score", [P, NT])
        hit = sb("hit", [P, NT])
        tile1 = sb("tile1", [P, NT])
        tmp_t = sb("tmp_t", [P, NT])
        bw = sb("bw", [P, NT])
        rden = sb("rden", [P, NT])
        rnode = sb("rnode", [P, NT])
        ident = sb("ident", [P, P])
        iota = sb("iota", [P, P])
        ones = sb("ones", [P, P])
        w0 = sb("w0", [P, P])
        w1, w2, w3 = (sb(n, [P, P]) for n in ("w1s", "w2s", "w3s"))
        muneg = sb("muneg", [P, 1])
        b1c, b2c, nb1, nb2, kb2, b1m = (sb(n, [P, 1]) for n in ("b1c", "b2c", "nb1", "nb2", "kb2", "b1m"))
        b3row = sb("b3row", [1, F])
        b3all, b3sum = sb("b3all", [P, F]), sb("b3sum", [P, F])
        b3part = sb("b3part", [P, F], BF16)
        b3parts = sb("b3parts", [P, QUAD, F], BF16)
        epst = sb("epst", [P, 1])
        halfpi = sb("halfpi", [P, 1])
        crow = sb("crow", [P, F])
        ctmp = sb("ctmp", [P, F])
        ctmp2 = sb("ctmp2", [P, F])
        cstat = sb("cstat", [P, 6])
        cneg2 = sb("cneg2", [P, 1])
        ceps = sb("ceps", [P, 1])
        c3 = sb("c3", [P, QUAD, F], BF16)
        ones_bf = sb("ones_bf", [P, P], BF16)
        ident_bf = sb("ident_bf", [P, P], BF16)
        rhs_sel = sb("rhs_sel", [P, OCT, F], BF16)
        blk, kind, kind12, cterm, last3 = (sb(n, [P, k]) for n, k in (("blk", OCT), ("kind", 4), ("kind12", 12),
                                                                          ("cterm", F), ("last3", 1)))
        junk = sb("junk", [P, 4, F])
        ajunk = sb("ajunk", [P, 2, F])

        dst_c, prev_c = (sb(n, [H, 256], I32) for n in ("dst_c", "prev_c"))
        cont_c, pen_c, score_c, da_c, db_c, decay_c, bw_c, den_c = (
            sb(n, [H, 256]) for n in ("cont_c", "pen_c", "score_c", "da_c", "db_c", "decay_c", "bw_c", "den_c"))
        max_c = sb("max_c", [H, 257])
        zero_c = sb("zero_c", [H, 256])
        pass_c = sb("pass_c", [H, 2])
        rowbuf = sb("rowbuf", [1, 2 * P])
        carry_row = sb("carry_row", [1, P + 1])
        carry_c = sb("carry_c", [H, 1])

        WORK = 33 * QE
        work = sb("work", [P, WORK])
        used = [0]

        def take(*free, parts=P, dt=F32):
            n = 1
            for f in free:
                n *= f
            v = work[0:parts, used[0]:used[0] + n]
            used[0] += n
            assert used[0] <= WORK
            if dt is not F32:
                v = v.bitcast(dt)
            return v.rearrange("p (a b) -> p a b", b=free[1]) if len(free) == 2 else v

        def take2(*free, **kw):
            return [take(*free, **kw) for _ in range(2)]

        xo, oo = take2(OCT, F), take2(OCT, F)
        st = take2(OCT, 6)
        (df, v2, dd, V, q1, q2, t1, t2, t3, t4, lnv, rstd, lnv2, rstd2, scale, qsum) = (
            take2(OCT) for _ in range(16))
        stats = take2(4, OCT)
        rest1, rest2 = take2(4 * OCT), take2(4 * OCT)
        parts = take2(P // 2, dt=BF16)
        statsT = take2(P // 2, dt=BF16)
        srcrow = take2(QE, dt=I32)
        ge = [take(QE, dt=F16).rearrange("p (g e) -> p g e", g=2) for _ in range(2)]
        drow_i, dnext_i, prow_i, pnext_i = (take(2, P, parts=H, dt=I32) for _ in range(4))
        dfirst = take(2)
        dcode, dprev, dlow = (take(2, P + 1, parts=H) for _ in range(3))
        dhigh, drest = [take(P + 2, dt=F16).rearrange("p (g e) -> p g e", g=2) for _ in range(2)]
        arow, bx, RT, xd, U = take2(QE), take2(QUAD, F), take2(QE), take2(QUAD, F), take2(QUAD, F)
        used[0] = 0
        wrow, attr_s, first_nodes, cont = take2(QE), take2(QUAD, F), take2(QUAD, F), take2(QE)
        e0 = take(QE)
        l1, l2, l3 = take(QE), take(QE), take(QE)
        h1 = take(QE)
        bf = take2(QE)
        hn, hm = take2(QUAD, F), take2(QUAD, F)
        m, d0, d1 = take(QE), take(QE), take(QE)
        prod = take2(QE)
        t_, y = take(QE), take2(QUAD, F)
        o = take2(QUAD, F)
        bst = take2(2 * QUAD, 6)
        (bsm, bdf, bv2, bdd, bV, bln, brs) = (take2(2 * QUAD) for _ in range(7))
        brc, bnm = take2(QUAD), take2(QUAD)
        yst = take2(QUAD, 6)
        (ysm, ydf, yv2, ydd, yV, yln, yrs, ynm) = (take2(QUAD) for _ in range(8))

        banks = [ctx.enter_context(nc.psum_tensor(f"bank{i}", [P, 512], F32)) for i in range(8)]
        D = [banks[0:2], banks[2:4]]
        psT = banks[4]
        psF = banks[5:7]
        psX = banks[5:7]
        psR = banks[7]
        E0, E1, E2 = banks[5], banks[6], banks[7]
        Z1, Z2, MT, Z3 = banks[0:2], banks[2:4], banks[4:6], banks[6:8]

        idx_in, tab_in, par_in = sem("idx_in"), sem("tab_in"), sem("par_in")
        setup_dve, setup_pe, setup_act = sem("setup_dve"), sem("setup_pe"), sem("setup_act")
        idx_ready, find_setup, cont_ready, cut_t, cut_sin, const_ready = (
            sem(n) for n in ("idx_ready", "find_setup", "cont_ready", "cut_t", "cut_sin", "const_ready"))
        x_in, o_stored = sem2("x_in"), sem2("o_stored")
        d_filled, o_ready = sem2("d_filled"), sem2("o_ready")
        bn_done, stat_T, stat_copied, d_final = (sem(n) for n in ("bn_done", "stat_T", "stat_copied", "d_final"))
        c_split = sem("c_split")
        c_var, c_var2, c_r, c_r2, c_found, c_score, c_qsum = (
            sem(n) for n in ("c_var", "c_var2", "c_r", "c_r2", "c_found", "c_score", "c_qsum"))
        g_in, srcrow_in = sem2("g_in"), sem2("srcrow_in")
        ge_ready = sem2("ge_ready")
        found, find_used, rows_found, sums_ready = (
            sem(n) for n in ("found", "find_used", "rows_found", "sums_ready"))
        soft_dve, soft_pe, soft_act, decay_ready, decay_stored, cont_stored = (
            sem(n) for n in ("soft_dve", "soft_pe", "soft_act", "decay_ready", "decay_stored", "cont_stored"))
        arow_in, xd_in, u_stored = sem2("arow_in"), sem2("xd_in"), sem2("u_stored")
        bx_ready, bx_T, scan_done, r_T, u_ready = (sem(n) for n in ("bx_ready", "bx_T", "scan_done", "r_T", "u_ready"))
        a_done, a_stored = sem("a_done"), sem("a_stored")
        wrow_in, attr_in, ur_in, cont_in = sem2("wrow_in"), sem2("attr_in"), sem2("ur_in"), sem2("cont_in")
        row_in, scattered = sem2("row_in"), sem2("scattered")
        hn_ready = sem2("hn_ready")
        c_basis, c_l1, c_l2, c_norm_r, c_bvar, c_bmul = (
            sem(n) for n in ("c_basis", "c_l1", "c_l2", "c_norm_r", "c_bvar", "c_bmul"))
        z1_done, h1_ready, z2_done, bf_ready, hm_ready, m_T = (
            sem(n) for n in ("z1_done", "h1_ready", "z2_done", "bf_ready", "hm_ready", "m_T"))
        c_prod, z3_done, c_l3, c_y, c_yr, ynm_ready, row_ready = (
            sem(n) for n in ("c_prod", "z3_done", "c_l3", "c_y", "c_yr", "ynm_ready", "row_ready"))

        def octet_rows(i):
            return x[bass.ds(i * OROWS, OROWS), :].rearrange("(p j) f -> p j f", j=OCT)

        def quad_rows(t, q):
            return t[bass.ds(q * QE, QE), :].rearrange("(j p) f -> p j f", p=P)

        def node_tiles(q):
            return first_nodes[q] if isinstance(q, int) and q < 2 else G[:, bass.ds(QUAD * (q - 2), QUAD), :]

        LAST = N - OROWS
        FRESH = (NO - 1) * OROWS - LAST
        assert FRESH % OCT == 0

        VAR_OPS, V_AT = 7, 6
        VAR2_OPS, VAR2_AT, SCALE_AT = 5, 4, 5
        SPLIT_OPS = 5
        SETUP_OPS = 10
        BVAR_OPS, BV_AT = 13, 13
        PROD_OPS, PROD_AT = 4, 4
        Y_OPS, YV_AT = 14, 14

        A1 = (0, 4, 4 + (NQ - 4) // 2 * 2, NQ)
        a2lo = NQ + 4 + NQ % 2
        A2 = (NQ, a2lo, max(a2lo, NO - 2), NO + 2)
        blo = 6
        B = (0, blo, max(blo, NQ // 2 * 2), NQ + 4)

        block = ctx.enter_context(nc.Block())

        @block.sync
        def _(sp):
            def load_dense(i, slot, half):
                wait_past(sp, bn_done, i - 1)
                wait_past(sp, d_filled[1], i - 1)
                if isinstance(i, int) and i == NO - 1:
                    rows_ = x[LAST:N, :].rearrange("(p j) f -> p j f", j=OCT)
                else:
                    rows_ = octet_rows(i)
                sp.dma_start(xo[slot], rows_).then_inc(x_in[slot], 16)

            load_dense(0, 0, 0)
            sp.dma_start(src_i[:, :], src_tiles).then_inc(idx_in, 16)
            for dst, src in ((dst_i, dst_tiles), (next_i, next_tiles), (wt, weight_tiles)):
                sp.dma_start(dst[:, :], src).then_inc(tab_in, 16)
            base = P
            for dst, off in ((drow_i, 0), (dnext_i, 1), (prow_i, -P), (pnext_i, 1 - P)):
                for g in range(2):
                    v = dst_flat[base + off + g * H * P:base + off + (g + 1) * H * P].rearrange("(k j) -> k j", j=P)
                    sp.dma_start(dst[:, g, :], v).then_inc(tab_in, 16)
            for dst, off in ((dst_c, 0), (prev_c, -1)):
                sp.dma_start(dst[:, :], dst_flat[base + off:base + off + NT * P].rearrange("(k j) -> k j", j=256)
                             ).then_inc(tab_in, 16)
            for dst, src in ((ident, eye), (iota, iota1), (w1, W1), (w2, W2), (w3, W3), (muneg, mu),
                             (b1c, b1.rearrange("(p a) -> p a", a=1)), (b2c, b2.rearrange("(p a) -> p a", a=1))):
                sp.dma_start(dst[:, :], src).then_inc(par_in, 16)
            sp.dma_start(w0[:, :], W0[0, :].partition_broadcast(P)).then_inc(par_in, 16)
            sp.dma_start(b3row[:, :], b3.rearrange("(a f) -> a f", a=1)).then_inc(par_in, 16)
            sp.dma_start(b3all[:, :], b3.partition_broadcast(P)).then_inc(par_in, 16)

            def store_dense(i, slot, half):
                sp.wait_ge(o_ready[1], i + 1)
                if isinstance(i, int) and i == NO - 1:
                    skip = FRESH // OCT
                    rows_ = out[(NO - 1) * OROWS:N, :].rearrange("(p j) f -> p j f", j=OCT)
                    sp.dma_start(rows_, oo[slot][skip:P]).then_inc(o_stored[slot], 16)
                else:
                    rows_ = out[bass.ds(i * OROWS, OROWS), :].rearrange("(p j) f -> p j f", j=OCT)
                    sp.dma_start(rows_, oo[slot]).then_inc(o_stored[slot], 16)

            def ahead(i, slot, half):
                return i + 1, 1 - slot, half + slot

            def load_sources(i, slot, half):
                wait_past(sp, ge_ready[0], i - 1)
                wait_past(sp, ge_ready[1], i - 1)
                sp.dma_start(srcrow[slot], src_flat[bass.ds(i * QE, QE)].partition_broadcast(P)
                             ).then_inc(srcrow_in[slot], 16)

            def step_a1(i, slot, half):
                n, s, h = ahead(i, slot, half)
                if live(n, NQ):
                    load_sources(n, s, h)
                load_dense(n, s, h)
                k, s, h = back(i, slot, half, 2)
                if live(k, NO):
                    store_dense(k, s, h)

            def step_a2(i, slot, half):
                n, s, h = ahead(i, slot, half)
                if live(n, NO):
                    load_dense(n, s, h)
                q, s, h = back(i, slot, half, NQ)
                if live(q, NQ):
                    wait_past(sp, scan_done, q - 1)
                    sp.dma_start(arow[s], decay_flat[bass.ds(q * QE, QE)].partition_broadcast(P)
                                 ).then_inc(arow_in[s], 16)
                k, s, h = back(i, slot, half, 2)
                if live(k, NO):
                    store_dense(k, s, h)
                q, s, h = back(i, slot, half, NQ + 2)
                if live(q, NQ):
                    store_u(q, s)

            def store_u(q, s):
                sp.wait_ge(u_ready, q + 1)
                sp.dma_start(quad_rows(node_rows, q), U[s]).then_inc(u_stored[s], 16)

            load_sources(0, 0, 0)
            sweep(sp, *A1, step_a1)
            sp.wait_ge(cont_ready, 1)
            sp.dma_start(cont_flat.rearrange("(k j) -> k j", j=256), cont_c[:, :]).then_inc(cont_stored, 16)
            sp.wait_ge(decay_ready, 1)
            sp.dma_start(decay_flat.rearrange("(k j) -> k j", j=256), decay_c[:, :]).then_inc(decay_stored, 16)
            sp.wait_ge(cont_stored, 16)
            sp.wait_ge(decay_stored, 16)
            sweep(sp, *A2, step_a2)
            for s in range(2):
                sp.wait_ge(o_stored[s], 16 * (NO // 2))
                sp.wait_ge(u_stored[s], 16 * ((NQ + 1 - s) // 2))
            sp.sem_inc(a_stored, 1)
            sp.wait_ge(a_done, 3)

            def step_b(q, slot, half):
                wait_past(sp, z1_done, q - 1)
                sp.dma_start(wrow[slot], weight_flat[bass.ds(q * QE, QE)].partition_broadcast(P)
                             ).then_inc(wrow_in[slot], 16)
                wait_past(sp, hn_ready[0], q - 1)
                wait_past(sp, hn_ready[1], q - 1)
                sp.dma_start(node_tiles(q), quad_rows(node_rows, q)).then_inc(ur_in[slot], 16)
                wait_past(sp, hm_ready, q - 1)
                if isinstance(q, int) and q == NQ - 1:
                    whole, rest = divmod(E - q * QE, P)
                    for j in range(whole):
                        r = q * QE + j * P
                        sp.dma_start(attr_s[slot][:, j, :], attr[r:r + P, :]).then_inc(attr_in[slot], 16)
                    if rest:
                        sp.dma_start(attr_s[slot][0:rest, whole, :], attr[E - rest:E, :]).then_inc(attr_in[slot], 16)
                else:
                    sp.dma_start(attr_s[slot], quad_rows(attr, q)).then_inc(attr_in[slot], 16)
                k, s, h = back(q, slot, half, 1)
                if live(k, NQ):
                    load_flags(k, s)

            def load_flags(q, slot):
                wait_past(sp, z3_done, q - 1)
                sp.dma_start(cont[slot], cont_flat[bass.ds(q * QE, QE)].partition_broadcast(P)
                             ).then_inc(cont_in[slot], 16)

            sweep(sp, 0, B[1], max(B[1], (NQ - 1) // 2 * 2), NQ, step_b)
            load_flags(NQ - 1, (NQ - 1) % 2)

        ATTR_LOADS = -(-(E - (NQ - 1) * QE) // P)

        @block.gpsimd
        def _(pool):
            pool.wait_ge(idx_in, 16)

            def gather(dst, table, idx, t, bound, s):
                nc.gpsimd.indirect_dma_start(dst, None, table, bass.IndirectOffsetOnAxis(ap=idx[:, t:t + 1], axis=0),
                                             bounds_check=bound, oob_is_err=False).then_inc(s, 16)

            def gather_sources(q):
                wait_past(pool, g_in[q % 2], 64 * (q // 2))
                for t in range(QUAD * q, QUAD * q + QUAD):
                    gather(G[:, t, :], x, src_i, t, N - 1, g_in[q % 2])

            gather_sources(0)
            gather_sources(1)
            pool.wait_ge(find_setup, 1)
            for q in range(NQ):
                s = q % 2
                pool.wait_ge(srcrow_in[s], 16 * (q // 2 + 1))
                wait_past(pool, found, 2 * (q - 1))
                nc.gpsimd.tensor_scalar(ge[s][:, 1, :], srcrow[s], dfirst[:, 1:2], None, ALU.is_ge
                                        ).then_inc(ge_ready[1], 1)
                if q + 2 < NQ:
                    gather_sources(q + 2)

            def gather_nodes(q):
                wait_past(pool, u_ready, q - 1)
                wait_past(pool, xd_in[q % 2], 64 * (q // 2))
                for j in range(QUAD):
                    gather(xd[q % 2][:, j, :], x, xd_idx, QUAD * q + j, N - 1, xd_in[q % 2])

            def weigh(q):
                wait_past(pool, bx_T, q - 1)
                nc.gpsimd.tensor_tensor(bx[q % 2], G[:, QUAD * q:QUAD * q + QUAD, :],
                                        bw[:, QUAD * q:QUAD * q + QUAD].unsqueeze(2).to_broadcast([P, QUAD, F]),
                                        ALU.mult).then_inc(bx_ready, 1)

            pool.wait_ge(idx_ready, 1)
            for s in range(2):
                pool.wait_ge(g_in[s], 64 * ((NQ + 1 - s) // 2))
            gather_nodes(0)
            gather_nodes(1)
            pool.wait_ge(sums_ready, 1)
            weigh(0)
            weigh(1)
            for q in range(2, NQ):
                weigh(q)
                gather_nodes(q)
            pool.wait_ge(rows_found, 1)
            pool.wait_ge(a_stored, 1)

            def gather_rows(q):
                wait_past(pool, row_in[q % 2], 64 * (q // 2))
                for t in range(QUAD * q, QUAD * q + QUAD):
                    gather(G[:, t, :], node_rows, row_idx, t, NT * P - 1, row_in[q % 2])

            LEAD = 3
            for q in range(LEAD):
                gather_rows(q)
            for i in range(NQ + 5):
                k = i - 5
                if k >= 0:
                    s = k % 2
                    pool.wait_ge(row_ready, k + 1)
                    wait_past(pool, scattered[s], 64 * (k // 2))
                    for j in range(QUAD):
                        t = QUAD * k + j
                        nc.gpsimd.indirect_dma_start(
                            out, bass.IndirectOffsetOnAxis(ap=out_idx[:, t:t + 1], axis=0), o[s][:, j, :], None,
                            bounds_check=N - 1, oob_is_err=False).then_inc(scattered[s], 16)
                k = i - 1
                if 0 <= k < NQ:
                    s = k % 2
                    pool.wait_ge(hn_ready[0], k + 1)
                    pool.wait_ge(hn_ready[1], k + 1)
                    pool.wait_ge(attr_in[s], 16 * (k // 2 + (ATTR_LOADS if k == NQ - 1 else 1)))
                    wait_past(pool, m_T, k - 1)
                    nc.gpsimd.tensor_tensor(hm[s], hn[s], attr_s[s], ALU.mult
                                                   ).then_inc(hm_ready, 1)
                if i + LEAD < NQ:
                    gather_rows(i + LEAD)
            for s in range(2):
                pool.wait_ge(scattered[s], 64 * ((NQ + 1 - s) // 2))

        @block.vector
        def _(dve):
            v = nc.vector
            ch = Chain(dve, setup_dve, 0)
            ch.begin(0)
            ch.add(v.memset(ones[:, :], 1.0))
            ch.add(v.memset(ones_bf[:, :], 1.0))
            ch.add(v.memset(epst[:, :], EPS))
            ch.add(v.memset(halfpi[:, :], PI / 2))
            ch.add(v.memset(zero_c[:, :], 0.0))
            for padded in (dhigh, drest, dfirst, parts[0], parts[1]):
                ch.add(v.memset(padded, 0.0))
            ch.settle()
            assert ch.n == SETUP_OPS
            for s in range(2):
                ch.add(v.memset(parts[s][:, TERMS:TERMS + 3], 1.0))
            var, var2 = Chain(dve, c_var, VAR_OPS), Chain(dve, c_var2, VAR2_OPS)

            def dense_stats(i, s, h, tiles):
                dve.wait_ge(x_in[s], 16 * (h + 1))
                for j in tiles:
                    ins = v.bn_stats(st[s][:, j, :], xo[s][:, j, :])
                    if j == OCT - 1:
                        ins.then_inc(bn_done, 1)

            def stats_part(i, s, between):
                between(0)
                dve.wait_ge(bn_done, i + 1)
                var.begin(i)
                twice_mean = stats[s][:, 3, :]
                var.add(v.tensor_tensor(twice_mean, st[s][:, :, 1], st[s][:, :, 4], ALU.add))
                var.add(v.tensor_tensor(df[s], st[s][:, :, 1], st[s][:, :, 4], ALU.subtract))
                var.add(v.tensor_tensor(v2[s], st[s][:, :, 2], st[s][:, :, 5], ALU.add))
                between(1)
                var.settle()
                var.add(v.tensor_tensor(dd[s], df[s], df[s], ALU.mult))
                var.add(v.tensor_tensor(q1[s], twice_mean, twice_mean, ALU.mult))
                between(2)
                var.settle()
                var.add(v.scalar_tensor_tensor(V[s], dd[s], float(F) / 4, v2[s], ALU.mult, ALU.add))
                between(3)
                var.settle()
                var.add(v.scalar_tensor_tensor(q2[s], q1[s], float(F) / 4, V[s], ALU.mult, ALU.add))
                var.end()

            def nothing(k):
                pass

            dense_stats(0, 0, 0, range(OCT))
            stats_part(0, 0, nothing)
            dve.wait_ge(idx_in, 16)
            dve.wait_ge(tab_in, 16 * 13)
            ch.add(v.tensor_scalar(xd_idx[:, :], dst_i[:, :], float(N - 1), None, ALU.min))
            ch.add(v.tensor_tensor(tmp_t[:, :], dst_i[:, :], next_i[:, :], ALU.is_equal))
            ch.add(v.tensor_scalar(src_code[:, :], src_i[:, :], 2.0 / CODE, 1.0 / CODE, ALU.mult, ALU.add))
            ch.settle()
            ch.link(v.scalar_tensor_tensor(out_idx[:, :], tmp_t[:, :], float(SKIP), dst_i[:, :], ALU.mult, ALU.add))
            v.sem_inc(idx_ready, 1)
            for rows_, nxt, code in ((drow_i, dnext_i, dcode), (prow_i, pnext_i, dprev)):
                ch.link(v.tensor_tensor(code[:, :, 0:P], rows_, nxt, ALU.is_equal))
                ch.link(v.tensor_scalar(code[:, :, 0:P], code[:, :, 0:P], -1.0, 1.0, ALU.mult, ALU.add))
                ch.link(v.scalar_tensor_tensor(code[:, :, 0:P], rows_, 2.0, code[:, :, 0:P], ALU.mult, ALU.add))
            ch.link(v.memset(dprev[0:1, 0, 0:P], 0.0))
            ch.link(v.tensor_tensor(dcode[:, :, 0:P], dcode[:, :, 0:P], dprev[:, :, 0:P], ALU.subtract))
            ch.link(v.tensor_scalar(dprev[:, :, 0:P], dcode[:, :, 0:P], RND, None, ALU.add))
            ch.link(v.tensor_scalar(dprev[:, :, 0:P], dprev[:, :, 0:P], -RND, None, ALU.add))
            ch.link(v.tensor_tensor(dlow[:, :, 0:P], dcode[:, :, 0:P], dprev[:, :, 0:P], ALU.subtract))
            for part, of in ((dhigh, dprev), (drest, dlow)):
                ch.add(v.tensor_scalar(part[0:H, :, 0:P], of[:, :, 0:P], 1.0 / CODE, None, ALU.mult))
            ch.add(v.memset(dhigh[0:H, :, P:P + 1], 1.0))
            ch.add(v.tensor_copy(dfirst[0:H].unsqueeze(2), drow_i[:, :, 0:1]))
            ch.settle()
            v.sem_inc(find_setup, 1)
            ch.link(v.tensor_tensor(cont_c[:, :], dst_c[:, :], prev_c[:, :], ALU.is_equal))
            ch.add(v.tensor_scalar(pen_c[:, :], cont_c[:, :], -1.0, BIG, ALU.add, ALU.mult))
            ch.link(v.tensor_reduce(pass_c[:, 0:1], cont_c[:, :], AX.X, ALU.min))
            ch.link(v.tensor_scalar(pass_c[:, 1:2], pass_c[:, 0:1], -1.0, BIG, ALU.add, ALU.mult))
            v.sem_inc(cont_ready, 1)
            ch.link(v.tensor_scalar(tmp_t[:, :], wt[:, :], -ONSET, 1.0 / (CUTOFF - ONSET), ALU.add, ALU.mult))
            ch.link(v.tensor_scalar(tmp_t[:, :], tmp_t[:, :], 0.0, 1.0, ALU.max, ALU.min))
            v.sem_inc(cut_t, 1)
            dve.wait_ge(cut_sin, 1)
            ch.link(v.tensor_scalar(tmp_t[:, :], cut[:, :], 0.5, 0.5, ALU.mult, ALU.add))
            ch.link(v.tensor_scalar(cut[:, :], wt[:, :], ONSET, None, ALU.is_lt))
            ch.link(v.tensor_tensor(tmp_t[:, :], tmp_t[:, :], cut[:, :], ALU.max))
            ch.link(v.tensor_scalar(cut[:, :], wt[:, :], CUTOFF, None, ALU.is_le))
            ch.link(v.tensor_tensor(cut[:, :], cut[:, :], tmp_t[:, :], ALU.mult))
            dve.wait_ge(par_in, 16 * 11)
            ch.add(v.tensor_scalar(nb1[:, :], b1c[:, :], -1.0, None, ALU.mult))
            ch.link(v.tensor_scalar(b1m[:, :], b1c[:, :], -LN2, None, ALU.add))
            v.sem_inc(const_ready, 1)
            dve.wait_ge(setup_pe, 2)
            ch.link(v.tensor_tensor(b2c[:, :], b2c[:, :], E1[:, 0:1], ALU.add))
            ch.add(v.tensor_scalar(nb2[:, :], b2c[:, :], -1.0, None, ALU.mult))
            ch.add(v.tensor_scalar(kb2[:, :], b2c[:, :], -LN2, None, ALU.add))
            dve.wait_ge(setup_act, 3)
            ch.link(v.scalar_tensor_tensor(crow[:, :], E0[:, 0:F], 0.0, ctmp[:, :], ALU.max, ALU.add))
            ch.link(v.tensor_scalar(crow[:, :], crow[:, :], -LN2, None, ALU.add))
            ch.link(v.tensor_reduce(ceps[:, :], crow[:, :], AX.X, ALU.add))
            ch.link(v.tensor_scalar(ceps[:, :], ceps[:, :], -1.0 / F, None, ALU.mult))
            ch.link(v.tensor_scalar(crow[:, :], crow[:, :], ceps[:, :], None, ALU.add))
            ch.link(v.tensor_tensor(ctmp[:, :], crow[:, :], crow[:, :], ALU.mult))
            ch.link(v.tensor_reduce(cneg2[:, :], ctmp[:, :], AX.X, ALU.add))
            ch.link(v.tensor_scalar(ceps[:, :], cneg2[:, :], 1.0 / F, EPS, ALU.mult, ALU.add))
            ch.link(v.tensor_scalar(cneg2[:, :], cneg2[:, :], -1.0, None, ALU.mult))
            rows_ = ident[:, 0:TERMS]
            ch.add(v.tensor_reduce(blk[:, :], rows_.rearrange("k (g b) -> k b g", b=OCT), AX.X, ALU.add))
            ch.add(v.tensor_reduce(kind12[:, :], rows_.rearrange("k (g b) -> k g b", b=OCT), AX.X, ALU.add))
            ch.add(v.tensor_copy(ident_bf[:, :], ident[:, :]))
            ch.add(v.memset(ctmp2[:, :], 0.0))
            ch.settle()
            ch.link(v.tensor_reduce(kind[:, :], kind12[:, :].rearrange("k (p c) -> k c p", c=4), AX.X, ALU.add))
            ch.add(v.tensor_reduce(last3[:, :], ident[:, TERMS:TERMS + 3], AX.X, ALU.add))
            ch.add(v.tensor_scalar(cterm[:, :], ones[:, :], kind[:, 3:4], -0.5, ALU.mult, ALU.mult))
            ch.add(v.tensor_tensor(kind[:, 0:3], kind[:, 0:3], ident[:, TERMS:TERMS + 3], ALU.subtract))
            ch.settle()
            ch.link(v.tensor_scalar(blk[:, :], blk[:, :], last3[:, :], None, ALU.add))
            for k in range(3):
                part, left = rhs_sel[:, k, :], crow if k == 0 else ctmp
                ch.link(v.tensor_copy(part, left[:, :]))
                ch.add(v.scalar_tensor_tensor(ctmp2[:, :], part, ident[:, k:k + 1], ctmp2[:, :],
                                              ALU.mult, ALU.add))
                ch.add(v.scalar_tensor_tensor(cterm[:, :], part, kind[:, k:k + 1], cterm[:, :], ALU.mult, ALU.add))
                ch.link(v.tensor_tensor(ctmp[:, :], left[:, :], part, ALU.subtract))
            ch.link(v.memset(b3sum[:, :], 0.0))
            for k in range(3):
                ch.link(v.tensor_copy(b3part[:, :], b3all[:, :]))
                ch.add(v.scalar_tensor_tensor(b3sum[:, :], b3part[:, :], ident[:, k:k + 1], b3sum[:, :],
                                              ALU.mult, ALU.add))
                ch.link(v.tensor_tensor(b3all[:, :], b3all[:, :], b3part[:, :], ALU.subtract))
            ch.add(v.tensor_copy(b3parts[:, :, :], b3sum[:, :].unsqueeze(1).to_broadcast([P, QUAD, F])))
            ch.link(v.tensor_copy(c3[:, :, :], ctmp2[:, :].unsqueeze(1).to_broadcast([P, QUAD, F])))
            ch.link(v.tensor_tensor(rhs_sel[:, :, :], blk[:, :].unsqueeze(2).to_broadcast([P, OCT, F]),
                                    cterm[:, :].unsqueeze(1).to_broadcast([P, OCT, F]), ALU.mult))
            v.sem_inc(const_ready, 1)


            split = Chain(dve, c_split, SPLIT_OPS)
            cf, cs = Chain(dve, c_found, QUAD), Chain(dve, c_score, QUAD)

            def second_variance(i, s, between):
                dve.wait_ge(c_r, 3 * i + 3)
                dve.wait_ge(c_var, VAR_OPS * (i + 1))
                dve.wait_ge(c_qsum, OCT * i + OCT)
                var2.begin(i)
                var2.add(v.tensor_tensor(t1[s], V[s], rstd[s], ALU.mult))
                var2.add(v.tensor_tensor(t2[s], qsum[s], q2[s], ALU.subtract))
                between(0)
                var2.settle()
                var2.add(v.scalar_tensor_tensor(t3[s], t2[s], cneg2[:, :], t1[s], ALU.add, ALU.add))
                between(1)
                var2.settle()
                var2.add(v.tensor_tensor(t4[s], t3[s], rstd[s], ALU.mult))

            def second_scale(i, s):
                dve.wait_ge(c_r2, 2 * i + 2)
                var2.add(v.tensor_tensor(scale[s], rstd[s], rstd2[s], ALU.mult))
                var2.end()

            def split_stats(i, s, between):
                dve.wait_ge(c_r, 3 * i + 3)
                dve.wait_ge(c_var, VAR_OPS * (i + 1))
                wait_past(dve, stat_T, i - 1)
                split.begin(i)
                n = 4 * OCT
                a0, a1, a2 = (parts[s][:, k * n:(k + 1) * n] for k in range(3))
                whole = stats[s].rearrange("p a b -> p (a b)")
                split.add(v.tensor_copy(a0, whole))
                between(0)
                split.settle()
                split.add(v.tensor_tensor(rest1[s], whole, a0, ALU.subtract))
                between(1)
                split.settle()
                split.add(v.tensor_copy(a1, rest1[s]))
                between(2)
                split.settle()
                split.add(v.tensor_tensor(rest2[s], rest1[s], a1, ALU.subtract))
                between(3)
                split.settle()
                split.add(v.tensor_copy(a2, rest2[s]))
                split.end()

            def compare_sources(q, s, h):
                dve.wait_ge(srcrow_in[s], 16 * (h + 1))
                wait_past(dve, found, 2 * (q - 1))
                v.tensor_scalar(ge[s][:, 0, :], srcrow[s], dfirst[:, 0:1], None, ALU.is_ge).then_inc(ge_ready[0], 1)

            def use_found(q, j):
                if j == 0:
                    dve.wait_ge(found, 2 * q + 2)
                    cf.begin(q)
                wait_past(dve, c_found, cf.base + cf.n - 1)
                codes = psF[j // 2][:, (j % 2) * (P + 1):(j % 2) * (P + 1) + P]
                cf.add(v.scalar_tensor_tensor(junk[:, j % 2, :], codes, src_code[:, bass.ds(QUAD * q + j, 1)],
                                              iota[:, :], ALU.is_equal, ALU.mult,
                                              accum_out=hit[:, bass.ds(QUAD * q + j, 1)]))
                if j % 2:
                    v.tensor_copy(tile1[:, bass.ds(QUAD * q + j - 1, 2)], psF[j // 2][:, P:2 * P + 2:P + 1]
                                  ).then_inc(find_used, 1)

            def scores(q, s, h, j):
                if j == 0:
                    dve.wait_ge(g_in[s], 64 * (h + 1))
                    cs.begin(q)
                wait_past(dve, c_score, cs.base + cs.n - 1)
                cs.add(v.scalar_tensor_tensor(junk[:, 2 + j % 2, :], G[:, bass.ds(QUAD * q + j, 1), :], 1.0, w0[:, :],
                                              ALU.mult, ALU.mult, accum_out=score[:, bass.ds(QUAD * q + j, 1)]))

            def step_a1(i, s, h):
                k, ks, kh = back(i, s, h, 1)
                if live(k, NO):
                    second_variance(k, ks, lambda n: compare_sources(i, s, h) if n == 0 else use_found(k, 0))
                else:
                    compare_sources(i, s, h)
                split_stats(i, s, lambda n: use_found(k, n + 1) if n < QUAD - 1 and live(k, NO) else None)
                if live(k, NO):
                    second_scale(k, ks)
                dense_stats(i + 1, 1 - s, h + s, range(OCT))
                stats_part(i + 1, 1 - s, lambda n: scores(i, s, h, n))
            straight(0, NQ, step_a1)
            for j in range(QUAD):
                use_found(NQ - 1, j)

            dve.wait_ge(c_found, QUAD * NQ)
            dve.wait_ge(c_score, QUAD * NQ)
            dve.wait_ge(find_used, 2 * NQ)
            ch.add(v.scalar_tensor_tensor(tmp_t[:, :], tile1[:, :], float(P), hit[:, :], ALU.mult, ALU.add))
            ch.add(v.tensor_scalar(src_code[:, :], hit[:, :], 0.0, float(SKIP), ALU.is_equal, ALU.mult))
            ch.settle()
            ch.link(v.scalar_tensor_tensor(row_idx[:, :], tmp_t[:, :], -float(P + 1), src_code[:, :], ALU.add, ALU.add))
            v.sem_inc(rows_found, 1)

            soft = Chain(dve, soft_dve, 0)
            soft.begin(0)
            v.sem_inc(soft_dve, 1)
            soft.n = 1
            dve.wait_ge(soft_pe, 2)
            soft.link(v.tensor_copy(score_c[:, :], E0[0:H, 0:256]))
            soft.link(v.tensor_tensor_scan(max_c[:, 1:257], pen_c[:, :], score_c[:, :], -BIG, ALU.add, ALU.max))
            assert soft.n == 3
            dve.wait_ge(soft_pe, 4)
            soft.add(v.tensor_copy(rowbuf[:, :], E1[0:1, 0:2 * P]))
            soft.link(v.memset(carry_row[:, 0:1], -BIG))
            soft.link(v.tensor_tensor_scan(carry_row[0:1, 1:H + 1], rowbuf[0:1, P:P + H], rowbuf[0:1, 0:H], -BIG,
                                           ALU.add, ALU.max))
            assert soft.n == 6
            dve.wait_ge(soft_pe, 5)
            soft.link(v.tensor_copy(max_c[:, 0:1], E2[0:H, 0:1]))
            soft.link(v.tensor_tensor_scan(max_c[:, 1:257], pen_c[:, :], score_c[:, :], max_c[:, 0:1], ALU.add,
                                           ALU.max))
            soft.add(v.tensor_tensor(da_c[:, :], max_c[:, 0:256], pen_c[:, :], ALU.add))
            soft.add(v.tensor_tensor(db_c[:, :], score_c[:, :], max_c[:, 1:257], ALU.subtract))
            soft.settle()
            soft.link(v.tensor_tensor(da_c[:, :], da_c[:, :], max_c[:, 1:257], ALU.subtract))
            assert soft.n == 11
            dve.wait_ge(soft_act, 2)
            soft.add(v.tensor_tensor_scan(den_c[:, :], decay_c[:, :], bw_c[:, :], 0.0, ALU.mult, ALU.add))
            soft.link(v.tensor_tensor_scan(da_c[:, :], decay_c[:, :], zero_c[:, :], 1.0, ALU.mult, ALU.add))
            assert soft.n == 13
            dve.wait_ge(soft_pe, 7)
            soft.add(v.tensor_copy(rowbuf[:, :], E1[0:1, 0:2 * P]))
            soft.link(v.memset(carry_row[:, 0:1], 0.0))
            soft.link(v.tensor_tensor_scan(carry_row[0:1, 1:H + 1], rowbuf[0:1, P:P + H], rowbuf[0:1, 0:H], 0.0,
                                           ALU.mult, ALU.add))
            assert soft.n == 16
            dve.wait_ge(soft_pe, 8)
            soft.link(v.tensor_copy(carry_c[:, :], E2[0:H, 0:1]))
            soft.link(v.tensor_tensor_scan(den_c[:, :], decay_c[:, :], bw_c[:, :], carry_c[:, :], ALU.mult, ALU.add))
            soft.link(v.tensor_scalar(den_c[:, :], den_c[:, :], 1e-20, None, ALU.max))
            soft.link(v.reciprocal(den_c[:, :], den_c[:, :]))
            assert soft.n == 20
            dve.wait_ge(soft_pe, 12)
            for g in range(2):
                soft.add(v.tensor_copy(bw[:, g:NT:2], E0[:, g * H:(g + 1) * H]))
                soft.add(v.tensor_copy(rden[:, g:NT:2], E1[:, g * H:(g + 1) * H]))
            soft.settle()
            v.sem_inc(sums_ready, 1)

            def running_sum(q, s, h):
                dve.wait_ge(arow_in[s], 16 * (h + 1))
                dve.wait_ge(bx_T, q + 1)
                wait_past(dve, r_T, q - 1)
                if isinstance(q, int) and q == 0:
                    start = 0.0
                else:
                    dve.wait_ge(scan_done, q)
                    start = RT[1 - s][:, QE - 1:QE]
                v.tensor_tensor_scan(RT[s], arow[s], psX[s][:, :], start, ALU.mult, ALU.add).then_inc(scan_done, 1)

            def node_sums(q, s, h, j):
                if j == 0:
                    dve.wait_ge(r_T, q + 1)
                    dve.wait_ge(xd_in[s], 64 * (h + 1))
                    wait_past(dve, u_stored[s], 16 * h)
                ins = v.scalar_tensor_tensor(U[s][:, j, :], psR[:, j * P:(j + 1) * P],
                                             rden[:, bass.ds(QUAD * q + j, 1)], xd[s][:, j, :],
                                             ALU.mult, ALU.add)
                if j == QUAD - 1:
                    ins.then_inc(u_ready, 1)

            def step_a2(i, s, h):
                k, ks, kh = back(i, s, h, 1)
                qr, sr, hr = back(i, s, h, NQ + 1)
                qn, sn, hn_ = back(i, s, h, NQ + 2)

                def sums(n):
                    if live(qn, NQ):
                        node_sums(qn, sn, hn_, n)

                def more(n):
                    if n < 2:
                        sums(n + 2)
                    elif live(i + 1, NO):
                        dense_stats(i + 1, 1 - s, h + s, (2 * n - 4, 2 * n - 3))

                def scan(n):
                    if n == 1 and live(qr, NQ):
                        running_sum(qr, sr, hr)

                if live(k, NO):
                    second_variance(k, ks, sums)
                else:
                    sums(0)
                    sums(1)
                if live(i, NO):
                    split_stats(i, s, more)
                else:
                    more(0)
                    more(1)
                if live(k, NO):
                    second_scale(k, ks)
                if live(i + 1, NO):
                    dense_stats(i + 1, 1 - s, h + s, range(4, OCT))
                    stats_part(i + 1, 1 - s, scan)
                else:
                    scan(1)

            straight(NQ, NO + 2, step_a2)
            dve.wait_ge(u_ready, NQ)
            v.sem_inc(a_done, 1)
            dve.wait_ge(a_done, 3)
            dve.wait_ge(a_stored, 1)

            bvar, bmul, prod_c, yc = (Chain(dve, c_bvar, BVAR_OPS), Chain(dve, c_bmul, 3),
                                      Chain(dve, c_prod, PROD_OPS), Chain(dve, c_y, Y_OPS))

            def variance(c, stat, sm_, df_, v2_, dd_, V_, between):
                c.add(v.tensor_tensor(sm_, stat[:, :, 1], stat[:, :, 4], ALU.add))
                c.add(v.tensor_tensor(df_, stat[:, :, 1], stat[:, :, 4], ALU.subtract))
                c.add(v.tensor_tensor(v2_, stat[:, :, 2], stat[:, :, 5], ALU.add))
                between(1)
                c.settle()
                c.add(v.tensor_tensor(dd_, df_, df_, ALU.mult))
                between(2)
                c.settle()
                c.add(v.scalar_tensor_tensor(V_, dd_, float(F) / 4, v2_, ALU.mult, ALU.add))

            def finish_rows(q, s, between):
                dve.wait_ge(c_l3, 3 * q + 3)
                yc.begin(q)
                yc.add(v.scalar_tensor_tensor(t_, Z3[s][:, :], 0.0, l3, ALU.max, ALU.add))
                between(-1)
                yc.settle()
                wait_past(dve, row_ready, q - 1)
                for j in range(QUAD):
                    yc.add(v.scalar_tensor_tensor(y[s][:, j, :], node_tiles(q)[:, j, :],
                                                  rnode[:, bass.ds(QUAD * q + j, 1)], t_[:, j * P:(j + 1) * P],
                                                  ALU.mult, ALU.add))
                between(0)
                yc.settle()
                for j in range(QUAD):
                    yc.add(v.bn_stats(yst[s][:, j, :], y[s][:, j, :]))
                between(3)
                yc.settle()
                variance(yc, yst[s], ysm[s], ydf[s], yv2[s], ydd[s], yV[s], between)
                yc.end()

            def norm_factors(q, s, n):
                if n == 0:
                    dve.wait_ge(c_norm_r, 2 * q + 2)
                    wait_past(dve, hn_ready[0], q - 1)
                    bmul.begin(q)
                    bmul.add(v.tensor_tensor(brc[s], brs[s][:, 0:QUAD], cut[:, bass.ds(QUAD * q, QUAD)], ALU.mult))
                    bmul.add(v.tensor_copy(rnode[:, bass.ds(QUAD * q, QUAD)], brs[s][:, QUAD:2 * QUAD]))
                    return
                bmul.settle()
                bmul.add(v.scalar_tensor_tensor(bnm[s], bsm[s][:, 0:QUAD], -0.5, brc[s], ALU.mult, ALU.mult))
                bmul.end()

            def norm_rows(q, s):
                bmul.settle()
                wait_past(dve, hm_ready, q - 1)
                for j in range(QUAD // 2, QUAD):
                    ins = v.tensor_scalar(hn[s][:, j, :], G[:, bass.ds(QUAD * q + j, 1), :], brc[s][:, j:j + 1],
                                          bnm[s][:, j:j + 1], ALU.mult, ALU.add)
                ins.then_inc(hn_ready[1], 1)

            def running_product(q, s, h, n):
                if n == 0:
                    dve.wait_ge(m_T, q + 1)
                    dve.wait_ge(bf_ready, q + 1)
                    prod_c.begin(q)
                    prod_c.add(v.scalar_tensor_tensor(m, bf[s], kb2[:, :], MT[s][:, :], ALU.add, ALU.mult))
                    return
                prod_c.settle()
                if n == 1:
                    dve.wait_ge(cont_in[s], 16 * (h + 1))
                    prod_c.add(v.tensor_tensor(d0, m, cont[s], ALU.mult))
                if n == 2:
                    prod_c.add(v.tensor_tensor(d1, m, d0, ALU.subtract))
                if n == 3:
                    wait_past(dve, z3_done, q - 1)
                    start = 1.0 if isinstance(q, int) and q == 0 else prod[1 - s][:, QE - 1:QE]
                    prod_c.add(v.tensor_tensor_scan(prod[s], d0, d1, start, ALU.mult, ALU.add))
                    prod_c.end()

            def row_stats(q, s, h, between):
                dve.wait_ge(row_in[s], 64 * (h + 1))
                dve.wait_ge(ur_in[s], 16 * (h + 1))
                wait_past(dve, c_bmul, 3 * (q - 1))
                wait_past(dve, c_norm_r, 2 * (q - 1))
                bvar.begin(q)
                for j in range(QUAD):
                    bvar.add(v.bn_stats(bst[s][:, j, :], G[:, bass.ds(QUAD * q + j, 1), :]))
                    bvar.add(v.bn_stats(bst[s][:, QUAD + j, :], node_tiles(q)[:, j, :]))
                between(0)
                bvar.settle()
                variance(bvar, bst[s], bsm[s], bdf[s], bv2[s], bdd[s], bV[s], between)
                bvar.end()

            def hidden(q, s):
                dve.wait_ge(c_l1, 3 * q + 3)
                wait_past(dve, z2_done, q)
                v.scalar_tensor_tensor(h1, Z1[s][:, :], nb1[:, :], l1, ALU.max, ALU.add).then_inc(h1_ready, 1)

            def filters(q, s):
                dve.wait_ge(c_l2, 3 * q + 3)
                wait_past(dve, c_prod, PROD_OPS * (q - 2) + 1)
                v.scalar_tensor_tensor(bf[s], Z2[s][:, :], nb2[:, :], l2, ALU.max, ALU.add).then_inc(bf_ready, 1)

            def step_b(i, s, h):
                q1_, s1_, h1_ = back(i, s, h, 1)
                q2_, s2_, h2_ = back(i, s, h, 2)
                q, qs, qh = back(i, s, h, 3)

                def product(n):
                    if live(q2_, NQ):
                        running_product(q2_, s2_, h2_, n)

                def beside_rows(n):
                    if n == -1:
                        product(3)
                    if n in (3, 1) and live(i, NQ):
                        norm_factors(i, s, 0 if n == 3 else 1)
                    if n == 2 and live(i, NQ):
                        norm_rows(i, s)

                if live(i, NQ):
                    row_stats(i, s, h, product)
                else:
                    for n in range(3):
                        product(n)
                if live(q1_, NQ):
                    hidden(q1_, s1_)
                q4, s4, h4 = back(i, s, h, 4)
                if live(q4, NQ):
                    dve.wait_ge(c_yr, 2 * q4 + 2)
                    v.scalar_tensor_tensor(ynm[s4], ysm[s4], -0.5, yrs[s4], ALU.mult, ALU.mult
                                           ).then_inc(ynm_ready, 1)
                if live(q, NQ):
                    finish_rows(q, qs, beside_rows)
                else:
                    for n in (-1, 3, 1, 2):
                        beside_rows(n)
                if live(q1_, NQ):
                    filters(q1_, s1_)
            straight(0, NQ + 4, step_b)

        @block.scalar
        def _(act):
            a = nc.scalar.activation
            one = ones[:, 0:1]
            act.wait_ge(cut_t, 1)
            a(cut[:, :], tmp_t[:, :], ACT.Sin, bias=halfpi[:, :], scale=-PI).then_inc(cut_sin, 1)
            nc.scalar.preload_act_table_set("natural_log_exp_and_others")
            act.wait_ge(setup_pe, 1)
            setup = Chain(act, setup_act, 3)
            setup.begin(0)
            setup.link(a(ctmp[:, :], E0[:, 0:F], ACT.Abs))
            setup.link(a(ctmp2[:, :], ctmp[:, :], ACT.Exp, scale=-1.0))
            setup.link(a(ctmp[:, :], ctmp2[:, :], ACT.Ln, bias=one))
            setup.end()
            act.wait_ge(const_ready, 2)

            r_c, r2_c, qs_c = Chain(act, c_r, 3), Chain(act, c_r2, 2), Chain(act, c_qsum, OCT)

            def second_rstd(i, s):
                act.wait_ge(c_var2, VAR2_OPS * i + VAR2_AT)
                r2_c.begin(i)
                r2_c.link(a(lnv2[s], t4[s], ACT.Ln, bias=ceps[:, :], scale=1.0 / F))
                r2_c.link(a(rstd2[s], lnv2[s], ACT.Exp, scale=-0.5))
                r2_c.end()

            def square_sums(i, s):
                qs_c.begin(i)
                for j in range(OCT):
                    if j % QUAD == 0:
                        act.wait_ge(d_filled[j // QUAD], i + 1)
                    wait_past(act, c_qsum, qs_c.base + qs_c.n - 1)
                    qs_c.add(a(ajunk[:, j % 2, :], D[s][j // QUAD][:, (j % QUAD) * P:(j % QUAD + 1) * P], ACT.Square,
                               accum_out=qsum[s][:, j:j + 1]))
                qs_c.end()

            def first_rstd(i, s):
                act.wait_ge(c_var, VAR_OPS * i + V_AT)
                r_c.begin(i)
                r_c.link(a(lnv[s], V[s], ACT.Ln, bias=epst[:, :], scale=1.0 / F))
                r_c.add(a(rstd[s], lnv[s], ACT.Exp, scale=-0.5))
                r_c.add(a(stats[s][:, 0:3, :], lnv[s].unsqueeze(1).to_broadcast([P, 3, OCT]), ACT.Exp, scale=0.5))
                r_c.end()

            def copy_stats(i, s):
                act.wait_ge(stat_T, i + 1)
                wait_past(act, d_final, i - 1)
                a(statsT[s], psT[:, 0:P], ACT.Copy).then_inc(stat_copied, 1)

            def dense_out(i, s, h, b):
                act.wait_ge(d_final, i + 1)
                act.wait_ge(c_var2, VAR2_OPS * i + SCALE_AT)
                wait_past(act, o_stored[s], 16 * h)
                for j in range(QUAD * b, QUAD * b + QUAD):
                    ins = a(oo[s][:, j, :], D[s][b][:, (j % QUAD) * P:(j % QUAD + 1) * P], ACT.Copy,
                            scale=scale[s][:, j:j + 1])
                ins.then_inc(o_ready[b], 1)

            def dense_step(i, s, h):
                k, ks, kh = back(i, s, h, 2)
                if live(k, NO):
                    dense_out(k, ks, kh, 0)
                if live(i, NO):
                    first_rstd(i, s)
                if live(k, NO):
                    dense_out(k, ks, kh, 1)
                k, ks, kh = back(i, s, h, 1)
                if live(k, NO):
                    second_rstd(k, ks)
                if live(i, NO):
                    square_sums(i, s)
                    copy_stats(i, s)

            sweep(act, *A1, dense_step)
            act.wait_ge(soft_dve, 11)
            a(decay_c[:, :], da_c[:, :], ACT.Exp).then_inc(soft_act, 1)
            a(bw_c[:, :], db_c[:, :], ACT.Exp).then_inc(soft_act, 1)
            act.wait_ge(soft_act, 2)
            act.sem_inc(decay_ready, 1)
            sweep(act, *A2, dense_step)
            act.wait_ge(o_ready[1], NO)
            act.sem_inc(a_done, 1)
            act.wait_ge(a_done, 3)
            act.wait_ge(a_stored, 1)

            basis_c, l1_c, l2_c, l3_c = (Chain(act, sem_, n) for sem_, n in ((c_basis, 2), (c_l1, 3), (c_l2, 3),
                                                                              (c_l3, 3)))
            norm_c, yr_c = Chain(act, c_norm_r, 2), Chain(act, c_yr, 2)

            def log_term(chain, q, l, z, bias, n):
                if n == 0:
                    chain.begin(q)
                    chain.add(a(l, z, ACT.Abs, bias=bias))
                    return
                chain.settle()
                if n == 1:
                    chain.add(a(l, l, ACT.Exp, scale=-1.0))
                if n == 2:
                    chain.add(a(l, l, ACT.Ln, bias=one))
                    chain.end()

            def inverse_deviation(chain, q, ln_, r, V_, n):
                if n == 0:
                    chain.begin(q)
                    chain.add(a(ln_, V_, ACT.Ln, bias=epst[:, :], scale=1.0 / F))
                else:
                    chain.settle()
                    chain.add(a(r, ln_, ACT.Exp, scale=-0.5))
                    chain.end()

            def step_b(i, s, h):
                q, qs, qh = back(i, s, h, 3)
                q1_, s1_, h1_ = back(i, s, h, 1)
                q4, s4, h4 = back(i, s, h, 4)
                if live(q1_, NQ):
                    act.wait_ge(z1_done, q1_ + 1)
                    wait_past(act, h1_ready, q1_)
                if live(q4, NQ):
                    act.wait_ge(c_y, Y_OPS * q4 + YV_AT)
                for first, second in ((0, None), (1, 0), (2, 1), (None, 2)):
                    if live(q1_, NQ) and first is not None:
                        log_term(l1_c, q1_, l1, Z1[s1_][:, :], b1c[:, :], first)
                    if live(q, NQ) and second is not None:
                        if second == 0:
                            act.wait_ge(z3_done, q + 1)
                            wait_past(act, c_y, Y_OPS * (q - 1) + 1)
                        log_term(l3_c, q, l3, Z3[qs][:, :], 0.0, second)
                    if live(q4, NQ) and (first == 0 or second == 1):
                        inverse_deviation(yr_c, q4, yln[s4], yrs[s4], yV[s4], 0 if first == 0 else 1)
                if live(q1_, NQ):
                    act.wait_ge(c_bmul, 3 * q1_ + 3)
                    wait_past(act, hm_ready, q1_ - 1)
                    for j in range(QUAD // 2):
                        ins = a(hn[s1_][:, j, :], G[:, bass.ds(QUAD * q1_ + j, 1), :], ACT.Identity,
                                bias=bnm[s1_][:, j:j + 1], scale=brc[s1_][:, j:j + 1])
                    ins.then_inc(hn_ready[0], 1)
                if live(i, NQ):
                    act.wait_ge(wrow_in[s], 16 * (h + 1))
                    wait_past(act, z1_done, i)
                    basis_c.begin(i)
                    basis_c.add(a(e0, wrow[s], ACT.Square, bias=muneg[:, :]))
                    act.wait_ge(c_bvar, BVAR_OPS * i + BV_AT)
                    inverse_deviation(norm_c, i, bln[s], brs[s], bV[s], 0)
                    basis_c.settle()
                    basis_c.add(a(e0, e0, ACT.Exp, scale=-float(F)))
                    basis_c.end()
                    inverse_deviation(norm_c, i, bln[s], brs[s], bV[s], 1)
                if live(q4, NQ):
                    act.wait_ge(ynm_ready, q4 + 1)
                    wait_past(act, scattered[s4], 64 * h4)
                    for j in range(QUAD):
                        ins = a(o[s4][:, j, :], y[s4][:, j, :], ACT.Identity, bias=ynm[s4][:, j:j + 1],
                                scale=yrs[s4][:, j:j + 1])
                    ins.then_inc(row_ready, 1)
                if live(q1_, NQ):
                    act.wait_ge(z2_done, q1_ + 1)
                    wait_past(act, bf_ready, q1_)
                    log_term(l2_c, q1_, l2, Z2[s1_][:, :], b2c[:, :], 0)
                    log_term(l2_c, q1_, l2, Z2[s1_][:, :], b2c[:, :], 1)
                    log_term(l2_c, q1_, l2, Z2[s1_][:, :], b2c[:, :], 2)
            sweep(act, *B, step_b)

        @block.tensor
        def _(pe):
            mm = nc.tensor.matmul
            pe.wait_ge(par_in, 16 * 11)
            pe.wait_ge(setup_dve, SETUP_OPS)
            mm(E0[:, 0:F], ones[:, :], w3[:, :], start=True, stop=False)
            mm(E0[:, 0:F], ones[0:1, :], b3row[:, :], start=False, stop=True).then_inc(setup_pe, 1)
            pe.wait_ge(const_ready, 1)
            mm(E1[:, 0:1], w2[:, :], b1m[:, :], start=True, stop=True).then_inc(setup_pe, 1)
            pe.wait_ge(const_ready, 2)

            def fill(i, s, h):
                pe.wait_ge(x_in[s], 16 * (h + 1))
                for b in range(2):
                    wait_past(pe, o_ready[b], i - 1)
                    mm(D[s][b][:, :], ident[:, :], xo[s][:, QUAD * b:QUAD * (b + 1), :], start=True, stop=False)
                    mm(D[s][b][:, :], ones_bf[:, :], c3[:, :, :], start=False, stop=True).then_inc(d_filled[b], 1)

            def transpose_stats(i, s):
                pe.wait_ge(c_split, SPLIT_OPS * (i + 1))
                wait_past(pe, stat_copied, i)
                mm(psT[:, 0:P], parts[s], ident_bf[:, :], start=True, stop=True).then_inc(stat_T, 1)

            def add_terms(i, s):
                pe.wait_ge(stat_copied, i + 1)
                pe.wait_ge(c_qsum, OCT * i + OCT)
                for b in range(2):
                    ins = mm(D[s][b][:, :], statsT[s], rhs_sel[:, QUAD * b:QUAD * (b + 1), :], start=False, stop=True,
                             skip_group_check=True)
                ins.then_inc(d_final, 1)

            def find(q, s, b):
                pe.wait_ge(ge_ready[0], q + 1)
                pe.wait_ge(ge_ready[1], q + 1)
                wait_past(pe, find_used, 2 * q)
                for j in (2 * b, 2 * b + 1):
                    for g, part in ((0, dhigh), (0, drest), (1, dhigh), (1, drest)):
                        ins = mm(psF[b][:, (j % 2) * (P + 1):(j % 2 + 1) * (P + 1)],
                                 ge[s][:, g, j * P:(j + 1) * P], part[:, g, 0:P + 1],
                                 start=(g == 0 and part is dhigh), stop=(g == 1 and part is drest))
                ins.then_inc(found, 1)

            pe.wait_ge(find_setup, 1)

            def step_a1(i, s, h):
                fill(i, s, h)
                k, ks, kh = back(i, s, h, 1)
                if live(k, NO):
                    add_terms(k, ks)
                transpose_stats(i, s)
                find(i, s, 0)
                find(i, s, 1)

            sweep(pe, *A1, step_a1)

            eh, e1_ = ident[0:H, 0:H], ones[0:1, 0:1]
            pe.wait_ge(soft_dve, 1)
            nc.tensor.transpose(E0[0:H, 0:P], score[:, 0:NT:2], ident[:, :]).then_inc(soft_pe, 1)
            nc.tensor.transpose(E0[0:H, P:2 * P], score[:, 1:NT:2], ident[:, :]).then_inc(soft_pe, 1)
            pe.wait_ge(soft_dve, 3)
            mm(E1[0:1, 0:H], max_c[:, 256:257], eh, start=True, stop=True).then_inc(soft_pe, 1)
            mm(E1[0:1, P:P + H], pass_c[:, 1:2], eh, start=True, stop=True).then_inc(soft_pe, 1)
            pe.wait_ge(soft_dve, 6)
            mm(E2[0:H, 0:1], carry_row[0:1, 0:H], e1_, start=True, stop=True).then_inc(soft_pe, 1)
            pe.wait_ge(soft_dve, 13)
            mm(E1[0:1, 0:H], den_c[:, 255:256], eh, start=True, stop=True).then_inc(soft_pe, 1)
            mm(E1[0:1, P:P + H], da_c[:, 255:256], eh, start=True, stop=True).then_inc(soft_pe, 1)
            pe.wait_ge(soft_dve, 16)
            mm(E2[0:H, 0:1], carry_row[0:1, 0:H], e1_, start=True, stop=True).then_inc(soft_pe, 1)
            pe.wait_ge(soft_dve, 20)
            for bank, src in ((E0, bw_c), (E1, den_c)):
                for g in range(2):
                    nc.tensor.transpose(bank[:, g * H:(g + 1) * H], src[:, g * P:(g + 1) * P], eh
                                        ).then_inc(soft_pe, 1)

            def step_a2(i, s, h):
                k, ks, kh = back(i, s, h, 1)
                if live(i, NO):
                    fill(i, s, h)
                if live(k, NO):
                    add_terms(k, ks)
                q, qs, qh = back(i, s, h, NQ)
                if live(q, NQ):
                    pe.wait_ge(bx_ready, q + 1)
                    wait_past(pe, scan_done, q - 1)
                    for j in range(QUAD):
                        ins = nc.tensor.transpose(psX[qs][:, j * P:(j + 1) * P], bx[qs][:, j, :], ident[:, :])
                    ins.then_inc(bx_T, 1)
                if live(i, NO):
                    transpose_stats(i, s)
                q, qs, qh = back(i, s, h, NQ + 1)
                if live(q, NQ):
                    pe.wait_ge(scan_done, q + 1)
                    wait_past(pe, u_ready, q)
                    for j in range(QUAD):
                        ins = nc.tensor.transpose(psR[:, j * P:(j + 1) * P], RT[qs][:, j * P:(j + 1) * P],
                                                  ident[:, :])
                    ins.then_inc(r_T, 1)

            sweep(pe, *A2, step_a2)
            pe.wait_ge(r_T, NQ)
            pe.sem_inc(a_done, 1)
            pe.wait_ge(a_done, 3)
            pe.wait_ge(a_stored, 1)

            def step_b(i, s, h):
                q, qs, qh = back(i, s, h, 1)
                if live(q, NQ):
                    pe.wait_ge(h1_ready, q + 1)
                    wait_past(pe, bf_ready, q - 1)
                    mm(Z2[qs][:, :], w2[:, :], h1, start=True, stop=True).then_inc(z2_done, 1)
                if live(i, NQ):
                    pe.wait_ge(c_basis, 2 * i + 2)
                    wait_past(pe, h1_ready, i - 1)
                    mm(Z1[s][:, :], w1[:, :], e0, start=True, stop=True).then_inc(z1_done, 1)
                q, qs, qh = back(i, s, h, 2)
                if live(q, NQ):
                    pe.wait_ge(c_prod, PROD_OPS * q + PROD_AT)
                    wait_past(pe, c_y, Y_OPS * (q - 2) + 1)
                    mm(Z3[qs][:, :], ones_bf[:, :], b3parts[:, :, :], start=True, stop=False)
                    for j in range(QUAD):
                        ins = mm(Z3[qs][:, j * P:(j + 1) * P], prod[qs][:, j * P:(j + 1) * P], w3[:, :],
                                 start=False, stop=(j == QUAD - 1))
                    ins.then_inc(z3_done, 1)
                q, qs, qh = back(i, s, h, 1)
                if live(q, NQ):
                    pe.wait_ge(hm_ready, q + 1)
                    wait_past(pe, c_prod, PROD_OPS * (q - 2) + 1)
                    for j in range(QUAD):
                        ins = nc.tensor.transpose(MT[qs][:, j * P:(j + 1) * P], hm[qs][:, j, :], ident[:, :])
                    ins.then_inc(m_T, 1)

            sweep(pe, *B, step_b)


def kernel(x, src, dst, edge_attr_128, edge_weight, L0_gnn_W, L1_gnn_W1, L1_gnn_b1, L1_gnn_W2, L1_gnn_b2, L1_gnn_W3,
           L1_gnn_b3):
    import numpy as np
    import concourse.bacc as bacc
    from concourse.bass_utils import run_bass_kernel_spmd

    x, src, dst, attr, weight = (np.ascontiguousarray(a) for a in (x, src, dst, edge_attr_128, edge_weight))
    N, E = x.shape[0], src.shape[0]
    NT = -(-E // QE) * QUAD
    pad = NT * P - E

    def tiles(a):
        return np.ascontiguousarray(a.reshape(NT, P).T)

    src_flat = np.pad(src, (0, pad))
    weight_flat = np.pad(weight, (0, pad), constant_values=2 * CUTOFF)
    dst_flat = np.pad(np.pad(dst, (0, pad), constant_values=N), (P, 1), constant_values=-1)
    arrays = {
        "x": x, "src_tiles": tiles(src_flat), "dst_tiles": tiles(dst_flat[P:-1]), "next_tiles": tiles(dst_flat[P + 1:]),
        "weight_tiles": tiles(weight_flat), "src_flat": src_flat, "dst_flat": dst_flat, "weight_flat": weight_flat,
        "attr": attr, "W0": L0_gnn_W, "W1": L1_gnn_W1, "b1": L1_gnn_b1, "W2": L1_gnn_W2, "b2": L1_gnn_b2,
        "W3": L1_gnn_W3, "b3": L1_gnn_b3, "eye": np.eye(P, dtype=np.float32),
        "iota1": np.ascontiguousarray(np.broadcast_to(np.arange(1, P + 1, dtype=np.float32), (P, P))),
        "mu": -np.linspace(0.0, 1.0, P, dtype=np.float32)[:, None],
    }
    arrays = {f"in_{k}": np.ascontiguousarray(a) for k, a in arrays.items()}
    nc = bacc.Bacc("TRN2", target_bir_lowering=False, num_devices=1)
    args = [nc.dram_tensor(k, a.shape, mybir.dt.from_np(a.dtype), kind="ExternalInput").ap() for k, a in arrays.items()]
    args.append(nc.dram_tensor("out_dram", x.shape, mybir.dt.float32, kind="ExternalOutput").ap())
    gnn_kernel(nc, *args)
    r = run_bass_kernel_spmd(nc, [arrays], core_ids=[0])
    return r.results[0]["out_dram"]
```
